# Optimizing a Trainium2 kernel written in Bass

```python
import numpy as np
import jax
import jax.numpy as jnp

def _softmax(x, axis=-1):
    return jax.nn.softmax(x, axis=axis)

def _gelu(x):
    return jax.nn.gelu(x, approximate=True)

def _silu(x):
    return jax.nn.silu(x)

def _sigmoid(x):
    return jax.nn.sigmoid(x)

def _layernorm(x, axis=-1, eps=1e-05):
    m = jnp.mean(x, axis=axis, keepdims=True)
    v = jnp.var(x, axis=axis, keepdims=True)
    return (x - m) / jnp.sqrt(v + eps)

def _scatter_add(tgt, idx, src, axis=0):
    return tgt.at[idx].add(src)

def _segment_sum(src, seg, n):
    return jax.ops.segment_sum(src, seg, n)
kernel_name = 'mk_adj_resnorm_d4_adj_r2_343e44'

def setup_inputs(seed: int=0):
    np.random.seed(seed)
    _w = jnp.asarray

    def _rec_inputs():
        import jax
        import jax.numpy as jnp
        _gk = jax.random.key(seed)
        x = -0.0005963 + 1.001 * jax.random.normal(jax.random.fold_in(_gk, 1), (32, 256, 384), jnp.float32)
        _a = jax.random.bernoulli(jax.random.fold_in(_gk, 2), 0.0625, (32, 256, 256))
        _a = jnp.logical_or(_a, jnp.swapaxes(_a, -1, -2))
        _a = jnp.logical_or(_a, jnp.eye(256, dtype=bool))
        adj = _a
        return (x, adj)
    x, adj = _rec_inputs()

    def _L0_gnn_setup():
        import jax, jax.numpy as jnp
        import numpy as np
        ATT_HEAD = 12
        IN_DIM = 384
        OUT_DIM = IN_DIM // ATT_HEAD
        LEAKY_ALPHA = 0.2
        B, N = (8, 256)
        key = jax.random.key(seed)
        ks = jax.random.split(key, 8)
        feat_in = jax.random.normal(ks[0], (B, N, IN_DIM), dtype=jnp.float32)
        adj = jax.random.randint(ks[1], (B, N, N), 0, 2) > 0
        lim_W = float(np.sqrt(6.0 / (IN_DIM + OUT_DIM)))
        W = jax.random.uniform(ks[2], (ATT_HEAD, IN_DIM, OUT_DIM), minval=-lim_W, maxval=lim_W, dtype=jnp.float32)
        b = jnp.zeros((OUT_DIM,), dtype=jnp.float32)
        lim_w = float(np.sqrt(6.0 / (OUT_DIM + 1)))
        w_src = jax.random.uniform(ks[3], (ATT_HEAD, OUT_DIM, 1), minval=-lim_w, maxval=lim_w, dtype=jnp.float32)
        w_dst = jax.random.uniform(ks[4], (ATT_HEAD, OUT_DIM, 1), minval=-lim_w, maxval=lim_w, dtype=jnp.float32)
        std_H = float(np.sqrt(2.0 / (IN_DIM + IN_DIM)))
        H_w = jax.random.normal(ks[5], (IN_DIM, IN_DIM), dtype=jnp.float32) * std_H
        H_b = jax.random.normal(ks[6], (IN_DIM,), dtype=jnp.float32) * 0.01
        return {'feat_in': feat_in, 'adj': adj, 'W': W, 'b': b, 'w_src': w_src, 'w_dst': w_dst, 'H_w': H_w, 'H_b': H_b}
    _L0_gnn_all = _L0_gnn_setup()
    _L0_gnn_in = {k: v for k, v in _L0_gnn_all.items() if k in ('W', 'b', 'w_src', 'w_dst', 'H_w', 'H_b')}
    del _L0_gnn_all

    def _L1_gnn_setup():
        import jax, jax.numpy as jnp
        import numpy as np
        B, S, H = (4, 1024, 384)
        NUM_HEADS = 6
        HEAD_SIZE = H // NUM_HEADS
        NEG = -9000000000000000.0

        def _heads(x):
            b, s, _ = x.shape
            return x.reshape(b, s, NUM_HEADS, HEAD_SIZE).transpose(0, 2, 1, 3)
        key = jax.random.key(seed)
        ks = jax.random.split(key, 10)
        seq_inputs = jax.random.normal(ks[0], (B, S, H), dtype=jnp.float32)
        gm = jax.random.randint(ks[1], (B, S, S), 0, 2) > 0
        graph_mask = gm | jnp.eye(S, dtype=bool)[None]
        sc = 1.0 / np.sqrt(H)
        Wq = jax.random.normal(ks[2], (H, H), dtype=jnp.float32) * sc
        bq = jnp.zeros((H,), dtype=jnp.float32)
        Wk = jax.random.normal(ks[3], (H, H), dtype=jnp.float32) * sc
        bk = jnp.zeros((H,), dtype=jnp.float32)
        Wv = jax.random.normal(ks[4], (H, H), dtype=jnp.float32) * sc
        bv = jnp.zeros((H,), dtype=jnp.float32)
        Wf = jax.random.normal(ks[5], (H, H), dtype=jnp.float32) * sc
        bf = jnp.zeros((H,), dtype=jnp.float32)
        return {'seq_inputs': seq_inputs, 'Wq': Wq, 'bq': bq, 'Wk': Wk, 'bk': bk, 'Wv': Wv, 'bv': bv, 'Wf': Wf, 'bf': bf, 'graph_mask': graph_mask}
    _L1_gnn_all = _L1_gnn_setup()
    _L1_gnn_in = {k: v for k, v in _L1_gnn_all.items() if k in ('Wq', 'bq', 'Wk', 'bk', 'Wv', 'bv', 'Wf', 'bf')}
    del _L1_gnn_all

    def _L2_gnn_setup():
        import jax, jax.numpy as jnp
        import numpy as np
        ATT_HEAD = 12
        IN_DIM = 384
        OUT_DIM = IN_DIM // ATT_HEAD
        LEAKY_ALPHA = 0.2
        B, N = (8, 256)
        key = jax.random.key(seed)
        ks = jax.random.split(key, 8)
        feat_in = jax.random.normal(ks[0], (B, N, IN_DIM), dtype=jnp.float32)
        adj = jax.random.randint(ks[1], (B, N, N), 0, 2) > 0
        lim_W = float(np.sqrt(6.0 / (IN_DIM + OUT_DIM)))
        W = jax.random.uniform(ks[2], (ATT_HEAD, IN_DIM, OUT_DIM), minval=-lim_W, maxval=lim_W, dtype=jnp.float32)
        b = jnp.zeros((OUT_DIM,), dtype=jnp.float32)
        lim_w = float(np.sqrt(6.0 / (OUT_DIM + 1)))
        w_src = jax.random.uniform(ks[3], (ATT_HEAD, OUT_DIM, 1), minval=-lim_w, maxval=lim_w, dtype=jnp.float32)
        w_dst = jax.random.uniform(ks[4], (ATT_HEAD, OUT_DIM, 1), minval=-lim_w, maxval=lim_w, dtype=jnp.float32)
        std_H = float(np.sqrt(2.0 / (IN_DIM + IN_DIM)))
        H_w = jax.random.normal(ks[5], (IN_DIM, IN_DIM), dtype=jnp.float32) * std_H
        H_b = jax.random.normal(ks[6], (IN_DIM,), dtype=jnp.float32) * 0.01
        return {'feat_in': feat_in, 'adj': adj, 'W': W, 'b': b, 'w_src': w_src, 'w_dst': w_dst, 'H_w': H_w, 'H_b': H_b}
    _L2_gnn_all = _L2_gnn_setup()
    _L2_gnn_in = {k: v for k, v in _L2_gnn_all.items() if k in ('W', 'b', 'w_src', 'w_dst', 'H_w', 'H_b')}
    del _L2_gnn_all

    def _L3_gnn_setup():
        import jax, jax.numpy as jnp
        import numpy as np
        ATT_HEAD = 12
        IN_DIM = 384
        OUT_DIM = IN_DIM // ATT_HEAD
        LEAKY_ALPHA = 0.2
        B, N = (8, 256)
        key = jax.random.key(seed)
        ks = jax.random.split(key, 8)
        feat_in = jax.random.normal(ks[0], (B, N, IN_DIM), dtype=jnp.float32)
        adj = jax.random.randint(ks[1], (B, N, N), 0, 2) > 0
        lim_W = float(np.sqrt(6.0 / (IN_DIM + OUT_DIM)))
        W = jax.random.uniform(ks[2], (ATT_HEAD, IN_DIM, OUT_DIM), minval=-lim_W, maxval=lim_W, dtype=jnp.float32)
        b = jnp.zeros((OUT_DIM,), dtype=jnp.float32)
        lim_w = float(np.sqrt(6.0 / (OUT_DIM + 1)))
        w_src = jax.random.uniform(ks[3], (ATT_HEAD, OUT_DIM, 1), minval=-lim_w, maxval=lim_w, dtype=jnp.float32)
        w_dst = jax.random.uniform(ks[4], (ATT_HEAD, OUT_DIM, 1), minval=-lim_w, maxval=lim_w, dtype=jnp.float32)
        std_H = float(np.sqrt(2.0 / (IN_DIM + IN_DIM)))
        H_w = jax.random.normal(ks[5], (IN_DIM, IN_DIM), dtype=jnp.float32) * std_H
        H_b = jax.random.normal(ks[6], (IN_DIM,), dtype=jnp.float32) * 0.01
        return {'feat_in': feat_in, 'adj': adj, 'W': W, 'b': b, 'w_src': w_src, 'w_dst': w_dst, 'H_w': H_w, 'H_b': H_b}
    _L3_gnn_all = _L3_gnn_setup()
    _L3_gnn_in = {k: v for k, v in _L3_gnn_all.items() if k in ('W', 'b', 'w_src', 'w_dst', 'H_w', 'H_b')}
    del _L3_gnn_all
    return {'x': x, 'adj': adj, 'L0_gnn_W': _L0_gnn_in['W'], 'L0_gnn_b': _L0_gnn_in['b'], 'L0_gnn_w_src': _L0_gnn_in['w_src'], 'L0_gnn_w_dst': _L0_gnn_in['w_dst'], 'L0_gnn_H_w': _L0_gnn_in['H_w'], 'L0_gnn_H_b': _L0_gnn_in['H_b'], 'L1_gnn_Wq': _L1_gnn_in['Wq'], 'L1_gnn_bq': _L1_gnn_in['bq'], 'L1_gnn_Wk': _L1_gnn_in['Wk'], 'L1_gnn_bk': _L1_gnn_in['bk'], 'L1_gnn_Wv': _L1_gnn_in['Wv'], 'L1_gnn_bv': _L1_gnn_in['bv'], 'L1_gnn_Wf': _L1_gnn_in['Wf'], 'L1_gnn_bf': _L1_gnn_in['bf'], 'L2_gnn_W': _L2_gnn_in['W'], 'L2_gnn_b': _L2_gnn_in['b'], 'L2_gnn_w_src': _L2_gnn_in['w_src'], 'L2_gnn_w_dst': _L2_gnn_in['w_dst'], 'L2_gnn_H_w': _L2_gnn_in['H_w'], 'L2_gnn_H_b': _L2_gnn_in['H_b'], 'L3_gnn_W': _L3_gnn_in['W'], 'L3_gnn_b': _L3_gnn_in['b'], 'L3_gnn_w_src': _L3_gnn_in['w_src'], 'L3_gnn_w_dst': _L3_gnn_in['w_dst'], 'L3_gnn_H_w': _L3_gnn_in['H_w'], 'L3_gnn_H_b': _L3_gnn_in['H_b']}

def reference(x, adj, L0_gnn_W, L0_gnn_b, L0_gnn_w_src, L0_gnn_w_dst, L0_gnn_H_w, L0_gnn_H_b, L1_gnn_Wq, L1_gnn_bq, L1_gnn_Wk, L1_gnn_bk, L1_gnn_Wv, L1_gnn_bv, L1_gnn_Wf, L1_gnn_bf, L2_gnn_W, L2_gnn_b, L2_gnn_w_src, L2_gnn_w_dst, L2_gnn_H_w, L2_gnn_H_b, L3_gnn_W, L3_gnn_b, L3_gnn_w_src, L3_gnn_w_dst, L3_gnn_H_w, L3_gnn_H_b):
    import jax
    import jax.numpy as jnp

    def _L0_gnn_ref(feat_in, adj, W, b, w_src, w_dst, H_w, H_b):
        import jax, jax.numpy as jnp
        import numpy as np
        ATT_HEAD = 12
        IN_DIM = 384
        OUT_DIM = IN_DIM // ATT_HEAD
        LEAKY_ALPHA = 0.2
        B, N = (8, 256)
        h = jnp.einsum('bnd,ade->bane', feat_in, W)
        th = jnp.tanh(h)
        attn_src = jnp.einsum('bane,aeo->bano', th, w_src)
        attn_dst = jnp.einsum('bane,aeo->bano', th, w_dst)
        attn = attn_src + jnp.swapaxes(attn_dst, 2, 3)
        attn = jnp.where(attn >= 0, attn, LEAKY_ALPHA * attn)
        mask = ~adj[:, None, :, :]
        attn = jnp.where(mask, jnp.float32(-999.0), attn)
        attn = jax.nn.softmax(attn, axis=-1)
        feat_out = jnp.einsum('banm,bame->bane', attn, h) + b
        feat_out = jnp.swapaxes(feat_out, 1, 2).reshape(feat_in.shape[0], feat_in.shape[1], -1)
        feat_out = jax.nn.elu(feat_out)
        gate = jax.nn.sigmoid(feat_in @ H_w.T + H_b)
        return gate * feat_out + (1.0 - gate) * feat_in

    def _L1_gnn_ref(seq_inputs, Wq, bq, Wk, bk, Wv, bv, Wf, bf, graph_mask):
        import jax, jax.numpy as jnp
        import numpy as np
        B, S, H = (4, 1024, 384)
        NUM_HEADS = 6
        HEAD_SIZE = H // NUM_HEADS
        NEG = -9000000000000000.0

        def _heads(x):
            b, s, _ = x.shape
            return x.reshape(b, s, NUM_HEADS, HEAD_SIZE).transpose(0, 2, 1, 3)
        q = _heads(seq_inputs @ Wq + bq)
        k = _heads(seq_inputs @ Wk + bk)
        v = _heads(seq_inputs @ Wv + bv)
        scores = jnp.einsum('bhqd,bhkd->bhqk', q, k) / np.sqrt(HEAD_SIZE)
        bias = jnp.where(graph_mask, 0.0, NEG)[:, None]
        probs = jax.nn.softmax(scores + bias, axis=-1)
        ctx = jnp.einsum('bhqk,bhkd->bhqd', probs, v)
        ctx = ctx.transpose(0, 2, 1, 3).reshape(seq_inputs.shape[0], seq_inputs.shape[1], H)
        return ctx @ Wf + bf

    def _L2_gnn_ref(feat_in, adj, W, b, w_src, w_dst, H_w, H_b):
        import jax, jax.numpy as jnp
        import numpy as np
        ATT_HEAD = 12
        IN_DIM = 384
        OUT_DIM = IN_DIM // ATT_HEAD
        LEAKY_ALPHA = 0.2
        B, N = (8, 256)
        h = jnp.einsum('bnd,ade->bane', feat_in, W)
        th = jnp.tanh(h)
        attn_src = jnp.einsum('bane,aeo->bano', th, w_src)
        attn_dst = jnp.einsum('bane,aeo->bano', th, w_dst)
        attn = attn_src + jnp.swapaxes(attn_dst, 2, 3)
        attn = jnp.where(attn >= 0, attn, LEAKY_ALPHA * attn)
        mask = ~adj[:, None, :, :]
        attn = jnp.where(mask, jnp.float32(-999.0), attn)
        attn = jax.nn.softmax(attn, axis=-1)
        feat_out = jnp.einsum('banm,bame->bane', attn, h) + b
        feat_out = jnp.swapaxes(feat_out, 1, 2).reshape(feat_in.shape[0], feat_in.shape[1], -1)
        feat_out = jax.nn.elu(feat_out)
        gate = jax.nn.sigmoid(feat_in @ H_w.T + H_b)
        return gate * feat_out + (1.0 - gate) * feat_in

    def _L3_gnn_ref(feat_in, adj, W, b, w_src, w_dst, H_w, H_b):
        import jax, jax.numpy as jnp
        import numpy as np
        ATT_HEAD = 12
        IN_DIM = 384
        OUT_DIM = IN_DIM // ATT_HEAD
        LEAKY_ALPHA = 0.2
        B, N = (8, 256)
        h = jnp.einsum('bnd,ade->bane', feat_in, W)
        th = jnp.tanh(h)
        attn_src = jnp.einsum('bane,aeo->bano', th, w_src)
        attn_dst = jnp.einsum('bane,aeo->bano', th, w_dst)
        attn = attn_src + jnp.swapaxes(attn_dst, 2, 3)
        attn = jnp.where(attn >= 0, attn, LEAKY_ALPHA * attn)
        mask = ~adj[:, None, :, :]
        attn = jnp.where(mask, jnp.float32(-999.0), attn)
        attn = jax.nn.softmax(attn, axis=-1)
        feat_out = jnp.einsum('banm,bame->bane', attn, h) + b
        feat_out = jnp.swapaxes(feat_out, 1, 2).reshape(feat_in.shape[0], feat_in.shape[1], -1)
        feat_out = jax.nn.elu(feat_out)
        gate = jax.nn.sigmoid(feat_in @ H_w.T + H_b)
        return gate * feat_out + (1.0 - gate) * feat_in
    x = _layernorm(x + _L0_gnn_ref(x, adj, L0_gnn_W, L0_gnn_b, L0_gnn_w_src, L0_gnn_w_dst, L0_gnn_H_w, L0_gnn_H_b), axis=-1)
    x = _layernorm(x + _L1_gnn_ref(x, L1_gnn_Wq, L1_gnn_bq, L1_gnn_Wk, L1_gnn_bk, L1_gnn_Wv, L1_gnn_bv, L1_gnn_Wf, L1_gnn_bf, adj), axis=-1)
    x = _layernorm(x + _L2_gnn_ref(x, adj, L2_gnn_W, L2_gnn_b, L2_gnn_w_src, L2_gnn_w_dst, L2_gnn_H_w, L2_gnn_H_b), axis=-1)
    x = _layernorm(x + _L3_gnn_ref(x, adj, L3_gnn_W, L3_gnn_b, L3_gnn_w_src, L3_gnn_w_dst, L3_gnn_H_w, L3_gnn_H_b), axis=-1)
    return x

_drawn_inputs = setup_inputs


def setup_inputs(seed=0):
    import zlib

    import numpy as np

    out = dict(_drawn_inputs(seed))
    spreads = {'L0_gnn_b': (0.0, 0.1),
     'L1_gnn_bq': (0.0, 0.349),
     'L1_gnn_bk': (0.0, 2.0),
     'L1_gnn_bv': (0.0, 0.1),
     'L1_gnn_bf': (0.0, 0.1),
     'L2_gnn_b': (0.0, 0.384),
     'L3_gnn_b': (0.0, 0.321)}
    factors = {'L0_gnn_w_src': 2.703,
     'L0_gnn_H_b': 34.428,
     'L2_gnn_w_src': 2.966,
     'L2_gnn_H_b': 38.23,
     'L3_gnn_H_b': 39.841}
    for name, (base, spread) in spreads.items():
        noise = np.random.default_rng([zlib.crc32(name.encode()), seed]).standard_normal(out[name].shape)
        drawn = base * np.exp(spread * noise) if base else spread * noise
        out[name] = jnp.asarray(drawn.astype(out[name].dtype))
    for name, factor in factors.items():
        out[name] = (out[name] * factor).astype(out[name].dtype)
    return out
```

```python
import concourse.bass as bass
from concourse import mybir
from contextlib import ExitStack

P = 128
WSCALE = 64.0
EPS = 1e-5
NEG = 9.0e15


class Graph:

    def __init__(self, half, parity):
        self.half, self.p = half, parity
        self.s = half * 2 + parity

    def next(self):
        return Graph(self.half, 1) if self.p == 0 else Graph(self.half + 1, 0)

    def prev(self):
        return Graph(self.half, 0) if self.p == 1 else Graph(self.half - 1, 1)


class Signal:

    def __init__(self, sem, per=1):
        self.sem, self.per, self.base = sem, per, 0

    def at(self, graph, k=None):
        value = graph.s * self.per + (self.base + (self.per if k is None else k))
        return max(value, 0) if isinstance(value, int) else value


class ParitySignal:

    def __init__(self, sems):
        self.sems, self.base = sems, 0

    def of(self, graph):
        return self.sems[graph.p]

    def at(self, graph):
        value = graph.half * 16 + (self.base + 16)
        return max(value, 0) if isinstance(value, int) else value


def residual_graph_layers(nc, a, out):
    f32, f16, bf16, u8 = mybir.dt.float32, mybir.dt.float16, mybir.dt.bfloat16, mybir.dt.uint8
    ALU, ACT, AX = mybir.AluOpType, mybir.ActivationFunctionType, mybir.AxisListType
    B, N, C = a["x"].shape
    NT, KC = N // P, C // P
    HEADS = a["L0_gnn_wsrc"].shape[1] * KC
    HEADS = 12
    E = C // HEADS
    EV = E + 1
    PAIRS = HEADS // 2
    MH = 6
    DH = C // MH
    DV = DH + 1
    NW = 4
    BANK = 512
    x_dram = a["x"].rearrange("b (t p) c -> b p t c", p=P)
    out_dram = out.rearrange("b (t p) c -> b p t c", p=P)
    adj_dram = a["adj"].rearrange("b (t p) m -> b p t m", p=P)
    adjT_dram = a["adjT"].rearrange("b (t p) n -> b p t n", p=P)

    ctx = ExitStack()
    with ctx:
        def sb(name, shape, dt=f32):
            return ctx.enter_context(nc.sbuf_tensor(name, shape, dt))

        def sem(name):
            return ctx.enter_context(nc.semaphore(name))

        x_all = sb("x_all", [P, B, NT, C])
        x_in = sb("x_in", [P, 2, NT, C])
        x_res = sb("x_res", [P, 2, NT, C])
        mask = sb("mask", [P, 2, NT, N], u8)
        x_hi = sb("x_hi", [P, KC, N], f16)
        x_lo = sb("x_lo", [P, KC, N], f16)
        w_stage = sb("w_stage", [P, 2, KC, C])
        w_hi = sb("w_hi", [P, 4, KC, C], f16)
        w_lo = sb("w_lo", [P, 4, KC, C], f16)
        ident = sb("ident", [P, P])
        ident_bf = sb("ident_bf", [P, P], bf16)
        head_of = sb("head_of", [P, KC, HEADS])
        part_of = sb("part_of", [96, HEADS])
        pick_head = sb("pick_head", [96, HEADS, P], bf16)
        w_score = sb("w_score", [P, 2, KC])
        score_mat = sb("score_mat", [P, KC, 2 * HEADS])
        ones12 = sb("ones12", [HEADS, P])
        row_pq = sb("row_pq", [2, 2])
        row_hi = sb("row_hi", [2, 2, C], f16)
        bias_row = sb("bias_row", [2, 2, C], f16)
        ones_row = sb("ones_row", [2, P], f16)
        bias_col = sb("bias_col", [P, 2, KC])
        minus_half = sb("minus_half", [P, NT])
        minus_one = sb("minus_one", [P, NT])
        eps_whole = sb("eps_whole", [P, NT])
        eps_half = sb("eps_half", [P, NT])
        sd = sb("sd", [P, NT, 2 * HEADS])
        d_max = sb("d_max", [HEADS, 1])
        d_max_diag = sb("d_max_diag", [HEADS, HEADS])
        s_pos = sb("s_pos", [HEADS, N])
        b_exp = sb("b_exp", [HEADS, N])
        b_rest = sb("b_rest", [HEADS, N])
        b_mid = sb("b_mid", [HEADS, N], bf16)
        b_parts = sb("b_parts", [96, 2, N], bf16)
        d_rel = sb("d_rel", [P, NT, HEADS])
        G = sb("G", [P, 2, NT, HEADS])
        D = sb("D", [P, NT, HEADS])
        rden = sb("rden", [P, NT, HEADS])
        row_max = sb("row_max", [P, 2, NT])
        settled = sb("settled", [P, NT])
        stats = sb("stats", [P, NT, 6])
        mean_var = sb("mean_var", [P, NT, 2])
        var_eps = sb("var_eps", [P, NT])
        rstd = sb("rstd", [P, NT])
        mean_rstd = sb("mean_rstd", [P, NT])
        shift = sb("shift", [P, NT])
        buf_a = sb("buf_a", [P, NW * NT * N])
        buf_b = sb("buf_b", [P, 2 * NT * HEADS * EV])
        buf_c = sb("buf_c", [P, 2 * NT * C])
        buf_d = sb("buf_d", [P, 2 * NT * C])
        buf_e = sb("buf_e", [P, NT * C])
        buf_f = sb("buf_f", [P, NT * C])
        buf_g = sb("buf_g", [P, NT * C])
        row_in, row_64, row_lo = (b[0:2, :].rearrange("p (i c) -> p i c", i=2) for b in (buf_e, buf_f, buf_g))
        y = sb("y", [P, NT, C])
        x_out = sb("x_out", [P, 2, NT, C])
        def ps(name):
            return ctx.enter_context(nc.psum_tensor(name, [P, 2, BANK], f32))

        ps_t, ps_h, ps_b, ps_o = ps("ps_t"), ps("ps_h"), ps("ps_b"), ps("ps_o")
        t_flat = ps_t[:, :, :].rearrange("p t c -> p (t c)")
        tr_ps = t_flat[:, 0:KC * N].rearrange("p (k n) -> p k n", k=KC)

        x_loaded = ParitySignal([sem("x_loaded0"), sem("x_loaded1")])
        res_loaded = ParitySignal([sem("res_loaded0"), sem("res_loaded1")])
        mask_loaded = ParitySignal([sem("mask_loaded0"), sem("mask_loaded1")])
        saved = ParitySignal([sem("saved0"), sem("saved1")])
        xt_ready = Signal(sem("xt_ready"))
        hi_ready = Signal(sem("hi_ready"))
        lo_ready = Signal(sem("lo_ready"))
        y_ready = Signal(sem("y_ready"))
        stats_ready = Signal(sem("stats_ready"))
        mv_ready = Signal(sem("mv_ready"))
        veps_ready = Signal(sem("veps_ready"))
        rstd_ready = Signal(sem("rstd_ready"))
        mr_ready = Signal(sem("mr_ready"))
        shift_ready = Signal(sem("shift_ready"))
        normed = Signal(sem("normed"), 2)
        every = [x_loaded, res_loaded, mask_loaded, saved, xt_ready, hi_ready, lo_ready, y_ready, stats_ready,
                 mv_ready, veps_ready, rstd_ready, mr_ready, shift_ready, normed]
        w_loaded = [sem(f"w_loaded{i}") for i in range(2)]
        small_loaded = sem("small_loaded")
        w_hi_ready = sem("w_hi_ready")
        w_lo_ready = sem("w_lo_ready")
        prepared = sem("prepared")
        prep_step = sem("prep_step")
        const_ready = sem("const_ready")
        pick_ready = sem("pick_ready")
        count = {"w": 0, "small": 0, "prep": 0, "prepared": 0}

        def pipeline(eng, first, step, last):
            first(Graph(0, 0))
            step(Graph(0, 1))
            step(Graph(1, 0))
            with eng.Fori(1, (B - 2) // 2) as i:
                step(Graph(i, 1))
                step(Graph(i + 1, 0))
            last(Graph((B - 2) // 2, 1))

        def split_product(dst, lhs_hi, lhs_lo, w, more):
            for k in range(KC):
                nc.tensor.matmul(dst, lhs_hi(k), w_hi[:, w, k, :], start=(k == 0), stop=False)
                nc.tensor.matmul(dst, lhs_hi(k), w_lo[:, w, k, :], start=False, stop=False)
                last = nc.tensor.matmul(dst, lhs_lo(k), w_hi[:, w, k, :], start=False,
                                        stop=(k == KC - 1 and not more))
            return last

        def add_bias(dst, which, **kw):
            return nc.tensor.matmul(dst, ones_row[:, :], bias_row[:, which, :], start=False, stop=True, **kw)

        def project(which_w, hi, lo, bias=None):
            for t in range(NT):
                last = split_product(ps_h[:, t, 0:C], lambda k: hi[:, k, t * P:(t + 1) * P],
                                     lambda k: lo[:, k, t * P:(t + 1) * P], which_w, bias is not None)
                if bias is not None:
                    last = add_bias(ps_h[:, t, 0:C], bias)
            return last

        def transpose_tiles(src):
            for t in range(NT):
                for k in range(KC):
                    last = nc.tensor.transpose(tr_ps[:, k, t * P:(t + 1) * P], src[:, t, k * P:(k + 1) * P],
                                               ident[:, :])
            return last

        def normalise_stats(graph):
            nc.vector.wait_ge(y_ready.sem, y_ready.at(graph))
            for t in range(NT):
                last = nc.vector.bn_stats(stats[:, t, :], y[:, t, :])
            last.then_inc(stats_ready.sem, 1)

        def settle(graph):
            nc.vector.wait_ge(stats_ready.sem, stats_ready.at(graph))
            nc.vector.tensor_copy(settled[:, :], minus_one[:, :])

        def normalise_moments(graph):
            for t in range(NT):
                last = nc.vector.bn_aggr(mean_var[:, t, :], stats[:, t, :])
            last.then_inc(mv_ready.sem, 1)

        def normalise_factors(graph, eps):
            nc.gpsimd.wait_ge(mv_ready.sem, mv_ready.at(graph))
            nc.gpsimd.tensor_tensor(var_eps[:, :], mean_var[:, :, 1], eps, ALU.add).then_inc(veps_ready.sem, 1)
            nc.gpsimd.wait_ge(veps_ready.sem, veps_ready.at(graph))
            nc.gpsimd.tensor_tensor(rstd[:, :], var_eps[:, :], minus_half[:, :], ALU.pow)\
                .then_inc(rstd_ready.sem, 1)
            nc.gpsimd.wait_ge(rstd_ready.sem, rstd_ready.at(graph))
            nc.gpsimd.tensor_tensor(mean_rstd[:, :], mean_var[:, :, 0], rstd[:, :], ALU.mult)\
                .then_inc(mr_ready.sem, 1)
            nc.gpsimd.wait_ge(mr_ready.sem, mr_ready.at(graph))
            nc.gpsimd.tensor_tensor(shift[:, :], mean_rstd[:, :], minus_one[:, :], ALU.mult)\
                .then_inc(shift_ready.sem, 1)

        def normalise_apply(graph):
            nc.scalar.wait_ge(shift_ready.sem, shift_ready.at(graph))
            nc.scalar.wait_ge(saved.of(Graph(graph.half - 1, graph.p)), saved.at(Graph(graph.half - 1, graph.p)))
            for t in range(NT):
                nc.scalar.activation(x_out[:, graph.p, t, :], y[:, t, :], ACT.Identity, bias=shift[:, t:t + 1],
                                     scale=rstd[:, t:t + 1]).then_inc(normed.sem, 1)

        def load_x(sp, layer, graph):
            sp.wait_ge(xt_ready.sem, xt_ready.at(Graph(graph.half - 1, graph.p)))
            src = x_dram[graph.s] if layer == 0 else x_all[:, graph.s]
            sp.dma_start(x_in[:, graph.p], src).then_inc(x_loaded.of(graph), 16)

        def load_res(sp, layer, graph):
            sp.wait_ge(y_ready.sem, y_ready.at(Graph(graph.half - 1, graph.p)))
            src = x_dram[graph.s] if layer == 0 else x_all[:, graph.s]
            sp.dma_start(x_res[:, graph.p], src).then_inc(res_loaded.of(graph), 16)

        def store(sp, layer, graph):
            sp.wait_ge(normed.sem, normed.at(graph))
            dst = out_dram[graph.s] if layer == 3 else x_all[:, graph.s]
            sp.dma_start(dst, x_out[:, graph.p]).then_inc(saved.of(graph), 16)

        def sync_program(sp, layer):
            def first(g):
                load_x(sp, layer, g)
                load_x(sp, layer, g.next())
                load_x(sp, layer, g.next().next())
                load_res(sp, layer, g)

            def step(g):
                load_x(sp, layer, g.next().next())
                load_res(sp, layer, g)
                store(sp, layer, g.prev())

            first(Graph(0, 0))
            step(Graph(0, 1))
            step(Graph(1, 0))
            with sp.Fori(1, (B - 4) // 2) as i:
                step(Graph(i, 1))
                step(Graph(i + 1, 0))
            g = Graph((B - 4) // 2, 1)
            step(g)
            g = g.next()
            load_res(sp, layer, g)
            store(sp, layer, g.prev())
            g = g.next()
            load_res(sp, layer, g)
            store(sp, layer, g.prev())
            store(sp, layer, g)
            sp.wait_ge(saved.of(g.prev()), saved.at(g.prev()))
            sp.wait_ge(saved.of(g), saved.at(g))

        def prepare(block, mats, rows, extra_loads, extra_ops):
            @block.sync
            def _(sp):
                w0 = count["w"]
                for i, m in enumerate(mats):
                    if w0 + i >= 2:
                        sp.wait_ge(w_lo_ready, w0 + i - 1)
                    sp.dma_start(w_stage[:, (w0 + i) % 2], m).then_inc(w_loaded[(w0 + i) % 2], 16)
                for i, r in enumerate(rows):
                    for q in range(2):
                        sp.dma_start(row_in[q:q + 1, i, :].rearrange("o (h e) -> o h e", e=r.shape[-1]), r)\
                            .then_inc(small_loaded, 16)
                for dst, src in extra_loads:
                    sp.dma_start(dst, src).then_inc(small_loaded, 16)

            n_small = 16 * (2 * len(rows) + len(extra_loads))

            @block.scalar
            def _(act):
                for i in range(len(mats)):
                    n = count["w"] + i
                    act.wait_ge(w_loaded[n % 2], 16 * (n // 2 + 1))
                    nc.scalar.activation(w_hi[:, i], w_stage[:, n % 2], ACT.Copy, scale=WSCALE)\
                        .then_inc(w_hi_ready, 1)

            @block.vector
            def _(dve):
                def chain(ins):
                    count["prep"] += 1
                    ins.then_inc(prep_step, 1)
                    dve.wait_ge(prep_step, count["prep"])

                for i in range(len(mats)):
                    n = count["w"] + i
                    dve.wait_ge(w_hi_ready, n + 1)
                    nc.vector.scalar_tensor_tensor(w_lo[:, i], w_stage[:, n % 2], WSCALE, w_hi[:, i],
                                                   op0=ALU.mult, op1=ALU.subtract).then_inc(w_lo_ready, 1)
                dve.wait_ge(small_loaded, count["small"] + n_small)
                chain(nc.vector.tensor_scalar(row_64[:, :, :], row_in[:, :, :], WSCALE, None, ALU.mult))
                chain(nc.vector.tensor_copy(row_hi[:, :, :], row_64[:, :, :]))
                chain(nc.vector.tensor_scalar(row_lo[:, :, :], row_64[:, :, :], row_pq[:, 0:1], None, ALU.mult))
                chain(nc.vector.scalar_tensor_tensor(bias_row[:, :, :], row_hi[:, :, :], row_pq[:, 1:2],
                                                     row_lo[:, :, :], op0=ALU.mult, op1=ALU.add))
                extra_ops(dve, chain)
                dve.wait_ge(w_lo_ready, count["w"] + len(mats))
            count["w"] += len(mats)
            count["small"] += n_small

        w_att = buf_a[:, :].rearrange("p (i t n) -> p i t n", i=NW, t=NT)
        vals = buf_b[:, :].rearrange("p (q t h e) -> p q t h e", q=2, t=NT, h=HEADS)
        gate4 = buf_c[:, :].rearrange("p (q t c) -> p q t c", q=2, t=NT)
        z = buf_d[:, 0:NT * C].rearrange("p (t h e) -> p t h e", t=NT, h=HEADS)
        z_flat = buf_d[:, 0:NT * C].rearrange("p (t c) -> p t c", t=NT)
        z_exp = buf_d[:, NT * C:2 * NT * C].rearrange("p (t c) -> p t c", t=NT)
        th = buf_e[:, :].rearrange("p (t c) -> p t c", t=NT)
        thT = buf_f[:, :].rearrange("p (k n) -> p k n", k=KC)
        z_neg = buf_g[:, :].rearrange("p (t c) -> p t c", t=NT)
        w_flat = w_stage[:, :, :, :].rearrange("p i k c -> p (i k c)")
        delta = w_flat[:, 0:NT * C].rearrange("p (t c) -> p t c", t=NT)
        sd_ps = t_flat[:, 0:NT * 2 * HEADS].rearrange("p (t c) -> p t c", t=NT)
        sT_ps = t_flat[0:HEADS, N:2 * N]
        dT_ps = t_flat[0:HEADS, 2 * N:3 * N]
        dmax_ps = t_flat[:, 0:HEADS]

        h_ready = Signal(sem("h_ready"))
        th_ready = Signal(sem("th_ready"))
        tht_ready = Signal(sem("tht_ready"))
        hb_ready = Signal(sem("hb_ready"))
        tht_sb_ready = Signal(sem("tht_sb_ready"))
        sd_ps_ready = Signal(sem("sd_ps_ready"))
        sd_ready = Signal(sem("sd_ready"))
        sdt_ready = Signal(sem("sdt_ready"))
        dmax_ready = Signal(sem("dmax_ready"))
        spos_ready = Signal(sem("spos_ready"))
        diag_ready = Signal(sem("diag_ready"))
        dmax_ps_ready = Signal(sem("dmax_ps_ready"))
        b_ready = Signal(sem("b_ready"))
        b_hi_ready = Signal(sem("b_hi_ready"))
        b_rest_ready = Signal(sem("b_rest_ready"))
        b_mid_ready = Signal(sem("b_mid_ready"))
        parts_ready = Signal(sem("parts_ready"))
        drel_ready = Signal(sem("drel_ready"))
        gd_ready = Signal(sem("gd_ready"))
        vals_ready = Signal(sem("vals_ready"))
        gate_ps_ready = Signal(sem("gate_ps_ready"))
        gate_t_ready = Signal(sem("gate_t_ready"))
        gate_ready = Signal(sem("gate_ready"))
        bcast_ready = Signal(sem("bcast_ready"), PAIRS)
        w_ready = Signal(sem("w_ready"), HEADS)
        summed = Signal(sem("summed"), HEADS)
        rden_ready = Signal(sem("rden_ready"))
        z_ready = Signal(sem("z_ready"))
        zexp_ready = Signal(sem("zexp_ready"))
        zpos_ready = Signal(sem("zpos_ready"))
        zneg_ready = Signal(sem("zneg_ready"))
        elu_ready = Signal(sem("elu_ready"))
        delta_ready = Signal(sem("delta_ready"))
        gated_ready = Signal(sem("gated_ready"))
        gat_signals = [h_ready, th_ready, tht_ready, hb_ready, tht_sb_ready, sd_ps_ready, sd_ready, sdt_ready,
                       dmax_ready, spos_ready, diag_ready, dmax_ps_ready, b_ready, b_hi_ready, b_rest_ready,
                       b_mid_ready, parts_ready, drel_ready, gd_ready, vals_ready, gate_ps_ready, gate_t_ready,
                       gate_ready, bcast_ready, w_ready, summed, rden_ready, z_ready, zexp_ready, zpos_ready, zneg_ready,
                       elu_ready, delta_ready, gated_ready]

        def gat_layer(block, layer):
            def load_mask(act, graph):
                act.wait_ge(w_ready.sem, w_ready.at(Graph(graph.half - 1, graph.p)))
                act.dma_start(mask[:, graph.p], adjT_dram[graph.s]).then_inc(mask_loaded.of(graph), 16)

            @block.sync
            def _(sp):
                sync_program(sp, layer)

            @block.tensor
            def _(pe):
                def transpose_x(g):
                    pe.wait_ge(x_loaded.of(g), x_loaded.at(g))
                    pe.wait_ge(drel_ready.sem, drel_ready.at(g.prev()))
                    transpose_tiles(x_in[:, g.p]).then_inc(xt_ready.sem, 1)

                def values(g):
                    pe.wait_ge(lo_ready.sem, lo_ready.at(g))
                    pe.wait_ge(gate_t_ready.sem, gate_t_ready.at(g.prev()))
                    project(0, x_hi, x_lo).then_inc(h_ready.sem, 1)

                def transpose_th(g):
                    pe.wait_ge(th_ready.sem, th_ready.at(g))
                    transpose_tiles(th).then_inc(tht_ready.sem, 1)
                    for t in range(NT):
                        last = add_bias(ps_h[:, t, 0:C], 0, skip_group_check=True)
                    last.then_inc(hb_ready.sem, 1)

                def scores(g):
                    pe.wait_ge(tht_sb_ready.sem, tht_sb_ready.at(g))
                    for t in range(NT):
                        for k in range(KC):
                            last = nc.tensor.matmul(sd_ps[:, t, :], thT[:, k, t * P:(t + 1) * P],
                                                    score_mat[:, k, :], start=(k == 0), stop=(k == KC - 1))
                    last.then_inc(sd_ps_ready.sem, 1)

                def transpose_scores(g):
                    pe.wait_ge(sd_ready.sem, sd_ready.at(g))
                    for dst, c in ((sT_ps, 0), (dT_ps, HEADS)):
                        for t in range(NT):
                            last = nc.tensor.transpose(dst[:, t * P:(t + 1) * P], sd[:, t, c:c + HEADS], ident[:, :])
                    last.then_inc(sdt_ready.sem, 1)

                def broadcast_dmax(g):
                    pe.wait_ge(diag_ready.sem, diag_ready.at(g))
                    nc.tensor.matmul(dmax_ps, ones12[:, :], d_max_diag[:, :], start=True, stop=True)\
                        .then_inc(dmax_ps_ready.sem, 1)

                def gate(g):
                    pe.wait_ge(vals_ready.sem, vals_ready.at(g))
                    project(1, x_hi, x_lo, bias=1).then_inc(gate_ps_ready.sem, 1)

                def broadcast_b(g, j):
                    if j == 0:
                        pe.wait_ge(parts_ready.sem, parts_ready.at(g))
                    pe.wait_ge(w_ready.sem, w_ready.at(g, 2 * (j - 1)))
                    for h in range(2):
                        last = nc.tensor.matmul(ps_b[:, j % 2, h * N:(h + 1) * N], pick_head[:, 2 * j + h, :],
                                                b_parts[:, g.p, :], start=True, stop=True)
                    last.then_inc(bcast_ready.sem, 1)

                def sum_neighbours(g, j):
                    if j == 0:
                        pe.wait_ge(z_ready.sem, z_ready.at(g.prev()))
                    for h in (2 * j, 2 * j + 1):
                        pe.wait_ge(w_ready.sem, w_ready.at(g, h + 1))
                        for t in range(NT):
                            for m in range(NT):
                                last = nc.tensor.matmul(ps_o[:, t, h * EV:(h + 1) * EV],
                                                        w_att[:, h % NW, m, t * P:(t + 1) * P],
                                                        vals[:, g.p, m, h, :], start=(m == 0), stop=(m == NT - 1))
                        last.then_inc(summed.sem, 1)

                def step(g, front=True):
                    n = g.next()
                    broadcast_b(g, 0)
                    gate(g)
                    broadcast_b(g, 1)
                    if front:
                        transpose_x(n)
                    for j in range(PAIRS):
                        sum_neighbours(g, j)
                        if j + 2 < PAIRS:
                            broadcast_b(g, j + 2)
                        if front and j < 5:
                            (values, transpose_th, scores, transpose_scores, broadcast_dmax)[j](n)

                def first(g):
                    pe.wait_ge(prepared, count["prepared"])
                    transpose_x(g)
                    values(g)
                    transpose_th(g)
                    scores(g)
                    transpose_scores(g)
                    broadcast_dmax(g)
                    step(g)

                pipeline(pe, first, step, lambda g: step(g, front=False))

            @block.scalar
            def _(act):
                def split_hi(g):
                    act.wait_ge(xt_ready.sem, xt_ready.at(g))
                    act.wait_ge(gate_ps_ready.sem, gate_ps_ready.at(g.prev()))
                    nc.scalar.activation(x_hi[:, :, :], tr_ps, ACT.Copy).then_inc(hi_ready.sem, 1)

                def tanh_h(g):
                    act.wait_ge(h_ready.sem, h_ready.at(g))
                    nc.scalar.activation(th, ps_h[:, :, 0:C], ACT.Tanh, scale=1.0 / WSCALE).then_inc(th_ready.sem, 1)

                def keep_thT(g):
                    act.wait_ge(tht_ready.sem, tht_ready.at(g))
                    nc.scalar.activation(thT, tr_ps, ACT.Copy).then_inc(tht_sb_ready.sem, 1)

                def exp_b(g):
                    act.wait_ge(spos_ready.sem, spos_ready.at(g))
                    nc.scalar.activation(b_exp[:, :], s_pos[:, :], ACT.Exp, scale=-0.8).then_inc(b_ready.sem, 1)

                def exp_gd(g):
                    act.wait_ge(drel_ready.sem, drel_ready.at(g))
                    nc.scalar.activation(G[:, g.p], d_rel[:, :, :], ACT.Exp, scale=0.8)
                    nc.scalar.activation(D[:, :, :], d_rel[:, :, :], ACT.Exp, scale=0.2).then_inc(gd_ready.sem, 1)

                def gate(g):
                    act.wait_ge(gate_ps_ready.sem, gate_ps_ready.at(g))
                    nc.scalar.activation(gate4[:, g.p], ps_h[:, :, 0:C], ACT.Tanh, scale=0.5 / WSCALE)\
                        .then_inc(gate_t_ready.sem, 1)
                    act.wait_ge(gate_t_ready.sem, gate_t_ready.at(g))
                    nc.scalar.activation(gate4[:, g.p], gate4[:, g.p], ACT.Copy, scale=0.25, bias=0.25)\
                        .then_inc(gate_ready.sem, 1)

                def exp_z(g):
                    act.wait_ge(z_ready.sem, z_ready.at(g))
                    nc.scalar.activation(z_exp, z_flat, ACT.Exp).then_inc(zexp_ready.sem, 1)
                    act.wait_ge(zexp_ready.sem, zexp_ready.at(g))
                    nc.scalar.activation(z_flat, z_flat, ACT.Relu).then_inc(zpos_ready.sem, 1)

                def front(g):
                    tanh_h(g)
                    keep_thT(g)

                def step(g, front=True, back=True):
                    n, b = g.next(), g.prev()
                    if front:
                        load_mask(act, n)
                    if back:
                        exp_z(b)
                    gate(g)
                    if front:
                        split_hi(n)
                        tanh_h(n)
                        keep_thT(n)
                    if back:
                        normalise_apply(b)
                    if front:
                        exp_b(n)
                        exp_gd(n)

                def first(g):
                    load_mask(act, g)
                    split_hi(g)
                    tanh_h(g)
                    keep_thT(g)
                    exp_b(g)
                    exp_gd(g)
                    step(g, back=False)

                def last(g):
                    step(g, front=False)
                    exp_z(g)
                    normalise_apply(g)

                pipeline(act, first, step, last)

            @block.vector
            def _(dve):
                def split_lo(g):
                    dve.wait_ge(hi_ready.sem, hi_ready.at(g))
                    nc.vector.tensor_tensor(x_lo[:, :, :], tr_ps, x_hi[:, :, :], ALU.subtract)\
                        .then_inc(lo_ready.sem, 1)

                def keep_scores(g):
                    dve.wait_ge(sd_ps_ready.sem, sd_ps_ready.at(g))
                    nc.vector.tensor_copy(sd[:, :, :], sd_ps).then_inc(sd_ready.sem, 1)

                def max_scores(g):
                    dve.wait_ge(sdt_ready.sem, sdt_ready.at(g))
                    nc.vector.tensor_reduce(d_max[:, :], dT_ps, AX.X, ALU.max).then_inc(dmax_ready.sem, 1)
                    dve.wait_ge(dmax_ready.sem, dmax_ready.at(g))
                    nc.vector.tensor_scalar(s_pos[:, :], sT_ps, d_max[:, 0:1], 0.0, ALU.add, ALU.max)\
                        .then_inc(spos_ready.sem, 1)
                    nc.vector.tensor_scalar(d_max_diag[:, :], ident[0:HEADS, 0:HEADS], d_max[:, 0:1], None, ALU.mult)\
                        .then_inc(diag_ready.sem, 1)

                def split_b(g):
                    part = lambda q: b_parts[32 * q:32 * q + HEADS, g.p, :]
                    dve.wait_ge(b_ready.sem, b_ready.at(g))
                    nc.vector.tensor_copy(part(0), b_exp[:, :]).then_inc(b_hi_ready.sem, 1)
                    dve.wait_ge(b_hi_ready.sem, b_hi_ready.at(g))
                    nc.vector.tensor_tensor(b_rest[:, :], b_exp[:, :], part(0), ALU.subtract)\
                        .then_inc(b_rest_ready.sem, 1)
                    dve.wait_ge(b_rest_ready.sem, b_rest_ready.at(g))
                    nc.vector.tensor_copy(b_mid[:, :], b_rest[:, :]).then_inc(b_mid_ready.sem, 1)
                    nc.vector.tensor_copy(part(1), b_rest[:, :])
                    dve.wait_ge(b_mid_ready.sem, b_mid_ready.at(g))
                    nc.vector.tensor_tensor(part(2), b_rest[:, :], b_mid[:, :], ALU.subtract)\
                        .then_inc(parts_ready.sem, 1)

                def relative_scores(g):
                    dve.wait_ge(dmax_ps_ready.sem, dmax_ps_ready.at(g))
                    m = dmax_ps.rearrange("p (o h) -> p o h", o=1).to_broadcast([P, NT, HEADS])
                    nc.vector.tensor_tensor(d_rel[:, :, :], sd[:, :, HEADS:2 * HEADS], m, ALU.subtract)\
                        .then_inc(drel_ready.sem, 1)

                def scale_values(g):
                    dve.wait_ge(gd_ready.sem, gd_ready.at(g))
                    dve.wait_ge(hb_ready.sem, hb_ready.at(g))
                    h = ps_h[:, :, 0:C].rearrange("p t (h e) -> p t h e", e=E)
                    d = D[:, :, :].rearrange("p t (h o) -> p t h o", o=1)
                    nc.vector.tensor_scalar(vals[:, g.p, :, :, E:EV], d, WSCALE, None, ALU.mult)
                    nc.vector.tensor_tensor(vals[:, g.p, :, :, 0:E], h, d.to_broadcast([P, NT, HEADS, E]), ALU.mult)\
                        .then_inc(vals_ready.sem, 1)

                def weights(g, j):
                    if j == 0:
                        dve.wait_ge(mask_loaded.of(g), mask_loaded.at(g))
                    dve.wait_ge(bcast_ready.sem, bcast_ready.at(g, j + 1))
                    for i in range(2):
                        h = 2 * j + i
                        dve.wait_ge(summed.sem, summed.at(g, h - NW + 1))
                        for m in range(NT):
                            last = nc.vector.scalar_tensor_tensor(
                                w_att[:, h % NW, m, :], ps_b[:, j % 2, i * N:(i + 1) * N], G[:, g.p, m, h:h + 1],
                                mask[:, g.p, m, :], op0=ALU.max, op1=ALU.mult)
                        last.then_inc(w_ready.sem, 1)

                def divide(g):
                    dve.wait_ge(summed.sem, summed.at(g))
                    o = ps_o[:, :, 0:HEADS * EV].rearrange("p t (h e) -> p t h e", e=EV)
                    r = rden[:, :, :].rearrange("p t (h o) -> p t h o", o=1)
                    nc.vector.reciprocal(r, o[:, :, :, E:EV]).then_inc(rden_ready.sem, 1)
                    dve.wait_ge(rden_ready.sem, rden_ready.at(g))
                    nc.vector.tensor_tensor(z, o[:, :, :, 0:E], r.to_broadcast([P, NT, HEADS, E]), ALU.mult)\
                        .then_inc(z_ready.sem, 1)

                def negative_part(g):
                    dve.wait_ge(zexp_ready.sem, zexp_ready.at(g))
                    nc.vector.tensor_scalar(z_neg, z_exp, 1.0, -1.0, ALU.min, ALU.add).then_inc(zneg_ready.sem, 1)

                def front_end(g):
                    split_b(g)
                    relative_scores(g)
                    scale_values(g)

                def step(g, front=True, back=True):
                    n, b = g.next(), g.prev()
                    if back:
                        divide(b)
                    weights(g, 0)
                    if front:
                        split_lo(n)
                    if back:
                        negative_part(b)
                    weights(g, 1)
                    weights(g, 2)
                    if back:
                        normalise_stats(b)
                        dve.wait_ge(stats_ready.sem, stats_ready.at(b))
                    weights(g, 3)
                    if back:
                        normalise_moments(b)
                    if front:
                        keep_scores(n)
                    weights(g, 4)
                    if front:
                        max_scores(n)
                    weights(g, 5)
                    if front:
                        front_end(n)

                def first(g):
                    split_lo(g)
                    keep_scores(g)
                    max_scores(g)
                    front_end(g)
                    step(g, back=False)

                def last(g):
                    step(g, front=False)
                    divide(g)
                    negative_part(g)
                    normalise_stats(g)
                    settle(g)
                    normalise_moments(g)

                pipeline(dve, first, step, last)

            @block.gpsimd
            def _(pool):
                def back(g):
                    pool.wait_ge(zpos_ready.sem, zpos_ready.at(g))
                    pool.wait_ge(zneg_ready.sem, zneg_ready.at(g))
                    pool.wait_ge(normed.sem, normed.at(g.prev()))
                    nc.gpsimd.tensor_tensor(z_exp, z_flat, z_neg, ALU.add).then_inc(elu_ready.sem, 1)
                    pool.wait_ge(res_loaded.of(g), res_loaded.at(g))
                    pool.wait_ge(elu_ready.sem, elu_ready.at(g))
                    nc.gpsimd.tensor_tensor(delta, z_exp, x_res[:, g.p], ALU.subtract)\
                        .then_inc(delta_ready.sem, 1)
                    pool.wait_ge(gate_ready.sem, gate_ready.at(g))
                    pool.wait_ge(delta_ready.sem, delta_ready.at(g))
                    nc.gpsimd.tensor_tensor(z_neg, delta, gate4[:, g.p], ALU.mult)\
                        .then_inc(gated_ready.sem, 1)
                    pool.wait_ge(gated_ready.sem, gated_ready.at(g))
                    nc.gpsimd.tensor_tensor(y[:, :, :], z_neg, x_res[:, g.p], ALU.add).then_inc(y_ready.sem, 1)
                    normalise_factors(g, eps_half[:, :])

                def first(g):
                    pass

                pipeline(pool, first, lambda g: back(g.prev()), lambda g: (back(g.prev()), back(g)))

        probs = buf_a[:, 0:2 * NT * N].rearrange("p (i t k) -> p i t k", i=2, t=NT)
        probsT = buf_a[:, 2 * NT * N:4 * NT * N].rearrange("p (i t q) -> p i t q", i=2, t=NT)
        v_sb = buf_b[:, 0:2 * NT * MH * DV].rearrange("p (q t h e) -> p q t h e", q=2, t=NT, h=MH)
        qT = buf_c[:, :].rearrange("p (q k n) -> p q k n", q=2, k=KC)
        kT = buf_d[:, :].rearrange("p (q k n) -> p q k n", q=2, k=KC)
        att = buf_e[:, :].rearrange("p (t h e) -> p t h e", t=NT, h=MH)
        att_flat = buf_e[:, :].rearrange("p (t c) -> p t c", t=NT)
        att_parts = w_flat[:, 0:KC * N].bitcast(f16).rearrange("p (i k n) -> p i k n", i=2, k=KC)
        att_hi, att_lo = att_parts[:, 0], att_parts[:, 1]
        neg_mask = buf_f[:, 0:NT * N].bitcast(bf16).rearrange("p (q t k) -> p q t k", q=2, t=NT)
        qk_ps = ps_h[:, :, :].rearrange("p t c -> p (t c)")[:, 0:KC * N].rearrange("p (k n) -> p k n", k=KC)

        negm_ready = Signal(sem("negm_ready"))
        q_ps_ready = Signal(sem("q_ps_ready"))
        q_ready = Signal(sem("q_ready"))
        k_ps_ready = Signal(sem("k_ps_ready"))
        k_ready = Signal(sem("k_ready"))
        v_ps_ready = Signal(sem("v_ps_ready"))
        v_ready = Signal(sem("v_ready"))
        s_ready = Signal(sem("s_ready"), MH)
        max_ready = Signal(sem("max_ready"), MH)
        p_ready = Signal(sem("p_ready"), MH)
        pt_ps_ready = Signal(sem("pt_ps_ready"), MH)
        pt_dve = Signal(sem("pt_dve"), MH // 2)
        pt_act = Signal(sem("pt_act"), MH // 2)
        att_ps_ready = Signal(sem("att_ps_ready"), MH)
        mden_ready = Signal(sem("mden_ready"))
        att_ready = Signal(sem("att_ready"))
        attT_ready = Signal(sem("attT_ready"))
        atthi_ready = Signal(sem("atthi_ready"))
        attlo_ready = Signal(sem("attlo_ready"))
        out_ready = Signal(sem("out_ready"))

        def attention_layer(block, layer):
            def load_mask(act, graph):
                act.wait_ge(negm_ready.sem, negm_ready.at(Graph(graph.half - 1, graph.p)))
                act.dma_start(mask[:, graph.p], adj_dram[graph.s]).then_inc(mask_loaded.of(graph), 16)

            @block.sync
            def _(sp):
                sync_program(sp, layer)

            def wait_probsT(eng, g, h):
                half = pt_dve if h % 2 == 0 else pt_act
                eng.wait_ge(half.sem, half.at(g, h // 2 + 1))

            @block.tensor
            def _(pe):
                def transpose_x(g):
                    pe.wait_ge(x_loaded.of(g), x_loaded.at(g))
                    transpose_tiles(x_in[:, g.p]).then_inc(xt_ready.sem, 1)

                def project_T(which, done):
                    for e in range(KC):
                        for k in range(KC):
                            for n, (w, x) in enumerate(((w_hi, x_hi), (w_hi, x_lo), (w_lo, x_hi))):
                                last = nc.tensor.matmul(qk_ps[:, e, :], w[:, which, k, e * P:(e + 1) * P], x[:, k, :],
                                                        start=(k == 0 and n == 0), stop=(k == KC - 1 and n == 2))
                    last.then_inc(done.sem, 1)

                def project_q(g):
                    pe.wait_ge(lo_ready.sem, lo_ready.at(g))
                    pe.wait_ge(y_ready.sem, y_ready.at(Graph(g.half - 1, g.p)))
                    project_T(0, q_ps_ready)

                def project_k(g):
                    pe.wait_ge(q_ready.sem, q_ready.at(g))
                    project_T(1, k_ps_ready)

                def project_v(g):
                    pe.wait_ge(k_ready.sem, k_ready.at(g))
                    project(2, x_hi, x_lo, bias=0).then_inc(v_ps_ready.sem, 1)

                def score(g, h):
                    if h == 0:
                        pe.wait_ge(v_ready.sem, v_ready.at(g))
                        pe.wait_ge(negm_ready.sem, negm_ready.at(g))
                    if h >= 2:
                        wait_probsT(pe, g, h - 2)
                    else:
                        wait_probsT(pe, g.prev(), MH + h - 2)
                    r = (h % 2) * DH
                    for t in range(NT):
                        dst = ps_b[:, h % 2, t * N:(t + 1) * N]
                        nc.tensor.matmul(dst, qT[r:r + DH, g.p, h // 2, t * P:(t + 1) * P],
                                         kT[r:r + DH, g.p, h // 2, :], start=True, stop=False)
                        last = nc.tensor.matmul(dst, ident_bf[:, :], neg_mask[:, g.p, t, :], start=False, stop=True)
                    last.then_inc(s_ready.sem, 1)

                def transpose_probs(g, h):
                    pe.wait_ge(p_ready.sem, p_ready.at(g, h + 1))
                    for t in range(NT):
                        for k in range(NT):
                            last = nc.tensor.transpose(ps_b[:, h % 2, k * N + t * P:k * N + (t + 1) * P],
                                                       probs[:, h % 2, t, k * P:(k + 1) * P], ident[:, :])
                    last.then_inc(pt_ps_ready.sem, 1)

                def attend(g, h):
                    wait_probsT(pe, g, h)
                    if h == 0:
                        pe.wait_ge(att_ready.sem, att_ready.at(g.prev()))
                    for t in range(NT):
                        for k in range(NT):
                            last = nc.tensor.matmul(ps_o[:, t, h * DV:(h + 1) * DV],
                                                    probsT[:, h % 2, k, t * P:(t + 1) * P], v_sb[:, g.p, k, h, :],
                                                    start=(k == 0), stop=(k == NT - 1))
                    last.then_inc(att_ps_ready.sem, 1)

                def transpose_att(g):
                    pe.wait_ge(att_ready.sem, att_ready.at(g))
                    transpose_tiles(att_flat).then_inc(attT_ready.sem, 1)

                def project_out(g):
                    pe.wait_ge(attlo_ready.sem, attlo_ready.at(g))
                    project(3, att_hi, att_lo, bias=1).then_inc(out_ready.sem, 1)

                def step(g, front=True, back=True):
                    n, b = g.next(), g.prev()
                    score(g, 0)
                    if back:
                        transpose_att(b)
                    score(g, 1)
                    transpose_probs(g, 0)
                    if back:
                        pe.wait_ge(attlo_ready.sem, attlo_ready.at(b))
                    if front:
                        transpose_x(n)
                    attend(g, 0)
                    for h in range(1, MH):
                        if h == 1 and back:
                            project_out(b)
                        if front and h in (2, 3, 4):
                            (project_q, project_k, project_v)[h - 2](n)
                        if h + 1 < MH:
                            score(g, h + 1)
                        transpose_probs(g, h)
                        attend(g, h)

                def first(g):
                    pe.wait_ge(prepared, count["prepared"])
                    transpose_x(g)
                    project_q(g)
                    project_k(g)
                    project_v(g)
                    step(g, back=False)

                def last(g):
                    step(g, front=False)
                    transpose_att(g)
                    project_out(g)

                pipeline(pe, first, step, last)

            @block.scalar
            def _(act):
                def split_hi(g):
                    act.wait_ge(xt_ready.sem, xt_ready.at(g))
                    act.wait_ge(v_ps_ready.sem, v_ps_ready.at(g.prev()))
                    nc.scalar.activation(x_hi[:, :, :], tr_ps, ACT.Copy).then_inc(hi_ready.sem, 1)

                def keep_q(g):
                    act.wait_ge(q_ps_ready.sem, q_ps_ready.at(g))
                    for e in range(KC):
                        last = nc.scalar.activation(qT[:, g.p, e, :], qk_ps[:, e, :], ACT.Identity,
                                                    bias=bias_col[:, 0, e:e + 1], scale=1.0 / (WSCALE * DH ** 0.5))
                    last.then_inc(q_ready.sem, 1)

                def keep_v(g):
                    act.wait_ge(v_ps_ready.sem, v_ps_ready.at(g))
                    src = ps_h[:, :, 0:C].rearrange("p t (h e) -> p t h e", e=DH)
                    nc.scalar.activation(v_sb[:, g.p, :, :, 0:DH], src, ACT.Copy, scale=1.0 / WSCALE)\
                        .then_inc(v_ready.sem, 1)

                def exp_scores(g, h):
                    act.wait_ge(max_ready.sem, max_ready.at(g, h + 1))
                    act.wait_ge(pt_ps_ready.sem, pt_ps_ready.at(g, h - 1))
                    for t in range(NT):
                        last = nc.scalar.activation(probs[:, h % 2, t, :], ps_b[:, h % 2, t * N:(t + 1) * N],
                                                    ACT.Exp, bias=row_max[:, h % 2, t:t + 1])
                    last.then_inc(p_ready.sem, 1)

                def keep_probsT(g, h):
                    act.wait_ge(pt_ps_ready.sem, pt_ps_ready.at(g, h + 1))
                    act.wait_ge(att_ps_ready.sem, att_ps_ready.at(g, h - 1))
                    nc.scalar.activation(probsT[:, h % 2].rearrange("p t q -> p (t q)"), ps_b[:, h % 2, :],
                                         ACT.Copy).then_inc(pt_act.sem, 1)

                def att_split_hi(g):
                    act.wait_ge(attT_ready.sem, attT_ready.at(g))
                    act.wait_ge(out_ready.sem, out_ready.at(g.prev()))
                    nc.scalar.activation(att_hi[:, :, :], tr_ps, ACT.Copy).then_inc(atthi_ready.sem, 1)

                def step(g, front=True, back=True):
                    n, b = g.next(), g.prev()
                    if front:
                        load_mask(act, n)
                    exp_scores(g, 0)
                    if back:
                        att_split_hi(b)
                    exp_scores(g, 1)
                    if front:
                        split_hi(n)
                    keep_probsT(g, 1)
                    exp_scores(g, 2)
                    if front:
                        keep_q(n)
                    exp_scores(g, 3)
                    keep_probsT(g, 3)
                    if back:
                        normalise_apply(b)
                    exp_scores(g, 4)
                    if front:
                        keep_v(n)
                    exp_scores(g, 5)
                    keep_probsT(g, 5)

                def first(g):
                    load_mask(act, g)
                    split_hi(g)
                    keep_q(g)
                    keep_v(g)
                    step(g, back=False)

                def last(g):
                    step(g, front=False)
                    att_split_hi(g)
                    normalise_apply(g)

                pipeline(act, first, step, last)

            @block.vector
            def _(dve):
                def split_lo(g):
                    dve.wait_ge(hi_ready.sem, hi_ready.at(g))
                    nc.vector.tensor_tensor(x_lo[:, :, :], tr_ps, x_hi[:, :, :], ALU.subtract)\
                        .then_inc(lo_ready.sem, 1)

                def negate_mask(g):
                    dve.wait_ge(mask_loaded.of(g), mask_loaded.at(g))
                    dve.wait_ge(s_ready.sem, s_ready.at(Graph(g.half - 1, g.p)))
                    nc.vector.tensor_scalar(neg_mask[:, g.p], mask[:, g.p], -1.0, NEG, ALU.add, ALU.mult)\
                        .then_inc(negm_ready.sem, 1)

                def keep_k(g):
                    dve.wait_ge(k_ps_ready.sem, k_ps_ready.at(g))
                    for e in range(KC):
                        last = nc.vector.tensor_scalar(kT[:, g.p, e, :], qk_ps[:, e, :], 1.0 / WSCALE,
                                                       bias_col[:, 1, e:e + 1], ALU.mult, ALU.add)
                    last.then_inc(k_ready.sem, 1)

                def max_scores(g, h):
                    dve.wait_ge(s_ready.sem, s_ready.at(g, h + 1))
                    dve.wait_ge(p_ready.sem, p_ready.at(g, h - 1))
                    nc.vector.tensor_reduce(row_max[:, h % 2, :], ps_b[:, h % 2, :].rearrange("p (t k) -> p t k", t=NT),
                                            AX.X, ALU.max, negate=True).then_inc(max_ready.sem, 1)

                def keep_probsT(g, h):
                    dve.wait_ge(pt_ps_ready.sem, pt_ps_ready.at(g, h + 1))
                    dve.wait_ge(att_ps_ready.sem, att_ps_ready.at(g, h - 1))
                    nc.vector.tensor_copy(probsT[:, h % 2].rearrange("p t q -> p (t q)"), ps_b[:, h % 2, :])\
                        .then_inc(pt_dve.sem, 1)

                def divide(g):
                    dve.wait_ge(att_ps_ready.sem, att_ps_ready.at(g))
                    dve.wait_ge(attT_ready.sem, attT_ready.at(g.prev()))
                    o = ps_o[:, :, 0:MH * DV].rearrange("p t (h e) -> p t h e", e=DV)
                    r = rden[:, :, 0:MH].rearrange("p t (h o) -> p t h o", o=1)
                    nc.vector.reciprocal(r, o[:, :, :, DH:DV]).then_inc(mden_ready.sem, 1)
                    dve.wait_ge(mden_ready.sem, mden_ready.at(g))
                    nc.vector.tensor_tensor(att, o[:, :, :, 0:DH], r.to_broadcast([P, NT, MH, DH]), ALU.mult)\
                        .then_inc(att_ready.sem, 1)

                def att_split_lo(g):
                    dve.wait_ge(atthi_ready.sem, atthi_ready.at(g))
                    nc.vector.tensor_tensor(att_lo[:, :, :], tr_ps, att_hi[:, :, :], ALU.subtract)\
                        .then_inc(attlo_ready.sem, 1)

                def add_residual(g):
                    dve.wait_ge(out_ready.sem, out_ready.at(g))
                    dve.wait_ge(res_loaded.of(g), res_loaded.at(g))
                    dve.wait_ge(normed.sem, normed.at(g.prev()))
                    nc.vector.scalar_tensor_tensor(y[:, :, :], ps_h[:, :, 0:C], 1.0 / WSCALE, x_res[:, g.p],
                                                   op0=ALU.mult, op1=ALU.add).then_inc(y_ready.sem, 1)

                def step(g, front=True, back=True):
                    n, b = g.next(), g.prev()
                    if back:
                        divide(b)
                    max_scores(g, 0)
                    if back:
                        att_split_lo(b)
                    max_scores(g, 1)
                    keep_probsT(g, 0)
                    if front:
                        split_lo(n)
                    if back:
                        add_residual(b)
                    max_scores(g, 2)
                    if back:
                        normalise_stats(b)
                        dve.wait_ge(stats_ready.sem, stats_ready.at(b))
                    keep_probsT(g, 2)
                    if back:
                        normalise_moments(b)
                    max_scores(g, 3)
                    if front:
                        keep_k(n)
                        negate_mask(n)
                    max_scores(g, 4)
                    keep_probsT(g, 4)
                    max_scores(g, 5)

                def first(g):
                    split_lo(g)
                    keep_k(g)
                    negate_mask(g)
                    step(g, back=False)

                def last(g):
                    step(g, front=False)
                    divide(g)
                    att_split_lo(g)
                    add_residual(g)
                    normalise_stats(g)
                    settle(g)
                    normalise_moments(g)

                pipeline(dve, first, step, last)

            @block.gpsimd
            def _(pool):
                def step(g, front=True, back=True):
                    if back:
                        normalise_factors(g.prev(), eps_whole[:, :])

                def first(g):
                    pass

                def last(g):
                    step(g)
                    normalise_factors(g, eps_whole[:, :])

                pipeline(pool, first, step, last)

        def after_layer(signals):
            for sig in signals:
                sig.base += 16 * (B // 2) if isinstance(sig, ParitySignal) else sig.per * B

        def weights_of(name):
            return a[name].rearrange("(k p) c -> p k c", p=P)

        def gat_extra(layer):
            loads = [(w_score[:, 0, :], a[f"L{layer}_gnn_wsrc"]), (w_score[:, 1, :], a[f"L{layer}_gnn_wdst"])]

            def ops(dve, chain):
                for i in range(2):
                    w = w_score[:, i, :].rearrange("p (k o) -> p k o", o=1).to_broadcast([P, KC, HEADS])
                    ins = nc.vector.tensor_tensor(score_mat[:, :, i * HEADS:(i + 1) * HEADS], head_of[:, :, :], w,
                                                  ALU.mult)
                    chain(ins)
            return loads, ops

        for layer in range(4):
            with nc.Block() as block:
                if layer == 0:
                    @block.sync
                    def _(sp):
                        sp.dma_start(ident[:, :], a["c_ident"]).then_inc(small_loaded, 16)
                        sp.dma_start(head_of[:, :, :], a["c_head_of"]).then_inc(small_loaded, 16)
                        sp.dma_start(part_of[:, :], a["c_part_of"]).then_inc(small_loaded, 16)
                        sp.dma_start(row_pq[:, :], a["c_row_pq"]).then_inc(small_loaded, 16)
                        sp.wait_ge(small_loaded, 64)

                    @block.gpsimd
                    def _(pool):
                        nc.gpsimd.memset(ones12[:, :], 1.0)
                        nc.gpsimd.memset(ones_row[:, :], 1.0)
                        nc.gpsimd.memset(minus_half[:, :], -0.5)
                        nc.gpsimd.memset(minus_one[:, :], -1.0)
                        nc.gpsimd.memset(eps_whole[:, :], EPS)
                        nc.gpsimd.memset(eps_half[:, :], EPS / 4)
                        nc.gpsimd.memset(b_parts[:, :, :], 0.0).then_inc(const_ready, 1)
                        pool.wait_ge(const_ready, 1)

                    @block.vector
                    def _(dve):
                        dve.wait_ge(small_loaded, 64)
                        nc.vector.tensor_copy(ident_bf[:, :], ident[:, :])
                        src = part_of[:, :].rearrange("p (h o) -> p h o", o=1).to_broadcast([96, HEADS, P])
                        nc.vector.tensor_copy(pick_head[:, :, :], src).then_inc(pick_ready, 1)
                        dve.wait_ge(pick_ready, 1)
                    count["small"] = 64
                if layer != 1:
                    mats = [weights_of(f"L{layer}_gnn_W"), weights_of(f"L{layer}_gnn_H_w")]
                    rows = [a[f"L{layer}_gnn_b"].rearrange("(o h e) -> o h e", o=1, h=1).to_broadcast([1, HEADS, E]),
                            a[f"L{layer}_gnn_H_b"].rearrange("(o h e) -> o h e", o=1, h=1)]
                    loads, ops = gat_extra(layer)
                else:
                    mats = [weights_of(f"L1_gnn_{w}") for w in ("Wq", "Wk", "Wv", "Wf")]
                    rows = [a[f"L1_gnn_{w}"].rearrange("(o h e) -> o h e", o=1, h=1) for w in ("bv", "bf")]
                    loads = [(bias_col[:, 0, :], a["L1_gnn_bq"]),
                             (bias_col[:, 1, :], a["L1_gnn_bk"])]

                    def ops(dve, chain):
                        chain(nc.vector.tensor_scalar(bias_col[:, 0, :], bias_col[:, 0, :], 1.0 / DH ** 0.5, None,
                                                      ALU.mult))
                        chain(nc.vector.memset(v_sb[:, :, :, :, DH:DV], 1.0))
                prepare(block, mats, rows, loads, ops)
            with nc.Block() as block:
                if layer == 1:
                    attention_layer(block, layer)
                    after_layer(every)
                else:
                    gat_layer(block, layer)
                    after_layer(every + gat_signals)


_WEIGHTS = ["L0_gnn_W", "L0_gnn_b", "L0_gnn_w_src", "L0_gnn_w_dst", "L0_gnn_H_w", "L0_gnn_H_b", "L1_gnn_Wq",
            "L1_gnn_bq", "L1_gnn_Wk", "L1_gnn_bk", "L1_gnn_Wv", "L1_gnn_bv", "L1_gnn_Wf", "L1_gnn_bf", "L2_gnn_W",
            "L2_gnn_b", "L2_gnn_w_src", "L2_gnn_w_dst", "L2_gnn_H_w", "L2_gnn_H_b", "L3_gnn_W", "L3_gnn_b",
            "L3_gnn_w_src", "L3_gnn_w_dst", "L3_gnn_H_w", "L3_gnn_H_b"]


def kernel(**inputs):
    import numpy as np
    import concourse.bacc as bacc
    from concourse import mybir as _mybir
    from concourse.bass_utils import run_bass_kernel_spmd

    arrays = {"x": np.asarray(inputs["x"])}
    adj = np.asarray(inputs["adj"])
    arrays["adj"] = adj
    arrays["adjT"] = adj.transpose(0, 2, 1)
    for name in _WEIGHTS:
        w = np.asarray(inputs[name])
        if name.endswith("gnn_W"):
            w = w.transpose(1, 0, 2).reshape(w.shape[1], -1)
        elif name.endswith("H_w"):
            w = w.T
        elif name.endswith(("w_src", "w_dst")):
            w = w.reshape(-1, 128).T
            name = name.replace("w_", "w")
        elif name.endswith(("bq", "bk")):
            w = w.reshape(-1, 128).T
        arrays[name] = w
    heads, e, chunks = 12, 32, 3
    p = np.arange(128)
    arrays["c_ident"] = np.eye(128, dtype=np.float32)
    arrays["c_head_of"] = np.stack([((k * 128 + p)[:, None] // e == np.arange(heads)[None]) for k in range(chunks)],
                                   axis=1).astype(np.float32)
    arrays["c_part_of"] = (p[:96, None] % 32 == np.arange(heads)[None]).astype(np.float32)
    arrays["c_row_pq"] = np.array([[0.0, 1.0], [1.0, -1.0]], np.float32)

    nc = bacc.Bacc("TRN2", target_bir_lowering=False, num_devices=1)
    args, ins = {}, {}
    for name, v in arrays.items():
        v = np.ascontiguousarray(v)
        ins[f"in_{name}"] = v
        args[name] = nc.dram_tensor(f"in_{name}", v.shape, _mybir.dt.from_np(v.dtype), kind="ExternalInput").ap()
    out = nc.dram_tensor("out_x", arrays["x"].shape, _mybir.dt.float32, kind="ExternalOutput").ap()
    residual_graph_layers(nc, args, out)
    r = run_bass_kernel_spmd(nc, [ins], core_ids=[0])
    return r.results[0]["out_x"]
```

```python
import concourse.bass as bass
from concourse import mybir
from contextlib import ExitStack

P = 128
WSCALE = 64.0
EPS = 1e-5
NEG = 9.0e15


class Graph:

    def __init__(self, half, parity):
        self.half, self.p = half, parity
        self.s = half * 2 + parity

    def next(self):
        return Graph(self.half, 1) if self.p == 0 else Graph(self.half + 1, 0)

    def prev(self):
        return Graph(self.half, 0) if self.p == 1 else Graph(self.half - 1, 1)


class Signal:

    def __init__(self, sem, per=1):
        self.sem, self.per, self.base = sem, per, 0

    def at(self, graph, k=None):
        value = graph.s * self.per + (self.base + (self.per if k is None else k))
        return max(value, 0) if isinstance(value, int) else value


class ParitySignal:

    def __init__(self, sems):
        self.sems, self.base = sems, 0

    def of(self, graph):
        return self.sems[graph.p]

    def at(self, graph):
        value = graph.half * 16 + (self.base + 16)
        return max(value, 0) if isinstance(value, int) else value


def residual_graph_layers(nc, a, out):
    f32, f16, bf16, u8 = mybir.dt.float32, mybir.dt.float16, mybir.dt.bfloat16, mybir.dt.uint8
    ALU, ACT, AX = mybir.AluOpType, mybir.ActivationFunctionType, mybir.AxisListType
    B, N, C = a["x"].shape
    NT, KC = N // P, C // P
    HEADS = 12
    E = C // HEADS
    EV = E + 1
    PAIRS = HEADS // 2
    MH = 6
    DH = C // MH
    DV = DH + 1
    NW = 4
    BANK = 512
    x_dram = a["x"].rearrange("b (t p) c -> b p t c", p=P)
    out_dram = out.rearrange("b (t p) c -> b p t c", p=P)
    adj_dram = a["adj"].rearrange("b (t p) m -> b p t m", p=P)
    adjT_dram = a["adjT"].rearrange("b (t p) n -> b p t n", p=P)

    ctx = ExitStack()
    with ctx:
        def sb(name, shape, dt=f32):
            return ctx.enter_context(nc.sbuf_tensor(name, shape, dt))

        def sem(name):
            return ctx.enter_context(nc.semaphore(name))

        x_all = sb("x_all", [P, B, NT, C])
        x_in = sb("x_in", [P, 2, NT, C])
        x_res = sb("x_res", [P, 2, NT, C])
        mask = sb("mask", [P, 2, NT, N], u8)
        x_hi = sb("x_hi", [P, 2, KC, N], f16)
        x_lo = sb("x_lo", [P, 2, KC, N], f16)
        w_stage = sb("w_stage", [P, 2, KC, C])
        w_hi = sb("w_hi", [P, 4, KC, C], f16)
        w_lo = sb("w_lo", [P, 4, KC, C], f16)
        ident = sb("ident", [P, P])
        ident_bf = sb("ident_bf", [P, P], bf16)
        head_of = sb("head_of", [P, KC, HEADS])
        part_of = sb("part_of", [96, HEADS])
        pick_head = sb("pick_head", [96, HEADS, P], bf16)
        w_score = sb("w_score", [P, 2, KC])
        score_mat = sb("score_mat", [P, KC, 2 * HEADS])
        ones12 = sb("ones12", [HEADS, P])
        row_pq = sb("row_pq", [2, 2])
        row_hi = sb("row_hi", [2, 2, C], f16)
        bias_row = sb("bias_row", [2, 2, C], f16)
        ones_row = sb("ones_row", [2, P], f16)
        bias_col = sb("bias_col", [P, 2, KC])
        minus_half = sb("minus_half", [P, NT])
        wscale = sb("wscale", [P, NT, HEADS, 1])
        minus_one = sb("minus_one", [P, NT])
        eps_whole = sb("eps_whole", [P, NT])
        eps_half = sb("eps_half", [P, NT])
        sd = sb("sd", [P, NT, 2 * HEADS])
        d_max = sb("d_max", [HEADS, 1])
        d_max_diag = sb("d_max_diag", [HEADS, HEADS])
        s_pos = sb("s_pos", [HEADS, N])
        b_exp = sb("b_exp", [HEADS, N])
        b_rest = sb("b_rest", [HEADS, N])
        b_mid = sb("b_mid", [HEADS, N], bf16)
        b_parts = sb("b_parts", [96, 2, N], bf16)
        d_rel = sb("d_rel", [P, NT, HEADS])
        G = sb("G", [P, 2, NT, HEADS])
        D = sb("D", [P, NT, HEADS])
        rden = sb("rden", [P, NT, HEADS])
        row_max = sb("row_max", [P, 2, NT])
        settled = sb("settled", [P, NT])
        stats = sb("stats", [P, NT, 6])
        mean_var = sb("mean_var", [P, NT, 2])
        var_eps = sb("var_eps", [P, NT])
        rstd = sb("rstd", [P, NT])
        mean_rstd = sb("mean_rstd", [P, NT])
        shift = sb("shift", [P, NT])
        buf_a = sb("buf_a", [P, NW * NT * N])
        buf_b = sb("buf_b", [P, 2 * NT * HEADS * EV])
        buf_c = sb("buf_c", [P, 2 * NT * C])
        buf_d = sb("buf_d", [P, 2 * NT * C])
        buf_e = sb("buf_e", [P, NT * C])
        buf_f = sb("buf_f", [P, NT * C])
        buf_g = sb("buf_g", [P, NT * C])
        row_in, row_64, row_lo = (b[0:2, :].rearrange("p (i c) -> p i c", i=2) for b in (buf_e, buf_f, buf_g))
        y = sb("y", [P, NT, C])
        x_out = sb("x_out", [P, 2, NT, C])
        def ps(name):
            return ctx.enter_context(nc.psum_tensor(name, [P, 2, BANK], f32))

        ps_t, ps_h, ps_b, ps_o = ps("ps_t"), ps("ps_h"), ps("ps_b"), ps("ps_o")
        t_flat = ps_t[:, :, :].rearrange("p t c -> p (t c)")
        tr_ps = t_flat[:, 0:KC * N].rearrange("p (k n) -> p k n", k=KC)

        x_loaded = ParitySignal([sem("x_loaded0"), sem("x_loaded1")])
        res_loaded = ParitySignal([sem("res_loaded0"), sem("res_loaded1")])
        mask_loaded = ParitySignal([sem("mask_loaded0"), sem("mask_loaded1")])
        saved = ParitySignal([sem("saved0"), sem("saved1")])
        xt_ready = Signal(sem("xt_ready"))
        hi_ready = Signal(sem("hi_ready"))
        lo_ready = Signal(sem("lo_ready"))
        y_ready = Signal(sem("y_ready"))
        stats_ready = Signal(sem("stats_ready"))
        mv_ready = Signal(sem("mv_ready"))
        veps_ready = Signal(sem("veps_ready"))
        rstd_ready = Signal(sem("rstd_ready"))
        mr_ready = Signal(sem("mr_ready"))
        shift_ready = Signal(sem("shift_ready"))
        normed = Signal(sem("normed"), 2)
        every = [x_loaded, res_loaded, mask_loaded, saved, xt_ready, hi_ready, lo_ready, y_ready, stats_ready,
                 mv_ready, veps_ready, rstd_ready, mr_ready, shift_ready, normed]
        w_loaded = [sem(f"w_loaded{i}") for i in range(2)]
        small_loaded = sem("small_loaded")
        w_hi_ready = sem("w_hi_ready")
        w_lo_ready = sem("w_lo_ready")
        prepared = sem("prepared")
        prep_step = sem("prep_step")
        const_ready = sem("const_ready")
        pick_ready = sem("pick_ready")
        count = {"w": 0, "small": 0, "prep": 0, "prepared": 0}

        def pipeline(eng, first, step, last):
            first(Graph(0, 0))
            step(Graph(0, 1))
            step(Graph(1, 0))
            step(Graph(1, 1))
            with eng.Fori(2, (B - 2) // 2) as i:
                step(Graph(i, 0))
                step(Graph(i, 1))
            last(Graph((B - 2) // 2, 1))

        def split_product(dst, lhs_hi, lhs_lo, w, more):
            for k in range(KC):
                nc.tensor.matmul(dst, lhs_hi(k), w_hi[:, w, k, :], start=(k == 0), stop=False)
                nc.tensor.matmul(dst, lhs_hi(k), w_lo[:, w, k, :], start=False, stop=False)
                last = nc.tensor.matmul(dst, lhs_lo(k), w_hi[:, w, k, :], start=False,
                                        stop=(k == KC - 1 and not more))
            return last

        def add_bias(dst, which, **kw):
            return nc.tensor.matmul(dst, ones_row[:, :], bias_row[:, which, :], start=False, stop=True, **kw)

        def project(which_w, hi, lo, tile=None, bias=None):
            for t in range(NT) if tile is None else (tile,):
                last = split_product(ps_h[:, t, 0:C], lambda k: hi[:, k, t * P:(t + 1) * P],
                                     lambda k: lo[:, k, t * P:(t + 1) * P], which_w, bias is not None)
                if bias is not None:
                    last = add_bias(ps_h[:, t, 0:C], bias)
            return last

        def transpose_tiles(src):
            for t in range(NT):
                for k in range(KC):
                    last = nc.tensor.transpose(tr_ps[:, k, t * P:(t + 1) * P], src[:, t, k * P:(k + 1) * P],
                                               ident[:, :])
            return last

        def normalise_stats(graph):
            nc.vector.wait_ge(y_ready.sem, y_ready.at(graph))
            for t in range(NT):
                last = nc.vector.bn_stats(stats[:, t, :], y[:, t, :])
            last.then_inc(stats_ready.sem, 1)

        def settle(graph):
            nc.vector.wait_ge(stats_ready.sem, stats_ready.at(graph))
            nc.vector.tensor_copy(settled[:, :], minus_one[:, :])

        def normalise_moments(graph):
            for t in range(NT):
                last = nc.vector.bn_aggr(mean_var[:, t, :], stats[:, t, :])
            last.then_inc(mv_ready.sem, 1)

        def normalise_factors(graph, eps):
            nc.gpsimd.wait_ge(mv_ready.sem, mv_ready.at(graph))
            nc.gpsimd.tensor_tensor(var_eps[:, :], mean_var[:, :, 1], eps, ALU.add).then_inc(veps_ready.sem, 1)
            nc.gpsimd.wait_ge(veps_ready.sem, veps_ready.at(graph))
            nc.gpsimd.tensor_tensor(rstd[:, :], var_eps[:, :], minus_half[:, :], ALU.pow)\
                .then_inc(rstd_ready.sem, 1)
            nc.gpsimd.wait_ge(rstd_ready.sem, rstd_ready.at(graph))
            nc.gpsimd.tensor_tensor(mean_rstd[:, :], mean_var[:, :, 0], rstd[:, :], ALU.mult)\
                .then_inc(mr_ready.sem, 1)
            nc.gpsimd.wait_ge(mr_ready.sem, mr_ready.at(graph))
            nc.gpsimd.tensor_tensor(shift[:, :], mean_rstd[:, :], minus_one[:, :], ALU.mult)\
                .then_inc(shift_ready.sem, 1)

        def normalise_apply(graph):
            nc.scalar.wait_ge(shift_ready.sem, shift_ready.at(graph))
            nc.scalar.wait_ge(saved.of(Graph(graph.half - 1, graph.p)), saved.at(Graph(graph.half - 1, graph.p)))
            for t in range(NT):
                nc.scalar.activation(x_out[:, graph.p, t, :], y[:, t, :], ACT.Identity, bias=shift[:, t:t + 1],
                                     scale=rstd[:, t:t + 1]).then_inc(normed.sem, 1)

        def load_x(sp, layer, graph):
            sp.wait_ge(xt_ready.sem, xt_ready.at(Graph(graph.half - 1, graph.p)))
            src = x_dram[graph.s] if layer == 0 else x_all[:, graph.s]
            sp.dma_start(x_in[:, graph.p], src).then_inc(x_loaded.of(graph), 16)

        def load_res(sp, layer, graph):
            sp.wait_ge(y_ready.sem, y_ready.at(Graph(graph.half - 1, graph.p)))
            src = x_dram[graph.s] if layer == 0 else x_all[:, graph.s]
            sp.dma_start(x_res[:, graph.p], src).then_inc(res_loaded.of(graph), 16)

        def store(sp, layer, graph):
            sp.wait_ge(normed.sem, normed.at(graph))
            dst = out_dram[graph.s] if layer == 3 else x_all[:, graph.s]
            sp.dma_start(dst, x_out[:, graph.p]).then_inc(saved.of(graph), 16)

        def sync_program(sp, layer):
            def first(g):
                load_x(sp, layer, g)
                load_x(sp, layer, g.next())
                load_x(sp, layer, g.next().next())
                load_res(sp, layer, g)

            def step(g):
                load_x(sp, layer, g.next().next())
                load_res(sp, layer, g)
                store(sp, layer, g.prev())

            first(Graph(0, 0))
            step(Graph(0, 1))
            step(Graph(1, 0))
            with sp.Fori(1, (B - 4) // 2) as i:
                step(Graph(i, 1))
                step(Graph(i + 1, 0))
            g = Graph((B - 4) // 2, 1)
            step(g)
            g = g.next()
            load_res(sp, layer, g)
            store(sp, layer, g.prev())
            g = g.next()
            load_res(sp, layer, g)
            store(sp, layer, g.prev())
            store(sp, layer, g)
            sp.wait_ge(saved.of(g.prev()), saved.at(g.prev()))
            sp.wait_ge(saved.of(g), saved.at(g))

        def prepare(block, mats, rows, extra_loads, extra_ops):
            @block.sync
            def _(sp):
                w0 = count["w"]
                for i, m in enumerate(mats):
                    if w0 + i >= 2:
                        sp.wait_ge(w_lo_ready, w0 + i - 1)
                    sp.dma_start(w_stage[:, (w0 + i) % 2], m).then_inc(w_loaded[(w0 + i) % 2], 16)
                for i, r in enumerate(rows):
                    for q in range(2):
                        sp.dma_start(row_in[q:q + 1, i, :].rearrange("o (h e) -> o h e", e=r.shape[-1]), r)\
                            .then_inc(small_loaded, 16)
                for dst, src in extra_loads:
                    sp.dma_start(dst, src).then_inc(small_loaded, 16)

            n_small = 16 * (2 * len(rows) + len(extra_loads))

            @block.scalar
            def _(act):
                for i in range(len(mats)):
                    n = count["w"] + i
                    act.wait_ge(w_loaded[n % 2], 16 * (n // 2 + 1))
                    nc.scalar.activation(w_hi[:, i], w_stage[:, n % 2], ACT.Copy, scale=WSCALE)\
                        .then_inc(w_hi_ready, 1)

            @block.vector
            def _(dve):
                def chain(ins):
                    count["prep"] += 1
                    ins.then_inc(prep_step, 1)
                    dve.wait_ge(prep_step, count["prep"])

                for i in range(len(mats)):
                    n = count["w"] + i
                    dve.wait_ge(w_hi_ready, n + 1)
                    nc.vector.scalar_tensor_tensor(w_lo[:, i], w_stage[:, n % 2], WSCALE, w_hi[:, i],
                                                   op0=ALU.mult, op1=ALU.subtract).then_inc(w_lo_ready, 1)
                dve.wait_ge(small_loaded, count["small"] + n_small)
                chain(nc.vector.tensor_scalar(row_64[:, :, :], row_in[:, :, :], WSCALE, None, ALU.mult))
                chain(nc.vector.tensor_copy(row_hi[:, :, :], row_64[:, :, :]))
                chain(nc.vector.tensor_scalar(row_lo[:, :, :], row_64[:, :, :], row_pq[:, 0:1], None, ALU.mult))
                chain(nc.vector.scalar_tensor_tensor(bias_row[:, :, :], row_hi[:, :, :], row_pq[:, 1:2],
                                                     row_lo[:, :, :], op0=ALU.mult, op1=ALU.add))
                extra_ops(dve, chain)
                dve.wait_ge(w_lo_ready, count["w"] + len(mats))
            count["w"] += len(mats)
            count["small"] += n_small

        w_att = buf_a[:, :].rearrange("p (i t n) -> p i t n", i=NW, t=NT)
        vals = buf_b[:, :].rearrange("p (q t h e) -> p q t h e", q=2, t=NT, h=HEADS)
        gate4 = buf_c[:, :].rearrange("p (q t c) -> p q t c", q=2, t=NT)
        z = buf_d[:, 0:NT * C].rearrange("p (t h e) -> p t h e", t=NT, h=HEADS)
        z_flat = buf_d[:, 0:NT * C].rearrange("p (t c) -> p t c", t=NT)
        z_exp = buf_d[:, NT * C:2 * NT * C].rearrange("p (t c) -> p t c", t=NT)
        th = buf_e[:, :].rearrange("p (t c) -> p t c", t=NT)
        thT = buf_f[:, :].rearrange("p (k n) -> p k n", k=KC)
        h_sb = sb("h_sb", [P, NT, HEADS, E])
        z_neg = buf_g[:, :].rearrange("p (t c) -> p t c", t=NT)
        w_flat = w_stage[:, :, :, :].rearrange("p i k c -> p (i k c)")
        delta = w_flat[:, 0:NT * C].rearrange("p (t c) -> p t c", t=NT)
        sd_ps = t_flat[:, 0:NT * 2 * HEADS].rearrange("p (t c) -> p t c", t=NT)
        sT_ps = t_flat[0:HEADS, N:2 * N]
        dT_ps = t_flat[0:HEADS, 2 * N:3 * N]
        dmax_ps = t_flat[:, 0:HEADS]

        h_ready = Signal(sem("h_ready"), NT)
        th_ready = Signal(sem("th_ready"))
        tht_ready = Signal(sem("tht_ready"))
        hb_ready = Signal(sem("hb_ready"))
        tht_sb_ready = Signal(sem("tht_sb_ready"))
        sd_ps_ready = Signal(sem("sd_ps_ready"))
        sd_ready = Signal(sem("sd_ready"))
        sdt_ready = Signal(sem("sdt_ready"))
        dmax_ready = Signal(sem("dmax_ready"))
        spos_ready = Signal(sem("spos_ready"))
        diag_ready = Signal(sem("diag_ready"))
        dmax_ps_ready = Signal(sem("dmax_ps_ready"))
        b_ready = Signal(sem("b_ready"))
        b_hi_ready = Signal(sem("b_hi_ready"))
        b_rest_ready = Signal(sem("b_rest_ready"))
        b_mid_ready = Signal(sem("b_mid_ready"))
        parts_ready = Signal(sem("parts_ready"))
        drel_ready = Signal(sem("drel_ready"))
        gd_ready = Signal(sem("gd_ready"))
        h_sb_ready = Signal(sem("h_sb_ready"))
        d64_ready = Signal(sem("d64_ready"))
        vals_ready = Signal(sem("vals_ready"))
        gate_ps_ready = Signal(sem("gate_ps_ready"), NT)
        gate_t_ready = Signal(sem("gate_t_ready"))
        gate_ready = Signal(sem("gate_ready"))
        bcast_ready = Signal(sem("bcast_ready"), PAIRS)
        w_ready = Signal(sem("w_ready"), HEADS)
        summed = Signal(sem("summed"), HEADS)
        rden_ready = Signal(sem("rden_ready"))
        z_ready = Signal(sem("z_ready"))
        zexp_ready = Signal(sem("zexp_ready"))
        zpos_ready = Signal(sem("zpos_ready"))
        zneg_ready = Signal(sem("zneg_ready"))
        elu_ready = Signal(sem("elu_ready"))
        delta_ready = Signal(sem("delta_ready"))
        gated_ready = Signal(sem("gated_ready"))
        gat_signals = [h_ready, th_ready, tht_ready, hb_ready, tht_sb_ready, sd_ps_ready, sd_ready, sdt_ready,
                       dmax_ready, spos_ready, diag_ready, dmax_ps_ready, b_ready, b_hi_ready, b_rest_ready,
                       b_mid_ready, parts_ready, drel_ready, gd_ready, h_sb_ready, d64_ready, vals_ready, gate_ps_ready, gate_t_ready,
                       gate_ready, bcast_ready, w_ready, summed, rden_ready, z_ready, zexp_ready, zpos_ready, zneg_ready,
                       elu_ready, delta_ready, gated_ready]

        def gat_layer(block, layer):
            def load_mask(act, graph):
                act.wait_ge(w_ready.sem, w_ready.at(Graph(graph.half - 1, graph.p)))
                act.dma_start(mask[:, graph.p], adjT_dram[graph.s]).then_inc(mask_loaded.of(graph), 16)

            @block.sync
            def _(sp):
                sync_program(sp, layer)

            @block.tensor
            def _(pe):
                def transpose_x(g):
                    pe.wait_ge(x_loaded.of(g), x_loaded.at(g))
                    pe.wait_ge(drel_ready.sem, drel_ready.at(g.prev()))
                    transpose_tiles(x_in[:, g.p]).then_inc(xt_ready.sem, 1)

                def values(g, t):
                    if t == 0:
                        pe.wait_ge(lo_ready.sem, lo_ready.at(g))
                        pe.wait_ge(gate_t_ready.sem, gate_t_ready.at(g.prev()))
                    project(0, x_hi[:, g.p], x_lo[:, g.p], t).then_inc(h_ready.sem, 1)

                def transpose_th(g):
                    pe.wait_ge(th_ready.sem, th_ready.at(g))
                    transpose_tiles(th).then_inc(tht_ready.sem, 1)
                    for t in range(NT):
                        last = add_bias(ps_h[:, t, 0:C], 0, skip_group_check=True)
                    last.then_inc(hb_ready.sem, 1)

                def scores(g):
                    pe.wait_ge(tht_sb_ready.sem, tht_sb_ready.at(g))
                    for t in range(NT):
                        for k in range(KC):
                            last = nc.tensor.matmul(sd_ps[:, t, :], thT[:, k, t * P:(t + 1) * P],
                                                    score_mat[:, k, :], start=(k == 0), stop=(k == KC - 1))
                    last.then_inc(sd_ps_ready.sem, 1)

                def transpose_scores(g):
                    pe.wait_ge(sd_ready.sem, sd_ready.at(g))
                    for dst, c in ((sT_ps, 0), (dT_ps, HEADS)):
                        for t in range(NT):
                            last = nc.tensor.transpose(dst[:, t * P:(t + 1) * P], sd[:, t, c:c + HEADS], ident[:, :])
                    last.then_inc(sdt_ready.sem, 1)

                def broadcast_dmax(g):
                    pe.wait_ge(diag_ready.sem, diag_ready.at(g))
                    nc.tensor.matmul(dmax_ps, ones12[:, :], d_max_diag[:, :], start=True, stop=True)\
                        .then_inc(dmax_ps_ready.sem, 1)

                def gate(g, t):
                    if t == 0:
                        pe.wait_ge(h_sb_ready.sem, h_sb_ready.at(g))
                    project(1, x_hi[:, g.p], x_lo[:, g.p], t, bias=1).then_inc(gate_ps_ready.sem, 1)

                def broadcast_b(g, j):
                    if j == 0:
                        pe.wait_ge(parts_ready.sem, parts_ready.at(g))
                    pe.wait_ge(w_ready.sem, w_ready.at(g, 2 * (j - 1)))
                    for h in range(2):
                        last = nc.tensor.matmul(ps_b[:, j % 2, h * N:(h + 1) * N], pick_head[:, 2 * j + h, :],
                                                b_parts[:, g.p, :], start=True, stop=True)
                    last.then_inc(bcast_ready.sem, 1)

                def sum_neighbours(g, j):
                    if j == 0:
                        pe.wait_ge(vals_ready.sem, vals_ready.at(g))
                        pe.wait_ge(z_ready.sem, z_ready.at(g.prev()))
                    for h in (2 * j, 2 * j + 1):
                        pe.wait_ge(w_ready.sem, w_ready.at(g, h + 1))
                        for t in range(NT):
                            for m in range(NT):
                                last = nc.tensor.matmul(ps_o[:, t, h * EV:(h + 1) * EV],
                                                        w_att[:, h % NW, m, t * P:(t + 1) * P],
                                                        vals[:, g.p, m, h, :], start=(m == 0), stop=(m == NT - 1))
                        last.then_inc(summed.sem, 1)

                def step(g, front=True, after_next=True):
                    n = g.next()
                    for j in range(PAIRS):
                        if front:
                            if j < NT:
                                values(n, j)
                            elif j == 2:
                                transpose_th(n)
                            elif j == 3:
                                scores(n)
                            elif j == 5:
                                broadcast_dmax(n)
                                gate(n, 1)
                                broadcast_b(n, 0)
                                if after_next:
                                    transpose_x(n.next())
                        sum_neighbours(g, j)
                        if j + 2 < PAIRS:
                            broadcast_b(g, j + 2)
                        if front:
                            if j == 3:
                                transpose_scores(n)
                                gate(n, 0)
                            elif j == 5:
                                broadcast_b(n, 1)

                def first(g):
                    pe.wait_ge(prepared, count["prepared"])
                    transpose_x(g)
                    values(g, 0)
                    values(g, 1)
                    transpose_th(g)
                    scores(g)
                    gate(g, 0)
                    gate(g, 1)
                    transpose_scores(g)
                    broadcast_dmax(g)
                    transpose_x(g.next())
                    broadcast_b(g, 0)
                    broadcast_b(g, 1)
                    step(g)

                def last(g):
                    step(g.prev(), after_next=False)
                    step(g, front=False)

                pipeline(pe, first, step, last)

            @block.scalar
            def _(act):
                def split_hi(g):
                    act.wait_ge(xt_ready.sem, xt_ready.at(g))
                    nc.scalar.activation(x_hi[:, g.p], tr_ps, ACT.Copy).then_inc(hi_ready.sem, 1)

                def tanh_h(g):
                    act.wait_ge(h_ready.sem, h_ready.at(g))
                    nc.scalar.activation(th, ps_h[:, :, 0:C], ACT.Tanh, scale=1.0 / WSCALE).then_inc(th_ready.sem, 1)

                def keep_thT(g):
                    act.wait_ge(tht_ready.sem, tht_ready.at(g))
                    nc.scalar.activation(thT, tr_ps, ACT.Copy).then_inc(tht_sb_ready.sem, 1)

                def keep_h(g):
                    act.wait_ge(hb_ready.sem, hb_ready.at(g))
                    act.wait_ge(vals_ready.sem, vals_ready.at(g.prev()))
                    nc.scalar.activation(h_sb[:, :, :, :].rearrange("p t h e -> p t (h e)"), ps_h[:, :, 0:C], ACT.Copy)\
                        .then_inc(h_sb_ready.sem, 1)

                def exp_b(g):
                    act.wait_ge(spos_ready.sem, spos_ready.at(g))
                    nc.scalar.activation(b_exp[:, :], s_pos[:, :], ACT.Exp, scale=-0.8).then_inc(b_ready.sem, 1)

                def exp_gd(g):
                    act.wait_ge(drel_ready.sem, drel_ready.at(g))
                    nc.scalar.activation(G[:, g.p], d_rel[:, :, :], ACT.Exp, scale=0.8)
                    nc.scalar.activation(D[:, :, :], d_rel[:, :, :], ACT.Exp, scale=0.2).then_inc(gd_ready.sem, 1)

                def gate_tanh(g):
                    act.wait_ge(gate_ps_ready.sem, gate_ps_ready.at(g))
                    nc.scalar.activation(gate4[:, g.p], ps_h[:, :, 0:C], ACT.Tanh, scale=0.5 / WSCALE)\
                        .then_inc(gate_t_ready.sem, 1)

                def gate_scale(g):
                    act.wait_ge(gate_t_ready.sem, gate_t_ready.at(g))
                    nc.scalar.activation(gate4[:, g.p], gate4[:, g.p], ACT.Copy, scale=0.25, bias=0.25)\
                        .then_inc(gate_ready.sem, 1)

                def exp_z(g):
                    act.wait_ge(z_ready.sem, z_ready.at(g))
                    nc.scalar.activation(z_exp, z_flat, ACT.Exp).then_inc(zexp_ready.sem, 1)
                    act.wait_ge(zexp_ready.sem, zexp_ready.at(g))
                    nc.scalar.activation(z_flat, z_flat, ACT.Relu).then_inc(zpos_ready.sem, 1)

                def front_half(g):
                    tanh_h(g)
                    keep_thT(g)
                    keep_h(g)

                def front_end(g, after_next=True):
                    exp_b(g)
                    exp_gd(g)
                    gate_tanh(g)
                    if after_next:
                        split_hi(g.next())
                    gate_scale(g)

                def step(g, front=True, back=True, after_next=True):
                    n, b = g.next(), g.prev()
                    if front:
                        load_mask(act, n)
                    if back:
                        exp_z(b)
                    if front:
                        front_half(n)
                    if back:
                        normalise_apply(b)
                    if front:
                        front_end(n, after_next)

                def first(g):
                    load_mask(act, g)
                    split_hi(g)
                    front_half(g)
                    front_end(g)
                    step(g, back=False)

                def last(g):
                    step(g.prev(), after_next=False)
                    step(g, front=False)
                    exp_z(g)
                    normalise_apply(g)

                pipeline(act, first, step, last)

            @block.vector
            def _(dve):
                def split_lo(g):
                    dve.wait_ge(hi_ready.sem, hi_ready.at(g))
                    nc.vector.tensor_tensor(x_lo[:, g.p], tr_ps, x_hi[:, g.p], ALU.subtract)\
                        .then_inc(lo_ready.sem, 1)

                def keep_scores(g):
                    dve.wait_ge(sd_ps_ready.sem, sd_ps_ready.at(g))
                    nc.vector.tensor_copy(sd[:, :, :], sd_ps).then_inc(sd_ready.sem, 1)

                def max_scores(g):
                    dve.wait_ge(sdt_ready.sem, sdt_ready.at(g))
                    nc.vector.tensor_reduce(d_max[:, :], dT_ps, AX.X, ALU.max).then_inc(dmax_ready.sem, 1)
                    dve.wait_ge(dmax_ready.sem, dmax_ready.at(g))
                    nc.vector.tensor_scalar(s_pos[:, :], sT_ps, d_max[:, 0:1], 0.0, ALU.add, ALU.max)\
                        .then_inc(spos_ready.sem, 1)
                    nc.vector.tensor_scalar(d_max_diag[:, :], ident[0:HEADS, 0:HEADS], d_max[:, 0:1], None, ALU.mult)\
                        .then_inc(diag_ready.sem, 1)

                def split_b(g):
                    part = lambda q: b_parts[32 * q:32 * q + HEADS, g.p, :]
                    dve.wait_ge(b_ready.sem, b_ready.at(g))
                    nc.vector.tensor_copy(part(0), b_exp[:, :]).then_inc(b_hi_ready.sem, 1)
                    dve.wait_ge(b_hi_ready.sem, b_hi_ready.at(g))
                    nc.vector.tensor_tensor(b_rest[:, :], b_exp[:, :], part(0), ALU.subtract)\
                        .then_inc(b_rest_ready.sem, 1)
                    dve.wait_ge(b_rest_ready.sem, b_rest_ready.at(g))
                    nc.vector.tensor_copy(b_mid[:, :], b_rest[:, :]).then_inc(b_mid_ready.sem, 1)
                    nc.vector.tensor_copy(part(1), b_rest[:, :])
                    dve.wait_ge(b_mid_ready.sem, b_mid_ready.at(g))
                    nc.vector.tensor_tensor(part(2), b_rest[:, :], b_mid[:, :], ALU.subtract)\
                        .then_inc(parts_ready.sem, 1)

                def relative_scores(g):
                    dve.wait_ge(dmax_ps_ready.sem, dmax_ps_ready.at(g))
                    m = dmax_ps.rearrange("p (o h) -> p o h", o=1).to_broadcast([P, NT, HEADS])
                    nc.vector.tensor_tensor(d_rel[:, :, :], sd[:, :, HEADS:2 * HEADS], m, ALU.subtract)\
                        .then_inc(drel_ready.sem, 1)

                def weights(g, j):
                    if j == 0:
                        dve.wait_ge(mask_loaded.of(g), mask_loaded.at(g))
                        dve.wait_ge(gd_ready.sem, gd_ready.at(g))
                    dve.wait_ge(bcast_ready.sem, bcast_ready.at(g, j + 1))
                    for i in range(2):
                        h = 2 * j + i
                        dve.wait_ge(summed.sem, summed.at(g, h - NW + 1))
                        for m in range(NT):
                            last = nc.vector.scalar_tensor_tensor(
                                w_att[:, h % NW, m, :], ps_b[:, j % 2, i * N:(i + 1) * N], G[:, g.p, m, h:h + 1],
                                mask[:, g.p, m, :], op0=ALU.max, op1=ALU.mult)
                        last.then_inc(w_ready.sem, 1)

                def divide(g):
                    dve.wait_ge(summed.sem, summed.at(g))
                    o = ps_o[:, :, 0:HEADS * EV].rearrange("p t (h e) -> p t h e", e=EV)
                    r = rden[:, :, :].rearrange("p t (h o) -> p t h o", o=1)
                    nc.vector.reciprocal(r, o[:, :, :, E:EV]).then_inc(rden_ready.sem, 1)
                    dve.wait_ge(rden_ready.sem, rden_ready.at(g))
                    nc.vector.tensor_tensor(z, o[:, :, :, 0:E], r.to_broadcast([P, NT, HEADS, E]), ALU.mult)\
                        .then_inc(z_ready.sem, 1)

                def negative_part(g):
                    dve.wait_ge(zexp_ready.sem, zexp_ready.at(g))
                    nc.vector.tensor_scalar(z_neg, z_exp, 1.0, -1.0, ALU.min, ALU.add).then_inc(zneg_ready.sem, 1)

                def front_end(g, after_next=True):
                    max_scores(g)
                    split_b(g)
                    relative_scores(g)
                    weights(g, 0)
                    if after_next:
                        split_lo(g.next())

                def step(g, front=True, back=True, after_next=True):
                    n, b = g.next(), g.prev()
                    if back:
                        divide(b)
                    weights(g, 1)
                    if back:
                        negative_part(b)
                    for j in range(2, 5):
                        weights(g, j)
                    if front:
                        keep_scores(n)
                    if back:
                        normalise_stats(b)
                        settle(b)
                        normalise_moments(b)
                    weights(g, 5)
                    if front:
                        front_end(n, after_next)

                def first(g):
                    split_lo(g)
                    keep_scores(g)
                    front_end(g)
                    step(g, back=False)

                def last(g):
                    step(g.prev(), after_next=False)
                    step(g, front=False)
                    divide(g)
                    negative_part(g)
                    normalise_stats(g)
                    settle(g)
                    normalise_moments(g)

                pipeline(dve, first, step, last)

            @block.gpsimd
            def _(pool):
                def back(g):
                    pool.wait_ge(zpos_ready.sem, zpos_ready.at(g))
                    pool.wait_ge(zneg_ready.sem, zneg_ready.at(g))
                    pool.wait_ge(normed.sem, normed.at(g.prev()))
                    nc.gpsimd.tensor_tensor(z_exp, z_flat, z_neg, ALU.add).then_inc(elu_ready.sem, 1)
                    pool.wait_ge(res_loaded.of(g), res_loaded.at(g))
                    pool.wait_ge(elu_ready.sem, elu_ready.at(g))
                    nc.gpsimd.tensor_tensor(delta, z_exp, x_res[:, g.p], ALU.subtract)\
                        .then_inc(delta_ready.sem, 1)
                    pool.wait_ge(gate_ready.sem, gate_ready.at(g))
                    pool.wait_ge(delta_ready.sem, delta_ready.at(g))
                    nc.gpsimd.tensor_tensor(z_neg, delta, gate4[:, g.p], ALU.mult)\
                        .then_inc(gated_ready.sem, 1)
                    pool.wait_ge(gated_ready.sem, gated_ready.at(g))
                    nc.gpsimd.tensor_tensor(y[:, :, :], z_neg, x_res[:, g.p], ALU.add).then_inc(y_ready.sem, 1)
                    normalise_factors(g, eps_half[:, :])

                def scale_values(g):
                    pool.wait_ge(gd_ready.sem, gd_ready.at(g))
                    d = D[:, :, :].rearrange("p t (h o) -> p t h o", o=1)
                    nc.gpsimd.tensor_tensor(vals[:, g.p, :, :, E:EV], d, wscale[:, :, :, :], ALU.mult)\
                        .then_inc(d64_ready.sem, 1)
                    pool.wait_ge(h_sb_ready.sem, h_sb_ready.at(g))
                    nc.gpsimd.tensor_tensor(vals[:, g.p, :, :, 0:E], h_sb[:, :, :, :],
                                            d.to_broadcast([P, NT, HEADS, E]), ALU.mult).then_inc(vals_ready.sem, 1)

                def step(g):
                    back(g.prev())
                    scale_values(g.next())

                def first(g):
                    scale_values(g)
                    scale_values(g.next())

                def last(g):
                    step(g.prev())
                    back(g.prev())
                    back(g)

                pipeline(pool, first, step, last)

        probs = buf_a[:, 0:2 * NT * N].rearrange("p (i t k) -> p i t k", i=2, t=NT)
        probsT = buf_a[:, 2 * NT * N:4 * NT * N].rearrange("p (i t q) -> p i t q", i=2, t=NT)
        v_sb = buf_b[:, 0:2 * NT * MH * DV].rearrange("p (q t h e) -> p q t h e", q=2, t=NT, h=MH)
        qT = buf_c[:, :].rearrange("p (q k n) -> p q k n", q=2, k=KC)
        kT = buf_d[:, :].rearrange("p (q k n) -> p q k n", q=2, k=KC)
        att = buf_e[:, :].rearrange("p (t h e) -> p t h e", t=NT, h=MH)
        att_flat = buf_e[:, :].rearrange("p (t c) -> p t c", t=NT)
        att_parts = w_flat[:, 0:KC * N].bitcast(f16).rearrange("p (i k n) -> p i k n", i=2, k=KC)
        att_hi, att_lo = att_parts[:, 0], att_parts[:, 1]
        neg_mask = buf_f[:, 0:NT * N].bitcast(bf16).rearrange("p (q t k) -> p q t k", q=2, t=NT)
        qk_ps = ps_h[:, :, :].rearrange("p t c -> p (t c)")[:, 0:KC * N].rearrange("p (k n) -> p k n", k=KC)

        negm_ready = Signal(sem("negm_ready"))
        q_ps_ready = Signal(sem("q_ps_ready"))
        q_ready = Signal(sem("q_ready"))
        k_ps_ready = Signal(sem("k_ps_ready"))
        k_ready = Signal(sem("k_ready"))
        v_ps_ready = Signal(sem("v_ps_ready"))
        v_ready = Signal(sem("v_ready"))
        s_ready = Signal(sem("s_ready"), MH)
        max_ready = Signal(sem("max_ready"), MH)
        p_ready = Signal(sem("p_ready"), MH)
        pt_ps_ready = Signal(sem("pt_ps_ready"), MH)
        pt_dve = Signal(sem("pt_dve"), MH // 2)
        pt_act = Signal(sem("pt_act"), MH // 2)
        att_ps_ready = Signal(sem("att_ps_ready"), MH)
        mden_ready = Signal(sem("mden_ready"))
        att_ready = Signal(sem("att_ready"))
        attT_ready = Signal(sem("attT_ready"))
        atthi_ready = Signal(sem("atthi_ready"))
        attlo_ready = Signal(sem("attlo_ready"))
        out_ready = Signal(sem("out_ready"), NT)

        def attention_layer(block, layer):
            def load_mask(act, graph):
                act.wait_ge(negm_ready.sem, negm_ready.at(Graph(graph.half - 1, graph.p)))
                act.dma_start(mask[:, graph.p], adj_dram[graph.s]).then_inc(mask_loaded.of(graph), 16)

            @block.sync
            def _(sp):
                sync_program(sp, layer)

            def wait_probsT(eng, g, h):
                half = pt_dve if h % 2 == 0 else pt_act
                eng.wait_ge(half.sem, half.at(g, h // 2 + 1))

            @block.tensor
            def _(pe):
                def transpose_x(g):
                    pe.wait_ge(x_loaded.of(g), x_loaded.at(g))
                    pe.wait_ge(attlo_ready.sem, attlo_ready.at(g.prev().prev().prev()))
                    transpose_tiles(x_in[:, g.p]).then_inc(xt_ready.sem, 1)

                def project_T(g, which, chunks):
                    for e in chunks:
                        for k in range(KC):
                            for n, (w, x) in enumerate(((w_hi, x_hi), (w_hi, x_lo), (w_lo, x_hi))):
                                last = nc.tensor.matmul(qk_ps[:, e, :], w[:, which, k, e * P:(e + 1) * P], x[:, g.p, k, :],
                                                        start=(k == 0 and n == 0), stop=(k == KC - 1 and n == 2))
                    return last

                def project_q(g):
                    pe.wait_ge(lo_ready.sem, lo_ready.at(g))
                    pe.wait_ge(y_ready.sem, y_ready.at(Graph(g.half - 1, g.p).prev()))
                    project_T(g, 0, range(KC)).then_inc(q_ps_ready.sem, 1)

                def project_k(g, chunks):
                    if 0 in chunks:
                        pe.wait_ge(q_ready.sem, q_ready.at(g))
                    last = project_T(g, 1, chunks)
                    if KC - 1 in chunks:
                        last.then_inc(k_ps_ready.sem, 1)

                def project_v(g):
                    pe.wait_ge(k_ready.sem, k_ready.at(g))
                    project(2, x_hi[:, g.p], x_lo[:, g.p], bias=0).then_inc(v_ps_ready.sem, 1)

                def score(g, h):
                    if h == 0:
                        pe.wait_ge(k_ready.sem, k_ready.at(g))
                        pe.wait_ge(negm_ready.sem, negm_ready.at(g))
                    if h >= 2:
                        wait_probsT(pe, g, h - 2)
                    else:
                        wait_probsT(pe, g.prev(), MH + h - 2)
                    r = (h % 2) * DH
                    for t in range(NT):
                        dst = ps_b[:, h % 2, t * N:(t + 1) * N]
                        nc.tensor.matmul(dst, qT[r:r + DH, g.p, h // 2, t * P:(t + 1) * P],
                                         kT[r:r + DH, g.p, h // 2, :], start=True, stop=False)
                        last = nc.tensor.matmul(dst, ident_bf[:, :], neg_mask[:, g.p, t, :], start=False, stop=True)
                    last.then_inc(s_ready.sem, 1)

                def transpose_probs(g, h):
                    pe.wait_ge(p_ready.sem, p_ready.at(g, h + 1))
                    for t in range(NT):
                        for k in range(NT):
                            last = nc.tensor.transpose(ps_b[:, h % 2, k * N + t * P:k * N + (t + 1) * P],
                                                       probs[:, h % 2, t, k * P:(k + 1) * P], ident[:, :])
                    last.then_inc(pt_ps_ready.sem, 1)

                def attend(g, h):
                    wait_probsT(pe, g, h)
                    if h == 0:
                        pe.wait_ge(v_ready.sem, v_ready.at(g))
                        pe.wait_ge(att_ready.sem, att_ready.at(g.prev()))
                    for t in range(NT):
                        for k in range(NT):
                            last = nc.tensor.matmul(ps_o[:, t, h * DV:(h + 1) * DV],
                                                    probsT[:, h % 2, k, t * P:(t + 1) * P], v_sb[:, g.p, k, h, :],
                                                    start=(k == 0), stop=(k == NT - 1))
                    last.then_inc(att_ps_ready.sem, 1)

                def transpose_att(g):
                    pe.wait_ge(att_ready.sem, att_ready.at(g))
                    transpose_tiles(att_flat).then_inc(attT_ready.sem, 1)

                def project_out(g, t):
                    if t == 0:
                        pe.wait_ge(attlo_ready.sem, attlo_ready.at(g))
                    project(3, att_hi, att_lo, t, bias=1).then_inc(out_ready.sem, 1)

                def step(g, front=True, back=True, after_next=True):
                    n, b = g.next(), g.prev()
                    for h in range(MH):
                        transpose_probs(g, h)
                        if h == 0 and front:
                            project_q(n)
                        if h == 1 and back:
                            transpose_att(b)
                        if h == 1 and front:
                            project_k(n, (0,))
                        if h == 2 and front:
                            project_k(n, (1, 2))
                        if h == 3 and front:
                            project_v(n)
                        if h == 4 and after_next:
                            transpose_x(n.next())
                        if h == 4 and front:
                            pe.wait_ge(v_ready.sem, v_ready.at(n))
                        if h in (4, 5) and back:
                            project_out(b, h - 4)
                        attend(g, h)
                        if h + 2 < MH:
                            score(g, h + 2)
                        elif front:
                            score(n, h + 2 - MH)

                def first(g):
                    pe.wait_ge(prepared, count["prepared"])
                    transpose_x(g)
                    project_q(g)
                    project_k(g, range(KC))
                    project_v(g)
                    transpose_x(g.next())
                    score(g, 0)
                    score(g, 1)
                    step(g, back=False)

                def last(g):
                    step(g.prev(), after_next=False)
                    step(g, front=False, after_next=False)
                    transpose_att(g)
                    project_out(g, 0)
                    project_out(g, 1)

                pipeline(pe, first, step, last)

            @block.scalar
            def _(act):
                def split_hi(g):
                    act.wait_ge(xt_ready.sem, xt_ready.at(g))
                    act.wait_ge(v_ps_ready.sem, v_ps_ready.at(g.prev()))
                    nc.scalar.activation(x_hi[:, g.p], tr_ps, ACT.Copy).then_inc(hi_ready.sem, 1)

                def keep_q(g):
                    act.wait_ge(q_ps_ready.sem, q_ps_ready.at(g))
                    for e in range(KC):
                        last = nc.scalar.activation(qT[:, g.p, e, :], qk_ps[:, e, :], ACT.Identity,
                                                    bias=bias_col[:, 0, e:e + 1], scale=1.0 / (WSCALE * DH ** 0.5))
                    last.then_inc(q_ready.sem, 1)

                def keep_v(g):
                    act.wait_ge(v_ps_ready.sem, v_ps_ready.at(g))
                    src = ps_h[:, :, 0:C].rearrange("p t (h e) -> p t h e", e=DH)
                    nc.scalar.activation(v_sb[:, g.p, :, :, 0:DH], src, ACT.Copy, scale=1.0 / WSCALE)\
                        .then_inc(v_ready.sem, 1)

                def exp_scores(g, h):
                    act.wait_ge(max_ready.sem, max_ready.at(g, h + 1))
                    act.wait_ge(pt_ps_ready.sem, pt_ps_ready.at(g, h - 1))
                    for t in range(NT):
                        last = nc.scalar.activation(probs[:, h % 2, t, :], ps_b[:, h % 2, t * N:(t + 1) * N],
                                                    ACT.Exp, bias=row_max[:, h % 2, t:t + 1])
                    last.then_inc(p_ready.sem, 1)

                def keep_probsT(g, h):
                    act.wait_ge(pt_ps_ready.sem, pt_ps_ready.at(g, h + 1))
                    act.wait_ge(att_ps_ready.sem, att_ps_ready.at(g, h - 1))
                    nc.scalar.activation(probsT[:, h % 2].rearrange("p t q -> p (t q)"), ps_b[:, h % 2, :],
                                         ACT.Copy).then_inc(pt_act.sem, 1)

                def att_split_hi(g):
                    act.wait_ge(attT_ready.sem, attT_ready.at(g))
                    act.wait_ge(out_ready.sem, out_ready.at(g.prev()))
                    nc.scalar.activation(att_hi[:, :, :], tr_ps, ACT.Copy).then_inc(atthi_ready.sem, 1)

                def step(g, front=True, back=True, after_next=True):
                    n, b = g.next(), g.prev()
                    if front:
                        load_mask(act, n)
                        keep_q(n)
                    exp_scores(g, 2)
                    keep_probsT(g, 1)
                    if back:
                        att_split_hi(b)
                    exp_scores(g, 3)
                    exp_scores(g, 4)
                    keep_probsT(g, 3)
                    if front:
                        keep_v(n)
                    exp_scores(g, 5)
                    if after_next:
                        split_hi(n.next())
                    if front:
                        exp_scores(n, 0)
                    keep_probsT(g, 5)
                    if front:
                        exp_scores(n, 1)
                    if back:
                        normalise_apply(b)

                def first(g):
                    load_mask(act, g)
                    split_hi(g)
                    keep_q(g)
                    keep_v(g)
                    split_hi(g.next())
                    exp_scores(g, 0)
                    exp_scores(g, 1)
                    step(g, back=False)

                def last(g):
                    step(g.prev(), after_next=False)
                    step(g, front=False, after_next=False)
                    att_split_hi(g)
                    normalise_apply(g)

                pipeline(act, first, step, last)

            @block.vector
            def _(dve):
                def split_lo(g):
                    dve.wait_ge(hi_ready.sem, hi_ready.at(g))
                    nc.vector.tensor_tensor(x_lo[:, g.p], tr_ps, x_hi[:, g.p], ALU.subtract)\
                        .then_inc(lo_ready.sem, 1)

                def negate_mask(g):
                    dve.wait_ge(mask_loaded.of(g), mask_loaded.at(g))
                    dve.wait_ge(s_ready.sem, s_ready.at(Graph(g.half - 1, g.p)))
                    nc.vector.tensor_scalar(neg_mask[:, g.p], mask[:, g.p], -1.0, NEG, ALU.add, ALU.mult)\
                        .then_inc(negm_ready.sem, 1)

                def keep_k(g):
                    dve.wait_ge(k_ps_ready.sem, k_ps_ready.at(g))
                    for e in range(KC):
                        last = nc.vector.tensor_scalar(kT[:, g.p, e, :], qk_ps[:, e, :], 1.0 / WSCALE,
                                                       bias_col[:, 1, e:e + 1], ALU.mult, ALU.add)
                    last.then_inc(k_ready.sem, 1)

                def max_scores(g, h):
                    dve.wait_ge(s_ready.sem, s_ready.at(g, h + 1))
                    dve.wait_ge(p_ready.sem, p_ready.at(g, h - 1))
                    nc.vector.tensor_reduce(row_max[:, h % 2, :], ps_b[:, h % 2, :].rearrange("p (t k) -> p t k", t=NT),
                                            AX.X, ALU.max, negate=True).then_inc(max_ready.sem, 1)

                def keep_probsT(g, h):
                    dve.wait_ge(pt_ps_ready.sem, pt_ps_ready.at(g, h + 1))
                    dve.wait_ge(att_ps_ready.sem, att_ps_ready.at(g, h - 1))
                    nc.vector.tensor_copy(probsT[:, h % 2].rearrange("p t q -> p (t q)"), ps_b[:, h % 2, :])\
                        .then_inc(pt_dve.sem, 1)

                def divide(g):
                    dve.wait_ge(att_ps_ready.sem, att_ps_ready.at(g))
                    dve.wait_ge(attT_ready.sem, attT_ready.at(g.prev()))
                    o = ps_o[:, :, 0:MH * DV].rearrange("p t (h e) -> p t h e", e=DV)
                    r = rden[:, :, 0:MH].rearrange("p t (h o) -> p t h o", o=1)
                    nc.vector.reciprocal(r, o[:, :, :, DH:DV]).then_inc(mden_ready.sem, 1)
                    dve.wait_ge(mden_ready.sem, mden_ready.at(g))
                    nc.vector.tensor_tensor(att, o[:, :, :, 0:DH], r.to_broadcast([P, NT, MH, DH]), ALU.mult)\
                        .then_inc(att_ready.sem, 1)

                def att_split_lo(g):
                    dve.wait_ge(atthi_ready.sem, atthi_ready.at(g))
                    nc.vector.tensor_tensor(att_lo[:, :, :], tr_ps, att_hi[:, :, :], ALU.subtract)\
                        .then_inc(attlo_ready.sem, 1)

                def add_residual(g):
                    dve.wait_ge(out_ready.sem, out_ready.at(g))
                    dve.wait_ge(res_loaded.of(g), res_loaded.at(g))
                    dve.wait_ge(normed.sem, normed.at(g.prev()))
                    nc.vector.scalar_tensor_tensor(y[:, :, :], ps_h[:, :, 0:C], 1.0 / WSCALE, x_res[:, g.p],
                                                   op0=ALU.mult, op1=ALU.add).then_inc(y_ready.sem, 1)

                def step(g, front=True, back=True, after_next=True):
                    n, b = g.next(), g.prev()
                    if back:
                        divide(b)
                    keep_probsT(g, 0)
                    max_scores(g, 2)
                    if front:
                        negate_mask(n)
                    if back:
                        att_split_lo(b)
                    max_scores(g, 3)
                    keep_probsT(g, 2)
                    if front:
                        keep_k(n)
                    max_scores(g, 4)
                    max_scores(g, 5)
                    keep_probsT(g, 4)
                    if after_next:
                        split_lo(n.next())
                    if front:
                        max_scores(n, 0)
                    if back:
                        add_residual(b)
                        normalise_stats(b)
                    if front:
                        max_scores(n, 1)
                    if back:
                        settle(b)
                        normalise_moments(b)

                def first(g):
                    split_lo(g)
                    keep_k(g)
                    negate_mask(g)
                    split_lo(g.next())
                    max_scores(g, 0)
                    max_scores(g, 1)
                    step(g, back=False)

                def last(g):
                    step(g.prev(), after_next=False)
                    step(g, front=False, after_next=False)
                    divide(g)
                    att_split_lo(g)
                    add_residual(g)
                    normalise_stats(g)
                    settle(g)
                    normalise_moments(g)

                pipeline(dve, first, step, last)

            @block.gpsimd
            def _(pool):
                def step(g, front=True, back=True):
                    if back:
                        normalise_factors(g.prev(), eps_whole[:, :])

                def first(g):
                    pass

                def last(g):
                    step(g.prev())
                    step(g)
                    normalise_factors(g, eps_whole[:, :])

                pipeline(pool, first, step, last)

        def after_layer(signals):
            for sig in signals:
                sig.base += 16 * (B // 2) if isinstance(sig, ParitySignal) else sig.per * B

        def weights_of(name):
            return a[name].rearrange("(k p) c -> p k c", p=P)

        def gat_extra(layer):
            loads = [(w_score[:, 0, :], a[f"L{layer}_gnn_wsrc"]), (w_score[:, 1, :], a[f"L{layer}_gnn_wdst"])]

            def ops(dve, chain):
                for i in range(2):
                    w = w_score[:, i, :].rearrange("p (k o) -> p k o", o=1).to_broadcast([P, KC, HEADS])
                    ins = nc.vector.tensor_tensor(score_mat[:, :, i * HEADS:(i + 1) * HEADS], head_of[:, :, :], w,
                                                  ALU.mult)
                    chain(ins)
            return loads, ops

        for layer in range(4):
            with nc.Block() as block:
                if layer == 0:
                    @block.sync
                    def _(sp):
                        sp.dma_start(ident[:, :], a["c_ident"]).then_inc(small_loaded, 16)
                        sp.dma_start(head_of[:, :, :], a["c_head_of"]).then_inc(small_loaded, 16)
                        sp.dma_start(part_of[:, :], a["c_part_of"]).then_inc(small_loaded, 16)
                        sp.dma_start(row_pq[:, :], a["c_row_pq"]).then_inc(small_loaded, 16)
                        sp.wait_ge(small_loaded, 64)

                    @block.gpsimd
                    def _(pool):
                        nc.gpsimd.memset(ones12[:, :], 1.0)
                        nc.gpsimd.memset(ones_row[:, :], 1.0)
                        nc.gpsimd.memset(minus_half[:, :], -0.5)
                        nc.gpsimd.memset(wscale[:, :, :, :], WSCALE)
                        nc.gpsimd.memset(minus_one[:, :], -1.0)
                        nc.gpsimd.memset(eps_whole[:, :], EPS)
                        nc.gpsimd.memset(eps_half[:, :], EPS / 4)
                        nc.gpsimd.memset(b_parts[:, :, :], 0.0).then_inc(const_ready, 1)
                        pool.wait_ge(const_ready, 1)

                    @block.vector
                    def _(dve):
                        dve.wait_ge(small_loaded, 64)
                        nc.vector.tensor_copy(ident_bf[:, :], ident[:, :])
                        src = part_of[:, :].rearrange("p (h o) -> p h o", o=1).to_broadcast([96, HEADS, P])
                        nc.vector.tensor_copy(pick_head[:, :, :], src).then_inc(pick_ready, 1)
                        dve.wait_ge(pick_ready, 1)
                    count["small"] = 64
                if layer != 1:
                    mats = [weights_of(f"L{layer}_gnn_W"), weights_of(f"L{layer}_gnn_H_w")]
                    rows = [a[f"L{layer}_gnn_b"].rearrange("(o h e) -> o h e", o=1, h=1).to_broadcast([1, HEADS, E]),
                            a[f"L{layer}_gnn_H_b"].rearrange("(o h e) -> o h e", o=1, h=1)]
                    loads, ops = gat_extra(layer)
                else:
                    mats = [weights_of(f"L1_gnn_{w}") for w in ("Wq", "Wk", "Wv", "Wf")]
                    rows = [a[f"L1_gnn_{w}"].rearrange("(o h e) -> o h e", o=1, h=1) for w in ("bv", "bf")]
                    loads = [(bias_col[:, 0, :], a["L1_gnn_bq"]),
                             (bias_col[:, 1, :], a["L1_gnn_bk"])]

                    def ops(dve, chain):
                        chain(nc.vector.tensor_scalar(bias_col[:, 0, :], bias_col[:, 0, :], 1.0 / DH ** 0.5, None,
                                                      ALU.mult))
                        chain(nc.vector.memset(v_sb[:, :, :, :, DH:DV], 1.0))
                prepare(block, mats, rows, loads, ops)
            with nc.Block() as block:
                if layer == 1:
                    attention_layer(block, layer)
                    after_layer(every)
                else:
                    gat_layer(block, layer)
                    after_layer(every + gat_signals)


_WEIGHTS = ["L0_gnn_W", "L0_gnn_b", "L0_gnn_w_src", "L0_gnn_w_dst", "L0_gnn_H_w", "L0_gnn_H_b", "L1_gnn_Wq",
            "L1_gnn_bq", "L1_gnn_Wk", "L1_gnn_bk", "L1_gnn_Wv", "L1_gnn_bv", "L1_gnn_Wf", "L1_gnn_bf", "L2_gnn_W",
            "L2_gnn_b", "L2_gnn_w_src", "L2_gnn_w_dst", "L2_gnn_H_w", "L2_gnn_H_b", "L3_gnn_W", "L3_gnn_b",
            "L3_gnn_w_src", "L3_gnn_w_dst", "L3_gnn_H_w", "L3_gnn_H_b"]


def kernel(**inputs):
    import numpy as np
    import concourse.bacc as bacc
    from concourse import mybir as _mybir
    from concourse.bass_utils import run_bass_kernel_spmd

    arrays = {"x": np.asarray(inputs["x"])}
    adj = np.asarray(inputs["adj"])
    arrays["adj"] = adj
    arrays["adjT"] = adj.transpose(0, 2, 1)
    for name in _WEIGHTS:
        w = np.asarray(inputs[name])
        if name.endswith("gnn_W"):
            w = w.transpose(1, 0, 2).reshape(w.shape[1], -1)
        elif name.endswith("H_w"):
            w = w.T
        elif name.endswith(("w_src", "w_dst")):
            w = w.reshape(-1, 128).T
            name = name.replace("w_", "w")
        elif name.endswith(("bq", "bk")):
            w = w.reshape(-1, 128).T
        arrays[name] = w
    heads, e, chunks = 12, 32, 3
    p = np.arange(128)
    arrays["c_ident"] = np.eye(128, dtype=np.float32)
    arrays["c_head_of"] = np.stack([((k * 128 + p)[:, None] // e == np.arange(heads)[None]) for k in range(chunks)],
                                   axis=1).astype(np.float32)
    arrays["c_part_of"] = (p[:96, None] % 32 == np.arange(heads)[None]).astype(np.float32)
    arrays["c_row_pq"] = np.array([[0.0, 1.0], [1.0, -1.0]], np.float32)

    nc = bacc.Bacc("TRN2", target_bir_lowering=False, num_devices=1)
    args, ins = {}, {}
    for name, v in arrays.items():
        v = np.ascontiguousarray(v)
        ins[f"in_{name}"] = v
        args[name] = nc.dram_tensor(f"in_{name}", v.shape, _mybir.dt.from_np(v.dtype), kind="ExternalInput").ap()
    out = nc.dram_tensor("out_x", arrays["x"].shape, _mybir.dt.float32, kind="ExternalOutput").ap()
    residual_graph_layers(nc, args, out)
    r = run_bass_kernel_spmd(nc, [ins], core_ids=[0])
    return r.results[0]["out_x"]
```

```python
import concourse.bass as bass
from concourse import mybir
from contextlib import ExitStack

P = 128
WSCALE = 64.0
EPS = 1e-5
NEG = 9.0e15


class Graph:

    def __init__(self, pairs, layer, half, parity):
        self.pairs, self.layer, self.half, self.p = pairs, layer, half, parity
        self.s = half * 2 + parity

    def moved(self, halves, parity):
        half, layer = self.half + halves, self.layer
        if isinstance(half, int) and half < 0:
            half, layer = self.pairs - 1, layer - 1
        elif isinstance(half, int) and half == self.pairs:
            half, layer = 0, layer + 1
        return Graph(self.pairs, layer, half, parity)

    def next(self):
        return self.moved(0, 1) if self.p == 0 else self.moved(1, 0)

    def prev(self):
        return self.moved(0, 0) if self.p == 1 else self.moved(-1, 1)

    def before(self):
        return self.moved(-1, self.p)

    def begins_layer(self):
        return isinstance(self.half, int) and self.half == 0 and self.p == 0

    def is_number(self, s):
        return isinstance(self.half, int) and self.s == s

    def ends_layer(self):
        return isinstance(self.half, int) and self.half == self.pairs - 1 and self.p == 1


class Signal:

    def __init__(self, sem, graphs, layers, per=1):
        self.sem, self.graphs, self.layers, self.per = sem, graphs, layers, per

    def at(self, graph, k=None):
        base = sum(self.per * self.graphs for layer in self.layers if layer < graph.layer)
        if graph.layer not in self.layers:
            return base
        value = graph.s * self.per + (base + (self.per if k is None else k))
        return max(value, 0) if isinstance(value, int) else value


class ParitySignal:

    def __init__(self, sems, graphs):
        self.sems, self.graphs = sems, graphs

    def of(self, graph):
        return self.sems[graph.p]

    def at(self, graph):
        if graph.layer < 0:
            return 0
        return graph.half * 16 + (graph.layer * 16 * (self.graphs // 2) + 16)


def residual_graph_layers(nc, a, out):
    f32, f16, bf16, u8 = mybir.dt.float32, mybir.dt.float16, mybir.dt.bfloat16, mybir.dt.uint8
    ALU, ACT, AX = mybir.AluOpType, mybir.ActivationFunctionType, mybir.AxisListType
    B, N, C = a["x"].shape
    NT, KC = N // P, C // P
    HEADS = 12
    E = C // HEADS
    EV = E + 1
    PAIRS = HEADS // 2
    MH = 6
    DH = C // MH
    DV = DH + 1
    LAYERS, ATT = 4, 1
    GATS = tuple(layer for layer in range(LAYERS) if layer != ATT)
    NW = 4
    BANK = 512
    x_dram = a["x"].rearrange("b (t p) c -> b p t c", p=P)
    out_dram = out.rearrange("b (t p) c -> b p t c", p=P)
    adj_dram = a["adj"].rearrange("b (t p) m -> b p t m", p=P)
    adjT_dram = a["adjT"].rearrange("b (t p) n -> b p t n", p=P)

    ctx = ExitStack()
    with ctx:
        def sb(name, shape, dt=f32):
            return ctx.enter_context(nc.sbuf_tensor(name, shape, dt))

        def sem(name):
            return ctx.enter_context(nc.semaphore(name))

        x_all = sb("x_all", [P, B, NT, C])
        x_in = sb("x_in", [P, 2, NT, C])
        x_res = sb("x_res", [P, 2, NT, C])
        mask = sb("mask", [P, 2, NT, N], u8)
        x_hi = sb("x_hi", [P, 2, KC, N], f16)
        x_lo = sb("x_lo", [P, 2, KC, N], f16)
        w_stage = sb("w_stage", [P, 2, KC, C])
        w_hi = sb("w_hi", [P, 4, KC, C], f16)
        w_lo = sb("w_lo", [P, 4, KC, C], f16)
        ident = sb("ident", [P, P])
        ident_bf = sb("ident_bf", [P, P], bf16)
        head_of = sb("head_of", [P, KC, HEADS])
        part_of = sb("part_of", [64, HEADS])
        pick_head = sb("pick_head", [64, HEADS, P], f16)
        w_score = sb("w_score", [P, 2, KC])
        score_mat = sb("score_mat", [P, 2, KC, 2 * HEADS])
        ones12 = sb("ones12", [HEADS, P])
        row_pq = sb("row_pq", [4, 4])
        row_in = sb("row_in", [4, C])
        row_hi = sb("row_hi", [4, C], f16)
        bias_row = sb("bias_row", [4, 2, C], f16)
        pick_row = sb("pick_row", [4, 2, P], f16)
        bias_col = sb("bias_col", [P, 2, KC])
        minus_half = sb("minus_half", [P, NT])
        w_scale_col = sb("w_scale_col", [P, NT, HEADS, 1])
        one = sb("one", [P, KC, 1])
        minus_one = sb("minus_one", [P, NT])
        eps_whole = sb("eps_whole", [P, NT])
        eps_half = sb("eps_half", [P, NT])
        sd = sb("sd", [P, NT, 2 * HEADS])
        d_max = sb("d_max", [HEADS, 1])
        d_max_diag = sb("d_max_diag", [HEADS, HEADS])
        s_pos = sb("s_pos", [HEADS, N])
        s_parts = sb("s_parts", [64, 2, N], f16)
        below = sb("below", [P, NT, HEADS])
        above = sb("above", [P, NT, HEADS])
        over = sb("over", [P, NT, N], bf16)
        G = sb("G", [P, NT, HEADS])
        D = sb("D", [P, NT, HEADS])
        b_node = sb("b_node", [P, 2, NT, HEADS])
        neg_adj = sb("neg_adj", [P, 2, NT, N], f16)
        rden = sb("rden", [P, NT, HEADS])
        row_max = sb("row_max", [P, 2, NT])
        settled = sb("settled", [P, NT])
        stats = sb("stats", [P, NT, 6])
        mean_var = sb("mean_var", [P, NT, 2])
        var_eps = sb("var_eps", [P, NT])
        rstd = sb("rstd", [P, NT])
        mean_rstd = sb("mean_rstd", [P, NT])
        shift = sb("shift", [P, NT])
        h_sb = sb("h_sb", [P, NT, HEADS, EV])
        buf_a = sb("buf_a", [P, NW * NT * N // 2])
        buf_b = sb("buf_b", [P, 2, 2 * NT * HEADS * EV])
        buf_c = sb("buf_c", [P, 2 * NT * C])
        buf_d = sb("buf_d", [P, 2 * NT * C])
        buf_e = sb("buf_e", [P, NT * HEADS * EV])
        buf_f = sb("buf_f", [P, NT * C])
        buf_g = sb("buf_g", [P, NT * HEADS * EV])
        y = sb("y", [P, NT, C])
        x_out = sb("x_out", [P, 2, NT, C])
        def ps(name):
            return ctx.enter_context(nc.psum_tensor(name, [P, 2, BANK], f32))

        ps_t, ps_h, ps_b, ps_o = ps("ps_t"), ps("ps_h"), ps("ps_b"), ps("ps_o")
        t_flat = ps_t[:, :, :].rearrange("p t c -> p (t c)")
        tr_ps = t_flat[:, 0:KC * N].rearrange("p (k n) -> p k n", k=KC)

        x_loaded = ParitySignal([sem("x_loaded0"), sem("x_loaded1")], B)
        res_loaded = ParitySignal([sem("res_loaded0"), sem("res_loaded1")], B)
        mask_loaded = ParitySignal([sem("mask_loaded0"), sem("mask_loaded1")], B)
        saved = ParitySignal([sem("saved0"), sem("saved1")], B)
        xt_ready = Signal(sem("xt_ready"), B, range(LAYERS))
        hi_ready = Signal(sem("hi_ready"), B, range(LAYERS))
        lo_ready = Signal(sem("lo_ready"), B, range(LAYERS))
        y_ready = Signal(sem("y_ready"), B, range(LAYERS))
        stats_ready = Signal(sem("stats_ready"), B, range(LAYERS))
        mv_ready = Signal(sem("mv_ready"), B, range(LAYERS))
        veps_ready = Signal(sem("veps_ready"), B, range(LAYERS))
        rstd_ready = Signal(sem("rstd_ready"), B, range(LAYERS))
        mr_ready = Signal(sem("mr_ready"), B, range(LAYERS))
        shift_ready = Signal(sem("shift_ready"), B, range(LAYERS))
        normed = Signal(sem("normed"), B, range(LAYERS), 2)
        w_loaded = [sem(f"w_loaded{i}") for i in range(2)]
        small_loaded = sem("small_loaded")
        w_hi_ready = sem("w_hi_ready")
        w_lo_ready = sem("w_lo_ready")
        rows_ready = sem("rows_ready")
        prep_step = sem("prep_step")
        const_ready = sem("const_ready")
        pick_ready = sem("pick_ready")
        count = {"prep": 0}

        def split_product(dst, lhs_hi, lhs_lo, w, more):
            for k in range(KC):
                nc.tensor.matmul(dst, lhs_hi(k), w_hi[:, w, k, :], start=(k == 0), stop=False)
                nc.tensor.matmul(dst, lhs_hi(k), w_lo[:, w, k, :], start=False, stop=False)
                last = nc.tensor.matmul(dst, lhs_lo(k), w_hi[:, w, k, :], start=False,
                                        stop=(k == KC - 1 and not more))
            return last

        def add_bias(dst, layer, which, **kw):
            return nc.tensor.matmul(dst, pick_row[:, which, :], bias_row[:, layer % 2, :], start=False, stop=True, **kw)

        def project(slot, hi, lo, layer, tile=None, bias=None):
            for t in range(NT) if tile is None else (tile,):
                last = split_product(ps_h[:, t, 0:C], lambda k: hi[:, k, t * P:(t + 1) * P],
                                     lambda k: lo[:, k, t * P:(t + 1) * P], slot, bias is not None)
                if bias is not None:
                    last = add_bias(ps_h[:, t, 0:C], layer, bias)
            return last

        def transpose_tiles(src):
            for t in range(NT):
                for k in range(KC):
                    last = nc.tensor.transpose(tr_ps[:, k, t * P:(t + 1) * P], src[:, t, k * P:(k + 1) * P],
                                               ident[:, :])
            return last

        def normalise_stats(graph):
            nc.vector.wait_ge(y_ready.sem, y_ready.at(graph))
            for t in range(NT):
                last = nc.vector.bn_stats(stats[:, t, :], y[:, t, :])
            last.then_inc(stats_ready.sem, 1)

        def settle(graph):
            nc.vector.wait_ge(stats_ready.sem, stats_ready.at(graph))
            nc.vector.tensor_copy(settled[:, :], minus_one[:, :])

        def normalise_moments(graph):
            for t in range(NT):
                last = nc.vector.bn_aggr(mean_var[:, t, :], stats[:, t, :])
            last.then_inc(mv_ready.sem, 1)

        def normalise_factors(graph, eps):
            nc.gpsimd.wait_ge(mv_ready.sem, mv_ready.at(graph))
            nc.gpsimd.tensor_tensor(var_eps[:, :], mean_var[:, :, 1], eps, ALU.add).then_inc(veps_ready.sem, 1)
            nc.gpsimd.wait_ge(veps_ready.sem, veps_ready.at(graph))
            nc.gpsimd.tensor_tensor(rstd[:, :], var_eps[:, :], minus_half[:, :], ALU.pow)\
                .then_inc(rstd_ready.sem, 1)
            nc.gpsimd.wait_ge(rstd_ready.sem, rstd_ready.at(graph))
            nc.gpsimd.tensor_tensor(mean_rstd[:, :], mean_var[:, :, 0], rstd[:, :], ALU.mult)\
                .then_inc(mr_ready.sem, 1)
            nc.gpsimd.wait_ge(mr_ready.sem, mr_ready.at(graph))
            nc.gpsimd.tensor_tensor(shift[:, :], mean_rstd[:, :], minus_one[:, :], ALU.mult)\
                .then_inc(shift_ready.sem, 1)

        def normalise_apply(graph):
            nc.scalar.wait_ge(shift_ready.sem, shift_ready.at(graph))
            nc.scalar.wait_ge(saved.of(graph), saved.at(graph.before()))
            for t in range(NT):
                nc.scalar.activation(x_out[:, graph.p, t, :], y[:, t, :], ACT.Identity, bias=shift[:, t:t + 1],
                                     scale=rstd[:, t:t + 1]).then_inc(normed.sem, 1)

        w_att = buf_a[:, :].bitcast(f16).rearrange("p (i t n) -> p i t n", i=NW, t=NT)
        vals = [buf_b[:, q, :].bitcast(f16).rearrange("p (r t h e) -> p r t h e", r=2, t=NT, h=HEADS)
                for q in range(2)]
        gvals = buf_g[:, :].rearrange("p (t h e) -> p t h e", t=NT, h=HEADS)
        gate4 = buf_c[:, :].rearrange("p (q t c) -> p q t c", q=2, t=NT)
        z = buf_d[:, 0:NT * C].rearrange("p (t h e) -> p t h e", t=NT, h=HEADS)
        z_flat = buf_d[:, 0:NT * C].rearrange("p (t c) -> p t c", t=NT)
        z_exp = buf_d[:, NT * C:2 * NT * C].rearrange("p (t c) -> p t c", t=NT)
        th = buf_e[:, 0:NT * C].rearrange("p (t c) -> p t c", t=NT)
        weighed = buf_e[:, :].rearrange("p (t h e) -> p t h e", t=NT, h=HEADS)
        thT = buf_f[:, :].rearrange("p (k n) -> p k n", k=KC)
        HALF = HEADS // 2
        sums = ps_o[:, :, 0:HALF * 2 * EV].rearrange("p t (h r e) -> p t h r e", r=2, e=EV)
        sd_ps = t_flat[:, 0:NT * 2 * HEADS].rearrange("p (t c) -> p t c", t=NT)
        sT_ps = t_flat[0:HEADS, N:2 * N]
        dT_ps = t_flat[0:HEADS, 2 * N:3 * N]
        dmax_ps = t_flat[:, 0:HEADS]

        h_ready = Signal(sem("h_ready"), B, GATS, NT)
        th_ready = Signal(sem("th_ready"), B, GATS)
        tht_ready = Signal(sem("tht_ready"), B, GATS)
        hb_ready = Signal(sem("hb_ready"), B, GATS)
        tht_sb_ready = Signal(sem("tht_sb_ready"), B, GATS)
        sd_ps_ready = Signal(sem("sd_ps_ready"), B, GATS)
        sd_ready = Signal(sem("sd_ready"), B, GATS)
        sdt_ready = Signal(sem("sdt_ready"), B, GATS)
        dmax_ready = Signal(sem("dmax_ready"), B, GATS)
        spos_ready = Signal(sem("spos_ready"), B, GATS)
        diag_ready = Signal(sem("diag_ready"), B, GATS)
        dmax_ps_ready = Signal(sem("dmax_ps_ready"), B, GATS)
        s_hi_ready = Signal(sem("s_hi_ready"), B, GATS)
        parts_ready = Signal(sem("parts_ready"), B, GATS)
        above_ready = Signal(sem("above_ready"), B, GATS)
        v_scaled = Signal(sem("v_scaled"), B, GATS)
        gv_scaled = Signal(sem("gv_scaled"), B, GATS)
        vals_hi = Signal(sem("vals_hi"), B, GATS)
        gvals_ready = Signal(sem("gvals_ready"), B, GATS)
        gvals_hi = Signal(sem("gvals_hi"), B, GATS)
        neg_adj_ready = Signal(sem("neg_adj_ready"), B, GATS)
        half_scaled = Signal(sem("half_scaled"), B, GATS, 2)
        half_read = Signal(sem("half_read"), B, GATS, 2)
        relative_ready = Signal(sem("relative_ready"), B, GATS)
        gd_ready = Signal(sem("gd_ready"), B, GATS)
        h_sb_ready = Signal(sem("h_sb_ready"), B, GATS)
        scaled_d_ready = Signal(sem("scaled_d_ready"), B, GATS)
        vals_ready = Signal(sem("vals_ready"), B, GATS)
        gate_ps_ready = Signal(sem("gate_ps_ready"), B, GATS, NT)
        gate_t_ready = Signal(sem("gate_t_ready"), B, GATS)
        gate_ready = Signal(sem("gate_ready"), B, GATS)
        bcast_ready = Signal(sem("bcast_ready"), B, GATS, PAIRS)
        OFFLOADED = (3, 9)
        w_ready = Signal(sem("w_ready"), B, GATS, HEADS - len(OFFLOADED))
        relu_ready = Signal(sem("relu_ready"), B, GATS, len(OFFLOADED))
        over_ready = Signal(sem("over_ready"), B, GATS, len(OFFLOADED))
        w_offloaded = Signal(sem("w_offloaded"), B, GATS, len(OFFLOADED))
        summed = Signal(sem("summed"), B, GATS, HEADS)
        rden_ready = Signal(sem("rden_ready"), B, GATS)
        z_ready = Signal(sem("z_ready"), B, GATS)
        zexp_ready = Signal(sem("zexp_ready"), B, GATS)
        zpos_ready = Signal(sem("zpos_ready"), B, GATS)
        elu_ready = Signal(sem("elu_ready"), B, GATS)
        delta_ready = Signal(sem("delta_ready"), B, GATS)
        gated_ready = Signal(sem("gated_ready"), B, GATS)

        def wait_weights(eng, g, h):
            if h in OFFLOADED:
                eng.wait_ge(w_offloaded.sem, w_offloaded.at(g, OFFLOADED.index(h) + 1))
            else:
                eng.wait_ge(w_ready.sem, w_ready.at(g, sum(i not in OFFLOADED for i in range(h + 1))))

        def wait_all_weights(eng, g):
            eng.wait_ge(w_ready.sem, w_ready.at(g))
            eng.wait_ge(w_offloaded.sem, w_offloaded.at(g))

        probs = buf_a[:, :].rearrange("p (i t k) -> p i t k", i=2, t=NT)
        V_WORDS = NT * MH * DV
        v_sb = [buf_b[:, q, 0:V_WORDS].bitcast(f16).rearrange("p (r t h e) -> p r t h e", r=2, t=NT, h=MH)
                for q in range(2)]
        probsT = [buf_b[:, 1, V_WORDS:V_WORDS + NT * N].bitcast(f16).rearrange("p (r t q) -> p r t q", r=2, t=NT),
                  neg_adj[:, :, :, :]]
        qT = [buf_c[:, q * NT * C:(q + 1) * NT * C].bitcast(f16).rearrange("p (r k n) -> p r k n", r=2, k=KC)
              for q in range(2)]
        kT = [b.bitcast(f16).rearrange("p (r k n) -> p r k n", r=2, k=KC)
              for b in (h_sb[:, :, :, :].rearrange("p t h e -> p (t h e)")[:, 0:NT * C], buf_d[:, 0:NT * C])]
        att = buf_e[:, 0:NT * C].rearrange("p (t h e) -> p t h e", t=NT, h=MH)
        att_flat = buf_e[:, 0:NT * C].rearrange("p (t c) -> p t c", t=NT)
        att_parts = buf_g[:, 0:NT * C].bitcast(f16).rearrange("p (i k n) -> p i k n", i=2, k=KC)
        att_hi, att_lo = att_parts[:, 0], att_parts[:, 1]
        neg_mask = [buf_f[:, 0:NT * N // 2].bitcast(bf16).rearrange("p (t k) -> p t k", t=NT),
                    buf_d[:, NT * C:NT * C + NT * N // 2].bitcast(bf16).rearrange("p (t k) -> p t k", t=NT)]
        qk_raw = buf_b[:, 0, V_WORDS:V_WORDS + KC * N].rearrange("p (k n) -> p k n", k=KC)
        qk_ps = ps_h[:, :, :].rearrange("p t c -> p (t c)")[:, 0:KC * N].rearrange("p (k n) -> p k n", k=KC)

        negm_ready = Signal(sem("negm_ready"), B, (ATT,))
        q_ps_ready = Signal(sem("q_ps_ready"), B, (ATT,))
        q_ready = Signal(sem("q_ready"), B, (ATT,))
        k_ps_ready = Signal(sem("k_ps_ready"), B, (ATT,))
        k_ready = Signal(sem("k_ready"), B, (ATT,))
        q_hi_ready = Signal(sem("q_hi_ready"), B, (ATT,))
        q_split = Signal(sem("q_split"), B, (ATT,))
        k_hi_ready = Signal(sem("k_hi_ready"), B, (ATT,))
        k_split = Signal(sem("k_split"), B, (ATT,))
        v_ps_ready = Signal(sem("v_ps_ready"), B, (ATT,))
        v_ready = Signal(sem("v_ready"), B, (ATT,))
        s_ready = Signal(sem("s_ready"), B, (ATT,), MH)
        max_ready = Signal(sem("max_ready"), B, (ATT,), MH)
        p_ready = Signal(sem("p_ready"), B, (ATT,), MH)
        pt_ps_ready = Signal(sem("pt_ps_ready"), B, (ATT,), MH)
        pt_hi_ready = Signal(sem("pt_hi_ready"), B, (ATT,), MH)
        pt_lo_ready = Signal(sem("pt_lo_ready"), B, (ATT,), MH)
        v_hi_ready = Signal(sem("v_hi_ready"), B, (ATT,))
        att_ps_ready = Signal(sem("att_ps_ready"), B, (ATT,), MH)
        mden_ready = Signal(sem("mden_ready"), B, (ATT,))
        att_ready = Signal(sem("att_ready"), B, (ATT,))
        attT_ready = Signal(sem("attT_ready"), B, (ATT,))
        atthi_ready = Signal(sem("atthi_ready"), B, (ATT,))
        attlo_ready = Signal(sem("attlo_ready"), B, (ATT,))
        out_ready = Signal(sem("out_ready"), B, (ATT,), NT)

        def weights_of(name):
            return a[name].rearrange("(k p) c -> p k c", p=P)

        W, H, WQ, WK, WV, WF = range(6)
        slot_of = {(0, W): 0, (0, H): 1, (1, WV): 2, (1, WF): 3, (1, WQ): 0, (1, WK): 1, (2, W): 2, (2, H): 0,
                   (3, W): 1, (3, H): 3}
        names = {W: "W", H: "H_w", WQ: "Wq", WK: "Wk", WV: "Wv", WF: "Wf"}
        order = list(slot_of)

        def splits_until(layer, which):
            return order.index((layer, which)) + 1

        def load_weights(sp, layer, which):
            i = order.index((layer, which))
            if i >= 2:
                sp.wait_ge(w_lo_ready, i - 1)
            sp.dma_start(w_stage[:, i % 2], weights_of(f"L{layer}_gnn_{names[which]}")).then_inc(w_loaded[i % 2], 16)

        def split_weights_hi(act, layer, which):
            i = order.index((layer, which))
            act.wait_ge(w_loaded[i % 2], 16 * (i // 2 + 1))
            nc.scalar.activation(w_hi[:, slot_of[layer, which]], w_stage[:, i % 2], ACT.Copy, scale=WSCALE)\
                .then_inc(w_hi_ready, 1)

        def split_weights_lo(dve, layer, which):
            i = order.index((layer, which))
            dve.wait_ge(w_hi_ready, i + 1)
            nc.vector.scalar_tensor_tensor(w_lo[:, slot_of[layer, which]], w_stage[:, i % 2], WSCALE,
                                           w_hi[:, slot_of[layer, which]], op0=ALU.mult, op1=ALU.subtract)\
                .then_inc(w_lo_ready, 1)

        def rows_of(layer):
            if layer == ATT:
                return [a[f"L{layer}_gnn_{w}"].rearrange("(o h e) -> o h e", o=1, h=1) for w in ("bv", "bf")]
            return [a[f"L{layer}_gnn_b"].rearrange("(o h e) -> o h e", o=1, h=1).to_broadcast([1, HEADS, E]),
                    a[f"L{layer}_gnn_H_b"].rearrange("(o h e) -> o h e", o=1, h=1)]

        N_CONSTANTS = 4
        N_ROWS = 6

        def load_rows(sp, layer):
            if layer > 0:
                sp.wait_ge(rows_ready, layer)
            for i, r in enumerate(rows_of(layer)):
                for q in range(2):
                    row = 2 * i + q
                    sp.dma_start(row_in[row:row + 1, :].rearrange("o (h e) -> o h e", e=r.shape[-1]), r)\
                        .then_inc(small_loaded, 16)
            if layer == ATT:
                sp.dma_start(bias_col[:, 0, :], a[f"L{layer}_gnn_bq"]).then_inc(small_loaded, 16)
                sp.dma_start(bias_col[:, 1, :], a[f"L{layer}_gnn_bk"]).then_inc(small_loaded, 16)
            else:
                sp.dma_start(w_score[:, 0, :], a[f"L{layer}_gnn_wsrc"]).then_inc(small_loaded, 16)
                sp.dma_start(w_score[:, 1, :], a[f"L{layer}_gnn_wdst"]).then_inc(small_loaded, 16)

        def prepare_rows(dve, layer):
            def chain(ins):
                count["prep"] += 1
                ins.then_inc(prep_step, 1)
                dve.wait_ge(prep_step, count["prep"])

            dve.wait_ge(small_loaded, 16 * (N_CONSTANTS + (layer + 1) * N_ROWS))
            chain(nc.vector.tensor_scalar(row_in[:, :], row_in[:, :], WSCALE, None, ALU.mult))
            chain(nc.vector.tensor_copy(row_hi[:, :], row_in[:, :]))
            chain(nc.vector.tensor_scalar(row_in[:, :], row_in[:, :], row_pq[:, 0:1], None, ALU.mult))
            chain(nc.vector.scalar_tensor_tensor(bias_row[:, layer % 2], row_hi[:, :], row_pq[:, 1:2],
                                                 row_in[:, :], op0=ALU.mult, op1=ALU.add))
            if layer == ATT:
                last = nc.vector.tensor_scalar(bias_col[:, 0, :], bias_col[:, 0, :], 1.0 / DH ** 0.5, None, ALU.mult)
            else:
                for i in range(2):
                    w = w_score[:, i, :].rearrange("p (k o) -> p k o", o=1).to_broadcast([P, KC, HEADS])
                    last = nc.vector.tensor_tensor(score_mat[:, layer % 2, :, i * HEADS:(i + 1) * HEADS],
                                                   head_of[:, :, :], w, ALU.mult)
            last.then_inc(rows_ready, 1)

        def graphs_stored_before(g):
            if g.s < 3:
                return [Graph(g.pairs, g.layer - 1, g.half, g.p)]
            return [Graph(g.pairs, g.layer - 1, g.pairs - 1, parity) for parity in range(2)]

        def load_x(sp, g):
            if g.layer > 0 and isinstance(g.half, int) and g.half < 2:
                for stored in graphs_stored_before(g):
                    sp.wait_ge(saved.of(stored), saved.at(stored))
            sp.wait_ge(xt_ready.sem, xt_ready.at(g.before()))
            src = x_dram[g.s] if g.layer == 0 else x_all[:, g.s]
            sp.dma_start(x_in[:, g.p], src).then_inc(x_loaded.of(g), 16)

        def load_res(sp, g):
            sp.wait_ge(y_ready.sem, y_ready.at(g.before()))
            src = x_dram[g.s] if g.layer == 0 else x_all[:, g.s]
            sp.dma_start(x_res[:, g.p], src).then_inc(res_loaded.of(g), 16)

        def store(sp, g):
            sp.wait_ge(normed.sem, normed.at(g))
            dst = out_dram[g.s] if g.layer == LAYERS - 1 else x_all[:, g.s]
            sp.dma_start(dst, x_out[:, g.p]).then_inc(saved.of(g), 16)

        def graph(layer, half, parity):
            return Graph(B // 2, layer, half, parity)

        START = graph(0, 0, 0)
        END = graph(LAYERS - 1, B // 2 - 1, 1)

        def exists(g):
            return 0 <= g.layer < LAYERS

        def is_gat(g):
            return g.layer in GATS

        def is_att(g):
            return g.layer == ATT

        def prepares_next(g):
            return g.is_number(3) and g.layer + 1 < LAYERS

        def pipeline(eng, layer, first, step, last):
            first(graph(layer, 0, 0))
            step(graph(layer, 0, 1))
            step(graph(layer, 1, 0))
            step(graph(layer, 1, 1))
            with eng.Fori(2, B // 2 - 1) as i:
                step(graph(layer, i, 0))
                step(graph(layer, i, 1))
            step(graph(layer, B // 2 - 1, 0))
            last(graph(layer, B // 2 - 1, 1))

        with nc.Block() as block:
            @block.sync
            def _(sp):
                load_weights(sp, 0, W)
                load_weights(sp, 0, H)
                load_x(sp, START)
                sp.dma_start(ident[:, :], a["c_ident"]).then_inc(small_loaded, 16)
                sp.dma_start(head_of[:, :, :], a["c_head_of"]).then_inc(small_loaded, 16)
                sp.dma_start(part_of[:, :], a["c_part_of"]).then_inc(small_loaded, 16)
                sp.dma_start(row_pq[:, :], a["c_row_pq"]).then_inc(small_loaded, 16)
                load_rows(sp, 0)
                load_x(sp, START.next())

            @block.scalar
            def _(act):
                split_weights_hi(act, 0, W)
                split_weights_hi(act, 0, H)

            @block.gpsimd
            def _(pool):
                nc.gpsimd.memset(ones12[:, :], 1.0)
                nc.gpsimd.memset(minus_half[:, :], -0.5)
                nc.gpsimd.memset(w_scale_col[:, :, :, :], WSCALE)
                nc.gpsimd.memset(one[:, :, :], 1.0)
                nc.gpsimd.memset(minus_one[:, :], -1.0)
                nc.gpsimd.memset(eps_whole[:, :], EPS)
                nc.gpsimd.memset(eps_half[:, :], EPS / 4)
                nc.gpsimd.memset(s_parts[:, :, :], 0.0).then_inc(const_ready, 1)
                pool.wait_ge(const_ready, 1)

            @block.vector
            def _(dve):
                split_weights_lo(dve, 0, W)
                split_weights_lo(dve, 0, H)
                prepare_rows(dve, 0)
                nc.vector.tensor_copy(ident_bf[:, :], ident[:, :])
                src = row_pq[:, 2:4].rearrange("p (w o) -> p w o", o=1).to_broadcast([4, 2, P])
                nc.vector.tensor_copy(pick_row[:, :, :], src)
                src = part_of[:, :].rearrange("p (h o) -> p h o", o=1).to_broadcast([64, HEADS, P])
                nc.vector.tensor_copy(pick_head[:, :, :], src).then_inc(pick_ready, 1)
                dve.wait_ge(pick_ready, 1)
                dve.wait_ge(rows_ready, 1)
                dve.wait_ge(w_lo_ready, 2)

        with nc.Block() as block:
            @block.sync
            def _(sp):
                def step(g):
                    ahead = g.next().next()
                    if exists(ahead):
                        load_x(sp, ahead)
                    load_res(sp, g)
                    if exists(g.prev()):
                        store(sp, g.prev())

                    following = g.layer + 1
                    if g.is_number(1) and following < LAYERS:
                        load_rows(sp, following)
                        for which in (WV, WF) if following == ATT else (W, H):
                            load_weights(sp, following, which)
                    if prepares_next(g) and following == ATT:
                        load_weights(sp, following, WQ)
                        load_weights(sp, following, WK)

                for layer in range(LAYERS):
                    pipeline(sp, layer, step, step, step)
                store(sp, END)
                sp.wait_ge(saved.of(END.prev()), saved.at(END.prev()))
                sp.wait_ge(saved.of(END), saved.at(END))

            @block.tensor
            def _(pe):
                def transpose_x(g):
                    pe.wait_ge(x_loaded.of(g), x_loaded.at(g))
                    transpose_tiles(x_in[:, g.p]).then_inc(xt_ready.sem, 1)

                def values(g, t):
                    if t == 0:
                        pe.wait_ge(lo_ready.sem, lo_ready.at(g))
                        pe.wait_ge(gate_t_ready.sem, gate_t_ready.at(g.prev()))
                        if g.begins_layer():
                            pe.wait_ge(w_lo_ready, splits_until(g.layer, W))
                            pe.wait_ge(rows_ready, g.layer + 1)
                    project(slot_of[g.layer, W], x_hi[:, g.p], x_lo[:, g.p], g.layer, t).then_inc(h_ready.sem, 1)

                def transpose_th(g):
                    pe.wait_ge(th_ready.sem, th_ready.at(g))
                    transpose_tiles(th).then_inc(tht_ready.sem, 1)
                    for t in range(NT):
                        last = add_bias(ps_h[:, t, 0:C], g.layer, 0, skip_group_check=True)
                    last.then_inc(hb_ready.sem, 1)

                def scores(g):
                    pe.wait_ge(tht_sb_ready.sem, tht_sb_ready.at(g))
                    for t in range(NT):
                        for k in range(KC):
                            last = nc.tensor.matmul(sd_ps[:, t, :], thT[:, k, t * P:(t + 1) * P],
                                                    score_mat[:, g.layer % 2, k, :], start=(k == 0), stop=(k == KC - 1))
                    last.then_inc(sd_ps_ready.sem, 1)

                def transpose_scores(g):
                    pe.wait_ge(sd_ready.sem, sd_ready.at(g))
                    for dst, c in ((sT_ps, 0), (dT_ps, HEADS)):
                        for t in range(NT):
                            last = nc.tensor.transpose(dst[:, t * P:(t + 1) * P], sd[:, t, c:c + HEADS], ident[:, :])
                    last.then_inc(sdt_ready.sem, 1)

                def broadcast_dmax(g):
                    pe.wait_ge(diag_ready.sem, diag_ready.at(g))
                    nc.tensor.matmul(dmax_ps, ones12[:, :], d_max_diag[:, :], start=True, stop=True)\
                        .then_inc(dmax_ps_ready.sem, 1)

                def gate(g, t):
                    if t == 0:
                        if g.begins_layer():
                            pe.wait_ge(w_lo_ready, splits_until(g.layer, H))
                        pe.wait_ge(h_sb_ready.sem, h_sb_ready.at(g))
                    project(slot_of[g.layer, H], x_hi[:, g.p], x_lo[:, g.p], g.layer, t, bias=1)\
                        .then_inc(gate_ps_ready.sem, 1)

                def broadcast_s(g, j):
                    if j == 0:
                        pe.wait_ge(parts_ready.sem, parts_ready.at(g))
                    if j < 2:
                        wait_all_weights(pe, g.prev())
                    else:
                        wait_weights(pe, g, 2 * j - 4)
                        wait_weights(pe, g, 2 * j - 3)
                    for h in range(2):
                        last = nc.tensor.matmul(ps_b[:, j % 2, h * N:(h + 1) * N], pick_head[:, 2 * j + h, :],
                                                s_parts[:, g.p, :], start=True, stop=True)
                    last.then_inc(bcast_ready.sem, 1)

                def sum_neighbours(g, j):
                    if j == 0:
                        pe.wait_ge(vals_ready.sem, vals_ready.at(g))
                        pe.wait_ge(gvals_ready.sem, gvals_ready.at(g))
                        pe.wait_ge(neg_adj_ready.sem, neg_adj_ready.at(g))
                    if 2 * j % HALF == 0:
                        pe.wait_ge(half_read.sem, half_read.at(g, 2 * j // HALF))
                        heads = slice(2 * j, 2 * j + HALF)
                        for t in range(NT):
                            for m in range(NT):
                                for r in range(2):
                                    nc.tensor.matmul(sums[:, t, :, 1, :], neg_adj[:, g.p, m, t * P:(t + 1) * P],
                                                     vals[g.p][:, r, m, heads, EV:2 * EV],
                                                     start=(m == 0 and r == 0), stop=False, skip_group_check=True)
                    for h in (2 * j, 2 * j + 1):
                        wait_weights(pe, g, h)
                        for t in range(NT):
                            for m in range(NT):
                                for r in range(2):
                                    last = nc.tensor.matmul(
                                        sums[:, t, h % HALF].rearrange("p r e -> p (r e)"),
                                        w_att[:, h % NW, m, t * P:(t + 1) * P], vals[g.p][:, r, m, h, :],
                                        start=False, stop=(m == NT - 1 and r == 1), skip_group_check=True)
                        last.then_inc(summed.sem, 1)

                def gat_step(g):
                    n, ahead = g.next(), g.next().next()
                    for j in range(PAIRS):
                        if exists(n):
                            if j == 0:
                                values(n, 0)
                                values(n, 1)
                            elif j == 2:
                                transpose_th(n)
                            elif j == 3:
                                scores(n)
                            elif j == 5:
                                broadcast_dmax(n)
                                gate(n, 1)
                                broadcast_s(n, 0)
                                if exists(ahead):
                                    pe.wait_ge(relative_ready.sem, relative_ready.at(n))
                                    transpose_x(ahead)
                        sum_neighbours(g, j)
                        if j + 2 < PAIRS:
                            broadcast_s(g, j + 2)
                        if exists(n):
                            if j == 3:
                                transpose_scores(n)
                                gate(n, 0)
                            elif j == 5:
                                broadcast_s(n, 1)

                def project_T(g, slot, chunks):
                    for e in chunks:
                        for k in range(KC):
                            for n, (w, x) in enumerate(((w_hi, x_hi), (w_hi, x_lo), (w_lo, x_hi))):
                                last = nc.tensor.matmul(qk_ps[:, e, :], w[:, slot, k, e * P:(e + 1) * P],
                                                        x[:, g.p, k, :], start=(k == 0 and n == 0),
                                                        stop=(k == KC - 1 and n == 2))
                    return last

                def project_q(g):
                    project_T(g, slot_of[ATT, WQ], range(KC)).then_inc(q_ps_ready.sem, 1)

                def project_k(g, chunks):
                    if 0 in chunks:
                        pe.wait_ge(q_ready.sem, q_ready.at(g))
                    last = project_T(g, slot_of[ATT, WK], chunks)
                    if KC - 1 in chunks:
                        last.then_inc(k_ps_ready.sem, 1)

                def project_v(g):
                    project(slot_of[ATT, WV], x_hi[:, g.p], x_lo[:, g.p], g.layer, bias=0)\
                        .then_inc(v_ps_ready.sem, 1)

                def score(g, h):
                    if h == 0:
                        pe.wait_ge(q_split.sem, q_split.at(g))
                        pe.wait_ge(k_split.sem, k_split.at(g))
                        pe.wait_ge(negm_ready.sem, negm_ready.at(g))
                    pe.wait_ge(pt_lo_ready.sem, pt_lo_ready.at(g, h - 1))
                    r = (h % 2) * DH
                    for t in range(NT):
                        dst = ps_b[:, h % 2, t * N:(t + 1) * N]
                        for i, (q_part, k_part) in enumerate(((0, 0), (0, 1), (1, 0))):
                            nc.tensor.matmul(dst, qT[g.p][r:r + DH, q_part, h // 2, t * P:(t + 1) * P],
                                             kT[g.p][r:r + DH, k_part, h // 2, :], start=(i == 0), stop=False)
                        last = nc.tensor.matmul(dst, ident_bf[:, :], neg_mask[g.p][:, t, :], start=False, stop=True)
                    last.then_inc(s_ready.sem, 1)

                def transpose_probs(g, h):
                    pe.wait_ge(p_ready.sem, p_ready.at(g, h + 1))
                    for t in range(NT):
                        for k in range(NT):
                            last = nc.tensor.transpose(ps_b[:, h % 2, k * N + t * P:k * N + (t + 1) * P],
                                                       probs[:, h % 2, t, k * P:(k + 1) * P], ident[:, :])
                    last.then_inc(pt_ps_ready.sem, 1)

                def attend(g, h):
                    pe.wait_ge(pt_lo_ready.sem, pt_lo_ready.at(g, h + 1))
                    if h == 0:
                        pe.wait_ge(v_ready.sem, v_ready.at(g))
                        pe.wait_ge(att_ready.sem, att_ready.at(g.prev()))
                    for t in range(NT):
                        for k in range(NT):
                            for i, (p_part, v_part) in enumerate(((0, 0), (0, 1), (1, 0))):
                                last = nc.tensor.matmul(ps_o[:, t, h * DV:(h + 1) * DV],
                                                        probsT[h % 2][:, p_part, k, t * P:(t + 1) * P],
                                                        v_sb[g.p][:, v_part, k, h, :],
                                                        start=(k == 0 and i == 0), stop=(k == NT - 1 and i == 2))
                    last.then_inc(att_ps_ready.sem, 1)

                def transpose_att(g):
                    pe.wait_ge(att_ready.sem, att_ready.at(g))
                    transpose_tiles(att_flat).then_inc(attT_ready.sem, 1)

                def project_out(g, t):
                    if t == 0:
                        pe.wait_ge(attlo_ready.sem, attlo_ready.at(g))
                    project(slot_of[ATT, WF], att_hi, att_lo, g.layer, t, bias=1).then_inc(out_ready.sem, 1)

                def att_step(g):
                    n, b, ahead = g.next(), g.prev(), g.next().next()
                    for h in range(MH):
                        transpose_probs(g, h)
                        if h == 0:
                            pe.wait_ge(lo_ready.sem, lo_ready.at(n))
                            pe.wait_ge(y_ready.sem, y_ready.at(b.prev()))
                            project_q(n)
                        if h == 1 and is_att(b):
                            transpose_att(b)
                        if h == 1:
                            project_k(n, (0,))
                        if h == 2:
                            project_k(n, (1, 2))
                        if h == 3:
                            pe.wait_ge(k_ready.sem, k_ready.at(n))
                            project_v(n)
                        if h == 4:
                            pe.wait_ge(attlo_ready.sem, attlo_ready.at(b))
                            transpose_x(ahead)
                            pe.wait_ge(v_ready.sem, v_ready.at(n))
                        if h in (4, 5) and is_att(b):
                            project_out(b, h - 4)
                        attend(g, h)
                        if h + 2 < MH:
                            score(g, h + 2)
                        else:
                            score(n, h + 2 - MH)

                def first(g):
                    transpose_x(g)
                    values(g, 0)
                    values(g, 1)
                    transpose_th(g)
                    scores(g)
                    gate(g, 0)
                    gate(g, 1)
                    transpose_scores(g)
                    broadcast_dmax(g)
                    pe.wait_ge(relative_ready.sem, relative_ready.at(g))
                    transpose_x(g.next())
                    broadcast_s(g, 0)
                    broadcast_s(g, 1)
                    gat_step(g)

                def gat_to_att(g):
                    n, ahead = g.next(), g.next().next()
                    for j in range(PAIRS):
                        if j == 0:
                            pe.wait_ge(w_lo_ready, splits_until(ATT, WF))
                            pe.wait_ge(rows_ready, ATT + 1)
                            pe.wait_ge(lo_ready.sem, lo_ready.at(n))
                            pe.wait_ge(gate_t_ready.sem, gate_t_ready.at(g))
                            project_v(n)
                        elif j == 2:
                            pe.wait_ge(w_lo_ready, splits_until(ATT, WK))
                            pe.wait_ge(v_ready.sem, v_ready.at(n))
                            project_q(n)
                        elif j == 4:
                            project_k(n, range(KC))
                        elif j == 5:
                            transpose_x(ahead)
                        sum_neighbours(g, j)
                        if j + 2 < PAIRS:
                            broadcast_s(g, j + 2)
                    score(n, 0)
                    score(n, 1)
                    pe.wait_ge(half_read.sem, half_read.at(g))

                def att_to_gat(g):
                    n, b, ahead = g.next(), g.prev(), g.next().next()
                    for h in range(MH):
                        transpose_probs(g, h)
                        if h == 0:
                            pe.wait_ge(y_ready.sem, y_ready.at(b.prev()))
                            values(n, 0)
                            values(n, 1)
                        elif h == 1:
                            transpose_att(b)
                        elif h == 2:
                            pe.wait_ge(attlo_ready.sem, attlo_ready.at(b))
                            transpose_th(n)
                        elif h == 3:
                            scores(n)
                        elif h == 4:
                            pe.wait_ge(h_sb_ready.sem, h_sb_ready.at(n))
                            project_out(b, 0)
                            project_out(b, 1)
                        elif h == 5:
                            transpose_scores(n)
                        attend(g, h)
                        if h + 2 < MH:
                            score(g, h + 2)
                    pe.wait_ge(y_ready.sem, y_ready.at(b))
                    gate(n, 0)
                    broadcast_dmax(n)
                    gate(n, 1)
                    pe.wait_ge(relative_ready.sem, relative_ready.at(n))
                    transpose_att(g)
                    pe.wait_ge(pt_lo_ready.sem, pt_lo_ready.at(g))
                    broadcast_s(n, 0)
                    broadcast_s(n, 1)
                    pe.wait_ge(gate_t_ready.sem, gate_t_ready.at(n))
                    pe.wait_ge(attlo_ready.sem, attlo_ready.at(g))
                    transpose_x(ahead)
                    project_out(g, 0)
                    project_out(g, 1)
                    pe.wait_ge(y_ready.sem, y_ready.at(g))

                for layer in range(LAYERS):
                    if layer == ATT:
                        pipeline(pe, layer, att_step, att_step, att_to_gat)
                    else:
                        pipeline(pe, layer, first if layer == 0 else gat_step, gat_step,
                                 gat_to_att if layer + 1 == ATT else gat_step)

            @block.scalar
            def _(act):
                def load_mask(g):
                    if is_att(g.before()):
                        act.wait_ge(negm_ready.sem, negm_ready.at(g.before()))
                    else:
                        wait_all_weights(act, g.before())
                    src = adjT_dram if is_gat(g) else adj_dram
                    act.dma_start(mask[:, g.p], src[g.s]).then_inc(mask_loaded.of(g), 16)

                def split_hi(g):
                    act.wait_ge(xt_ready.sem, xt_ready.at(g))
                    if is_att(g.before()):
                        act.wait_ge(k_ps_ready.sem, k_ps_ready.at(g.before()))
                        act.wait_ge(v_ps_ready.sem, v_ps_ready.at(g.before()))
                    else:
                        act.wait_ge(gate_ps_ready.sem, gate_ps_ready.at(g.before()))
                    nc.scalar.activation(x_hi[:, g.p], tr_ps, ACT.Copy).then_inc(hi_ready.sem, 1)

                def tanh_h(g):
                    act.wait_ge(h_ready.sem, h_ready.at(g))
                    nc.scalar.activation(th, ps_h[:, :, 0:C], ACT.Tanh, scale=1.0 / WSCALE).then_inc(th_ready.sem, 1)

                def keep_thT(g):
                    act.wait_ge(tht_ready.sem, tht_ready.at(g))
                    nc.scalar.activation(thT, tr_ps, ACT.Copy).then_inc(tht_sb_ready.sem, 1)

                def keep_h(g):
                    act.wait_ge(hb_ready.sem, hb_ready.at(g))
                    act.wait_ge(vals_ready.sem, vals_ready.at(g.prev()))
                    act.wait_ge(gvals_ready.sem, gvals_ready.at(g.prev()))
                    src = ps_h[:, :, 0:C].rearrange("p t (h e) -> p t h e", e=E)
                    nc.scalar.activation(h_sb[:, :, :, 0:E], src, ACT.Copy)\
                        .then_inc(h_sb_ready.sem, 1)

                def exp_gd(g):
                    act.wait_ge(relative_ready.sem, relative_ready.at(g))
                    nc.scalar.activation(D[:, :, :], below[:, :, :], ACT.Exp, scale=-0.2)
                    nc.scalar.activation(G[:, :, :], below[:, :, :], ACT.Exp, scale=-0.8)
                    nc.scalar.activation(b_node[:, g.p], above[:, :, :], ACT.Exp, scale=-0.8).then_inc(gd_ready.sem, 1)

                def negate_adj(g):
                    act.wait_ge(mask_loaded.of(g), mask_loaded.at(g))
                    nc.scalar.activation(neg_adj[:, g.p], mask[:, g.p], ACT.Copy, scale=-1.0)\
                        .then_inc(neg_adj_ready.sem, 1)

                def keep_vals_hi(g):
                    act.wait_ge(v_scaled.sem, v_scaled.at(g))
                    nc.scalar.activation(vals[g.p][:, 0, :, :, 0:EV], h_sb[:, :, :, :], ACT.Copy)\
                        .then_inc(vals_hi.sem, 1)

                def keep_gvals_hi(g):
                    act.wait_ge(gv_scaled.sem, gv_scaled.at(g))
                    nc.scalar.activation(vals[g.p][:, 0, :, :, EV:2 * EV], gvals, ACT.Copy).then_inc(gvals_hi.sem, 1)

                def gate_tanh(g):
                    act.wait_ge(gate_ps_ready.sem, gate_ps_ready.at(g))
                    act.wait_ge(gated_ready.sem, gated_ready.at(g.before()))
                    nc.scalar.activation(gate4[:, g.p], ps_h[:, :, 0:C], ACT.Tanh, scale=0.5 / WSCALE)\
                        .then_inc(gate_t_ready.sem, 1)

                def gate_scale(g):
                    act.wait_ge(gate_t_ready.sem, gate_t_ready.at(g))
                    nc.scalar.activation(gate4[:, g.p], gate4[:, g.p], ACT.Copy, scale=0.25, bias=0.25)\
                        .then_inc(gate_ready.sem, 1)

                def exp_z(g):
                    act.wait_ge(z_ready.sem, z_ready.at(g))
                    act.wait_ge(y_ready.sem, y_ready.at(g.prev()))
                    nc.scalar.activation(z_exp, z_flat, ACT.Exp).then_inc(zexp_ready.sem, 1)

                def differences(g, h):
                    act.wait_ge(relative_ready.sem, relative_ready.at(g))
                    act.wait_ge(bcast_ready.sem, bcast_ready.at(g, h // 2 + 1))
                    if h == OFFLOADED[0]:
                        act.wait_ge(w_offloaded.sem, w_offloaded.at(g.prev()))
                    else:
                        act.wait_ge(w_offloaded.sem, w_offloaded.at(g, OFFLOADED.index(h)))
                    for m in range(NT):
                        last = nc.scalar.activation(over[:, m, :], ps_b[:, h // 2 % 2, h % 2 * N:(h % 2 + 1) * N],
                                                    ACT.Relu, bias=below[:, m, h:h + 1], scale=-1.0)
                    last.then_inc(relu_ready.sem, 1)
                    act.wait_ge(relu_ready.sem, relu_ready.at(g, OFFLOADED.index(h) + 1))
                    nc.scalar.activation(over[:, :, :], over[:, :, :], ACT.Sign, scale=-1.0)\
                        .then_inc(over_ready.sem, 1)

                def gat_step(g):
                    n, b, ahead = g.next(), g.prev(), g.next().next()
                    if exists(n):
                        load_mask(n)
                    if is_gat(b):
                        exp_z(b)
                    gate_scale(g)
                    if prepares_next(g):
                        for which in (WV, WF) if g.layer + 1 == ATT else (W, H):
                            split_weights_hi(act, g.layer + 1, which)
                    if exists(n):
                        tanh_h(n)
                        keep_thT(n)
                        keep_h(n)
                        negate_adj(n)
                    differences(g, OFFLOADED[1])
                    if exists(n):
                        exp_gd(n)
                        gate_tanh(n)
                    if exists(ahead):
                        split_hi(ahead)
                    if exists(n):
                        keep_vals_hi(n)
                        keep_gvals_hi(n)
                        differences(n, OFFLOADED[0])
                    if exists(b):
                        normalise_apply(b)

                def keep_q(g):
                    act.wait_ge(q_ps_ready.sem, q_ps_ready.at(g))
                    act.wait_ge(k_split.sem, k_split.at(g.prev()))
                    for e in range(KC):
                        last = nc.scalar.activation(qk_raw[:, e, :], qk_ps[:, e, :], ACT.Identity,
                                                    bias=bias_col[:, 0, e:e + 1], scale=1.0 / (WSCALE * DH ** 0.5))
                    last.then_inc(q_ready.sem, 1)

                def keep_v_hi(g):
                    act.wait_ge(v_ps_ready.sem, v_ps_ready.at(g))
                    src = ps_h[:, :, 0:C].rearrange("p t (h e) -> p t h e", e=DH)
                    nc.scalar.activation(v_sb[g.p][:, 0, :, :, 0:DH], src, ACT.Copy, scale=1.0 / WSCALE)\
                        .then_inc(v_hi_ready.sem, 1)

                def exp_scores(g, h):
                    act.wait_ge(max_ready.sem, max_ready.at(g, h + 1))
                    act.wait_ge(pt_ps_ready.sem, pt_ps_ready.at(g, h - 1))
                    for t in range(NT):
                        last = nc.scalar.activation(probs[:, h % 2, t, :], ps_b[:, h % 2, t * N:(t + 1) * N],
                                                    ACT.Exp, bias=row_max[:, h % 2, t:t + 1])
                    last.then_inc(p_ready.sem, 1)

                def keep_probsT_hi(g, h):
                    act.wait_ge(pt_ps_ready.sem, pt_ps_ready.at(g, h + 1))
                    act.wait_ge(att_ps_ready.sem, att_ps_ready.at(g, h - 1))
                    nc.scalar.activation(probsT[h % 2][:, 0].rearrange("p t q -> p (t q)"), ps_b[:, h % 2, :],
                                         ACT.Copy).then_inc(pt_hi_ready.sem, 1)

                def att_split_hi(g):
                    act.wait_ge(attT_ready.sem, attT_ready.at(g))
                    act.wait_ge(out_ready.sem, out_ready.at(g.prev()))
                    nc.scalar.activation(att_hi[:, :, :], tr_ps, ACT.Copy).then_inc(atthi_ready.sem, 1)

                def att_step(g):
                    n, b, ahead = g.next(), g.prev(), g.next().next()
                    load_mask(n)
                    keep_probsT_hi(g, 0)
                    exp_scores(g, 1)
                    if is_att(b):
                        normalise_apply(b.prev())
                    keep_q(n)
                    keep_probsT_hi(g, 1)
                    exp_scores(g, 2)
                    if is_att(b):
                        att_split_hi(b)
                    keep_probsT_hi(g, 2)
                    exp_scores(g, 3)
                    keep_probsT_hi(g, 3)
                    exp_scores(g, 4)
                    keep_v_hi(n)
                    keep_probsT_hi(g, 4)
                    exp_scores(g, 5)
                    split_hi(ahead)
                    if n.ends_layer():
                        act.wait_ge(v_ps_ready.sem, v_ps_ready.at(n))
                        split_weights_hi(act, n.layer + 1, W)
                        split_weights_hi(act, n.layer + 1, H)
                    keep_probsT_hi(g, 5)
                    exp_scores(n, 0)

                def first(g):
                    if g.layer == 0:
                        load_mask(g)
                        split_hi(g)
                        tanh_h(g)
                        keep_thT(g)
                        keep_h(g)
                        negate_adj(g)
                        exp_gd(g)
                        keep_vals_hi(g)
                        gate_tanh(g)
                        split_hi(g.next())
                        keep_gvals_hi(g)
                        differences(g, OFFLOADED[0])
                    gat_step(g)

                def gat_to_att(g):
                    n, b, ahead = g.next(), g.prev(), g.next().next()
                    load_mask(n)
                    exp_z(b)
                    gate_scale(g)
                    act.wait_ge(gate_ps_ready.sem, gate_ps_ready.at(g))
                    split_weights_hi(act, ATT, WQ)
                    split_weights_hi(act, ATT, WK)
                    keep_v_hi(n)
                    act.wait_ge(rows_ready, ATT + 1)
                    keep_q(n)
                    differences(g, OFFLOADED[1])
                    normalise_apply(b)
                    split_hi(ahead)
                    exp_z(g)
                    exp_scores(n, 0)

                def att_to_gat(g):
                    n, b, ahead = g.next(), g.prev(), g.next().next()
                    load_mask(n)
                    keep_probsT_hi(g, 0)
                    exp_scores(g, 1)
                    normalise_apply(b.prev())
                    keep_probsT_hi(g, 1)
                    exp_scores(g, 2)
                    att_split_hi(b)
                    act.wait_ge(attT_ready.sem, attT_ready.at(b))
                    tanh_h(n)
                    keep_probsT_hi(g, 2)
                    exp_scores(g, 3)
                    keep_thT(n)
                    keep_h(n)
                    keep_probsT_hi(g, 3)
                    exp_scores(g, 4)
                    keep_probsT_hi(g, 4)
                    exp_scores(g, 5)
                    keep_probsT_hi(g, 5)
                    exp_gd(n)
                    keep_vals_hi(n)
                    gate_tanh(n)
                    keep_gvals_hi(n)
                    differences(n, OFFLOADED[0])
                    act.wait_ge(gvals_ready.sem, gvals_ready.at(n))
                    att_split_hi(g)
                    split_hi(ahead)
                    act.wait_ge(att_ps_ready.sem, att_ps_ready.at(g))
                    negate_adj(n)
                    normalise_apply(b)

                for layer in range(LAYERS):
                    if layer == ATT:
                        pipeline(act, layer, att_step, att_step, att_to_gat)
                    else:
                        pipeline(act, layer, first, gat_step, gat_to_att if layer + 1 == ATT else gat_step)
                exp_z(END)
                normalise_apply(END)

            @block.vector
            def _(dve):
                def split_lo(g):
                    dve.wait_ge(hi_ready.sem, hi_ready.at(g))
                    nc.vector.tensor_tensor(x_lo[:, g.p], tr_ps, x_hi[:, g.p], ALU.subtract)\
                        .then_inc(lo_ready.sem, 1)

                def keep_scores(g):
                    dve.wait_ge(sd_ps_ready.sem, sd_ps_ready.at(g))
                    nc.vector.tensor_copy(sd[:, :, :], sd_ps).then_inc(sd_ready.sem, 1)

                def max_targets(g):
                    dve.wait_ge(sdt_ready.sem, sdt_ready.at(g))
                    nc.vector.tensor_reduce(d_max[:, :], dT_ps, AX.X, ALU.max).then_inc(dmax_ready.sem, 1)
                    dve.wait_ge(dmax_ready.sem, dmax_ready.at(g))
                    nc.vector.tensor_scalar(s_pos[:, :], sT_ps, d_max[:, 0:1], 0.0, ALU.add, ALU.max)\
                        .then_inc(spos_ready.sem, 1)
                    nc.vector.tensor_scalar(d_max_diag[:, :], ident[0:HEADS, 0:HEADS], d_max[:, 0:1], None, ALU.mult)\
                        .then_inc(diag_ready.sem, 1)

                def split_s(g):
                    part = lambda q: s_parts[32 * q:32 * q + HEADS, g.p, :]
                    dve.wait_ge(spos_ready.sem, spos_ready.at(g))
                    nc.vector.tensor_copy(part(0), s_pos[:, :]).then_inc(s_hi_ready.sem, 1)
                    dve.wait_ge(s_hi_ready.sem, s_hi_ready.at(g))
                    nc.vector.tensor_tensor(part(1), s_pos[:, :], part(0), ALU.subtract).then_inc(parts_ready.sem, 1)

                def relative_scores(g):
                    dve.wait_ge(dmax_ps_ready.sem, dmax_ps_ready.at(g))
                    m = dmax_ps.rearrange("p (o h) -> p o h", o=1).to_broadcast([P, NT, HEADS])
                    nc.vector.tensor_tensor(above[:, :, :], sd[:, :, 0:HEADS], m, ALU.add).then_inc(above_ready.sem, 1)
                    nc.vector.tensor_tensor(below[:, :, :], m, sd[:, :, HEADS:2 * HEADS], ALU.subtract)
                    dve.wait_ge(above_ready.sem, above_ready.at(g))
                    nc.vector.tensor_scalar(above[:, :, :], above[:, :, :], 0.0, None, ALU.max)\
                        .then_inc(relative_ready.sem, 1)

                def weights(g, j):
                    if j == 0:
                        dve.wait_ge(mask_loaded.of(g), mask_loaded.at(g))
                        dve.wait_ge(relative_ready.sem, relative_ready.at(g))
                    dve.wait_ge(bcast_ready.sem, bcast_ready.at(g, j + 1))
                    if 2 * j + 1 in OFFLOADED:
                        dve.wait_ge(relu_ready.sem, relu_ready.at(g, OFFLOADED.index(2 * j + 1) + 1))
                    for h in (2 * j, 2 * j + 1):
                        if h in OFFLOADED:
                            continue
                        i = h % 2
                        dve.wait_ge(summed.sem, summed.at(g, h - NW + 1))
                        for m in range(NT):
                            last = nc.vector.scalar_tensor_tensor(
                                w_att[:, h % NW, m, :], ps_b[:, j % 2, i * N:(i + 1) * N], below[:, m, h:h + 1],
                                mask[:, g.p, m, :], op0=ALU.is_lt, op1=ALU.mult)
                        last.then_inc(w_ready.sem, 1)

                def keep_vals_lo(g):
                    dve.wait_ge(vals_hi.sem, vals_hi.at(g))
                    nc.vector.tensor_tensor(vals[g.p][:, 1, :, :, 0:EV], h_sb[:, :, :, :],
                                            vals[g.p][:, 0, :, :, 0:EV], ALU.subtract).then_inc(vals_ready.sem, 1)

                def weigh_half(g, half):
                    heads = slice(half * HALF, (half + 1) * HALF)
                    b = b_node[:, g.p, :, heads].rearrange("p t (h o) -> p t h o", o=1).to_broadcast([P, NT, HALF, EV])
                    dve.wait_ge(summed.sem, summed.at(g, (half + 1) * HALF))
                    if half == 0:
                        dve.wait_ge(tht_ready.sem, tht_ready.at(g.next()))
                    nc.vector.tensor_tensor(weighed[:, :, heads, :], sums[:, :, :, 0, :], b, ALU.mult)\
                        .then_inc(half_scaled.sem, 1)
                    dve.wait_ge(half_scaled.sem, half_scaled.at(g, half + 1))
                    nc.vector.tensor_tensor(weighed[:, :, heads, :], weighed[:, :, heads, :], sums[:, :, :, 1, :],
                                            ALU.subtract).then_inc(half_read.sem, 1)

                def gat_divide(g):
                    weigh_half(g, 1)
                    r = rden[:, :, :].rearrange("p t (h o) -> p t h o", o=1)
                    dve.wait_ge(half_read.sem, half_read.at(g))
                    nc.vector.reciprocal(r, weighed[:, :, :, E:EV]).then_inc(rden_ready.sem, 1)
                    dve.wait_ge(rden_ready.sem, rden_ready.at(g))
                    dve.wait_ge(gated_ready.sem, gated_ready.at(g.prev()))
                    nc.vector.tensor_tensor(z, weighed[:, :, :, 0:E], r.to_broadcast([P, NT, HEADS, E]), ALU.mult)\
                        .then_inc(z_ready.sem, 1)

                def elu(g):
                    dve.wait_ge(zexp_ready.sem, zexp_ready.at(g))
                    nc.vector.tensor_scalar(z_flat, z_flat, 0.0, -1.0, ALU.max, ALU.add).then_inc(zpos_ready.sem, 1)
                    dve.wait_ge(zpos_ready.sem, zpos_ready.at(g))
                    nc.vector.scalar_tensor_tensor(z_exp, z_exp, 1.0, z_flat, op0=ALU.min, op1=ALU.add)\
                        .then_inc(elu_ready.sem, 1)

                def normalise_rows(g):
                    normalise_stats(g)
                    settle(g)
                    normalise_moments(g)

                def gat_step(g):
                    n, b, ahead = g.next(), g.prev(), g.next().next()
                    if is_gat(b):
                        gat_divide(b)
                    weights(g, 1)
                    if is_gat(b):
                        elu(b)
                    for j in range(2, 5):
                        if j == 3:
                            weigh_half(g, 0)
                        weights(g, j)
                        if prepares_next(g) and j < 4:
                            which = ((WV, WF) if g.layer + 1 == ATT else (W, H))[j - 2]
                            split_weights_lo(dve, g.layer + 1, which)
                    if exists(n):
                        keep_scores(n)
                    weights(g, 5)
                    if exists(n):
                        max_targets(n)
                        split_s(n)
                        relative_scores(n)
                    if exists(b):
                        normalise_rows(b)
                    if exists(n):
                        if prepares_next(g):
                            prepare_rows(dve, g.layer + 1)
                        weights(n, 0)
                    if exists(ahead):
                        split_lo(ahead)
                    if exists(n):
                        keep_vals_lo(n)

                def negate_mask(g):
                    dve.wait_ge(mask_loaded.of(g), mask_loaded.at(g))
                    dve.wait_ge(s_ready.sem, s_ready.at(g.before()))
                    nc.vector.tensor_scalar(neg_mask[g.p], mask[:, g.p], -1.0, NEG, ALU.add, ALU.mult)\
                        .then_inc(negm_ready.sem, 1)

                def keep_k(g):
                    dve.wait_ge(k_ps_ready.sem, k_ps_ready.at(g))
                    dve.wait_ge(q_split.sem, q_split.at(g))
                    for e in range(KC):
                        last = nc.vector.tensor_scalar(qk_raw[:, e, :], qk_ps[:, e, :], 1.0 / WSCALE,
                                                       bias_col[:, 1, e:e + 1], ALU.mult, ALU.add)
                    last.then_inc(k_ready.sem, 1)

                def max_scores(g, h):
                    dve.wait_ge(s_ready.sem, s_ready.at(g, h + 1))
                    dve.wait_ge(p_ready.sem, p_ready.at(g, h - 1))
                    nc.vector.tensor_reduce(row_max[:, h % 2, :], ps_b[:, h % 2, :].rearrange("p (t k) -> p t k", t=NT),
                                            AX.X, ALU.max, negate=True).then_inc(max_ready.sem, 1)

                def keep_probsT_lo(g, h):
                    dve.wait_ge(pt_hi_ready.sem, pt_hi_ready.at(g, h + 1))
                    nc.vector.tensor_tensor(probsT[h % 2][:, 1].rearrange("p t q -> p (t q)"), ps_b[:, h % 2, :],
                                            probsT[h % 2][:, 0].rearrange("p t q -> p (t q)"), ALU.subtract)\
                        .then_inc(pt_lo_ready.sem, 1)

                def keep_v_lo(g):
                    dve.wait_ge(v_hi_ready.sem, v_hi_ready.at(g))
                    nc.vector.scalar_tensor_tensor(v_sb[g.p][:, 1, :, :, 0:DH],
                                                   ps_h[:, :, 0:C].rearrange("p t (h e) -> p t h e", e=DH),
                                                   1.0 / WSCALE, v_sb[g.p][:, 0, :, :, 0:DH],
                                                   op0=ALU.mult, op1=ALU.subtract).then_inc(v_ready.sem, 1)

                def att_divide(g):
                    dve.wait_ge(att_ps_ready.sem, att_ps_ready.at(g))
                    dve.wait_ge(attT_ready.sem, attT_ready.at(g.prev()))
                    o = ps_o[:, :, 0:MH * DV].rearrange("p t (h e) -> p t h e", e=DV)
                    r = rden[:, :, 0:MH].rearrange("p t (h o) -> p t h o", o=1)
                    nc.vector.reciprocal(r, o[:, :, :, DH:DV]).then_inc(mden_ready.sem, 1)
                    dve.wait_ge(mden_ready.sem, mden_ready.at(g))
                    nc.vector.tensor_tensor(att, o[:, :, :, 0:DH], r.to_broadcast([P, NT, MH, DH]), ALU.mult)\
                        .then_inc(att_ready.sem, 1)

                def att_split_lo(g):
                    dve.wait_ge(atthi_ready.sem, atthi_ready.at(g))
                    nc.vector.tensor_tensor(att_lo[:, :, :], tr_ps, att_hi[:, :, :], ALU.subtract)\
                        .then_inc(attlo_ready.sem, 1)

                def add_residual(g):
                    dve.wait_ge(out_ready.sem, out_ready.at(g))
                    dve.wait_ge(res_loaded.of(g), res_loaded.at(g))
                    dve.wait_ge(normed.sem, normed.at(g.prev()))
                    nc.vector.scalar_tensor_tensor(y[:, :, :], ps_h[:, :, 0:C], 1.0 / WSCALE, x_res[:, g.p],
                                                   op0=ALU.mult, op1=ALU.add).then_inc(y_ready.sem, 1)

                def ones_column(g):
                    nc.vector.memset(v_sb[g.p][:, 0, :, :, DH:DV], 1.0)
                    nc.vector.memset(v_sb[g.p][:, 1, :, :, DH:DV], 0.0)

                def att_step(g):
                    n, b, ahead = g.next(), g.prev(), g.next().next()
                    if is_att(b):
                        att_divide(b)
                    keep_probsT_lo(g, 0)
                    max_scores(g, 2)
                    if is_att(b):
                        negate_mask(n)
                    keep_probsT_lo(g, 1)
                    if is_att(b):
                        att_split_lo(b)
                    max_scores(g, 3)
                    keep_probsT_lo(g, 2)
                    if not is_att(b):
                        normalise_rows(b)
                        negate_mask(n)
                    keep_k(n)
                    max_scores(g, 4)
                    if prepares_next(g):
                        prepare_rows(dve, g.layer + 1)
                    keep_probsT_lo(g, 3)
                    keep_v_lo(n)
                    max_scores(g, 5)
                    keep_probsT_lo(g, 4)
                    split_lo(ahead)
                    if n.ends_layer():
                        dve.wait_ge(v_ps_ready.sem, v_ps_ready.at(n))
                        split_weights_lo(dve, n.layer + 1, W)
                    max_scores(n, 0)
                    keep_probsT_lo(g, 5)
                    if is_att(b):
                        add_residual(b)
                        normalise_stats(b)
                    max_scores(n, 1)
                    if is_att(b):
                        settle(b)
                        normalise_moments(b)
                    if n.ends_layer():
                        split_weights_lo(dve, n.layer + 1, H)

                def first(g):
                    if g.layer == 0:
                        split_lo(g)
                        keep_scores(g)
                        max_targets(g)
                        split_s(g)
                        relative_scores(g)
                        weights(g, 0)
                        keep_vals_lo(g)
                        split_lo(g.next())
                    gat_step(g)

                def gat_to_att(g):
                    n, b, ahead = g.next(), g.prev(), g.next().next()
                    gat_divide(b)
                    ones_column(n)
                    weights(g, 1)
                    elu(b)
                    dve.wait_ge(gate_ps_ready.sem, gate_ps_ready.at(g))
                    split_weights_lo(dve, ATT, WQ)
                    split_weights_lo(dve, ATT, WK)
                    keep_v_lo(n)
                    for j in range(2, 5):
                        if j == 3:
                            weigh_half(g, 0)
                        weights(g, j)
                    normalise_rows(b)
                    weights(g, 5)
                    keep_k(n)
                    negate_mask(n)
                    split_lo(ahead)
                    gat_divide(g)
                    max_scores(n, 0)
                    max_scores(n, 1)
                    elu(g)
                    ones_column(ahead)

                def att_to_gat(g):
                    n, b, ahead = g.next(), g.prev(), g.next().next()
                    att_divide(b)
                    keep_probsT_lo(g, 0)
                    max_scores(g, 2)
                    keep_probsT_lo(g, 1)
                    att_split_lo(b)
                    max_scores(g, 3)
                    keep_probsT_lo(g, 2)
                    max_scores(g, 4)
                    keep_probsT_lo(g, 3)
                    keep_scores(n)
                    max_scores(g, 5)
                    keep_probsT_lo(g, 4)
                    keep_probsT_lo(g, 5)
                    add_residual(b)
                    normalise_rows(b)
                    max_targets(n)
                    split_s(n)
                    dve.wait_ge(tht_ready.sem, tht_ready.at(n))
                    att_divide(g)
                    relative_scores(n)
                    dve.wait_ge(pt_ps_ready.sem, pt_ps_ready.at(g))
                    weights(n, 0)
                    keep_vals_lo(n)
                    att_split_lo(g)
                    add_residual(g)
                    split_lo(ahead)

                for layer in range(LAYERS):
                    if layer == ATT:
                        pipeline(dve, layer, att_step, att_step, att_to_gat)
                    else:
                        pipeline(dve, layer, first, gat_step, gat_to_att if layer + 1 == ATT else gat_step)
                gat_divide(END)
                elu(END)
                normalise_rows(END)

            @block.gpsimd
            def _(pool):
                def gat_back(g):
                    pool.wait_ge(res_loaded.of(g), res_loaded.at(g))
                    pool.wait_ge(elu_ready.sem, elu_ready.at(g))
                    nc.gpsimd.tensor_tensor(z_flat, z_exp, x_res[:, g.p], ALU.subtract)\
                        .then_inc(delta_ready.sem, 1)
                    pool.wait_ge(gate_ready.sem, gate_ready.at(g))
                    pool.wait_ge(delta_ready.sem, delta_ready.at(g))
                    nc.gpsimd.tensor_tensor(z_exp, z_flat, gate4[:, g.p], ALU.mult)\
                        .then_inc(gated_ready.sem, 1)
                    pool.wait_ge(gated_ready.sem, gated_ready.at(g))
                    pool.wait_ge(normed.sem, normed.at(g.prev()))
                    nc.gpsimd.tensor_tensor(y[:, :, :], z_exp, x_res[:, g.p], ALU.add).then_inc(y_ready.sem, 1)

                def scale_values(g):
                    pool.wait_ge(gd_ready.sem, gd_ready.at(g))
                    pool.wait_ge(h_sb_ready.sem, h_sb_ready.at(g))
                    d = D[:, :, :].rearrange("p t (h o) -> p t h o", o=1)
                    gg = G[:, :, :].rearrange("p t (h o) -> p t h o", o=1)
                    nc.gpsimd.tensor_tensor(h_sb[:, :, :, E:EV], d, w_scale_col[:, :, :, :], ALU.mult)\
                        .then_inc(scaled_d_ready.sem, 1)
                    nc.gpsimd.tensor_tensor(h_sb[:, :, :, 0:E], h_sb[:, :, :, 0:E],
                                            d.to_broadcast([P, NT, HEADS, E]), ALU.mult).then_inc(v_scaled.sem, 1)
                    pool.wait_ge(v_scaled.sem, v_scaled.at(g))
                    pool.wait_ge(scaled_d_ready.sem, scaled_d_ready.at(g))
                    if is_att(g.prev()):
                        pool.wait_ge(out_ready.sem, out_ready.at(g.prev().prev()))
                    nc.gpsimd.tensor_tensor(gvals, h_sb[:, :, :, :], gg.to_broadcast([P, NT, HEADS, EV]), ALU.mult)\
                        .then_inc(gv_scaled.sem, 1)

                def keep_gvals_lo(g):
                    pool.wait_ge(gvals_hi.sem, gvals_hi.at(g))
                    pool.wait_ge(gv_scaled.sem, gv_scaled.at(g))
                    nc.gpsimd.tensor_tensor(vals[g.p][:, 1, :, :, EV:2 * EV], gvals,
                                            vals[g.p][:, 0, :, :, EV:2 * EV], ALU.subtract).then_inc(gvals_ready.sem, 1)

                ones = one[:, :, :].to_broadcast([P, KC, N])

                def split_q(g):
                    pool.wait_ge(q_ready.sem, q_ready.at(g))
                    pool.wait_ge(s_ready.sem, s_ready.at(g.before()))
                    nc.gpsimd.tensor_tensor(qT[g.p][:, 0], qk_raw[:, :, :], ones, ALU.mult).then_inc(q_hi_ready.sem, 1)
                    pool.wait_ge(q_hi_ready.sem, q_hi_ready.at(g))
                    nc.gpsimd.tensor_tensor(qT[g.p][:, 1], qk_raw[:, :, :], qT[g.p][:, 0], ALU.subtract)\
                        .then_inc(q_split.sem, 1)

                def split_k(g):
                    pool.wait_ge(k_ready.sem, k_ready.at(g))
                    if is_gat(g.prev()):
                        pool.wait_ge(vals_ready.sem, vals_ready.at(g.prev()))
                        pool.wait_ge(gvals_ready.sem, gvals_ready.at(g.prev()))
                    nc.gpsimd.tensor_tensor(kT[g.p][:, 0], qk_raw[:, :, :], ones, ALU.mult).then_inc(k_hi_ready.sem, 1)
                    pool.wait_ge(k_hi_ready.sem, k_hi_ready.at(g))
                    nc.gpsimd.tensor_tensor(kT[g.p][:, 1], qk_raw[:, :, :], kT[g.p][:, 0], ALU.subtract)\
                        .then_inc(k_split.sem, 1)

                def offloaded_weights(g, h):
                    pool.wait_ge(over_ready.sem, over_ready.at(g, OFFLOADED.index(h) + 1))
                    if h < NW:
                        pool.wait_ge(summed.sem, summed.at(g.prev()))
                    else:
                        pool.wait_ge(summed.sem, summed.at(g, h - NW + 1))
                    pool.wait_ge(neg_adj_ready.sem, neg_adj_ready.at(g))
                    nc.gpsimd.tensor_tensor(w_att[:, h % NW], over[:, :, :], neg_adj[:, g.p], ALU.mult)\
                        .then_inc(w_offloaded.sem, 1)

                def step(g):
                    n, b = g.next(), g.prev()
                    if is_gat(g):
                        offloaded_weights(g, OFFLOADED[0])
                    if is_gat(b):
                        gat_back(b)
                    if is_gat(g):
                        offloaded_weights(g, OFFLOADED[1])
                    if is_att(n):
                        split_q(n)
                        if is_att(g):
                            split_k(n)
                    if exists(n) and is_gat(n):
                        scale_values(n)
                    if exists(b):
                        normalise_factors(b, eps_half[:, :] if is_gat(b) else eps_whole[:, :])
                    if is_att(n) and is_gat(g):
                        split_k(n)
                    if exists(n) and is_gat(n):
                        keep_gvals_lo(n)

                def first(g):
                    if g.layer == 0:
                        scale_values(g)
                        keep_gvals_lo(g)
                    step(g)

                for layer in range(LAYERS):
                    pipeline(pool, layer, first, step, step)
                gat_back(END)
                normalise_factors(END, eps_half[:, :])


_WEIGHTS = ["L0_gnn_W", "L0_gnn_b", "L0_gnn_w_src", "L0_gnn_w_dst", "L0_gnn_H_w", "L0_gnn_H_b", "L1_gnn_Wq",
            "L1_gnn_bq", "L1_gnn_Wk", "L1_gnn_bk", "L1_gnn_Wv", "L1_gnn_bv", "L1_gnn_Wf", "L1_gnn_bf", "L2_gnn_W",
            "L2_gnn_b", "L2_gnn_w_src", "L2_gnn_w_dst", "L2_gnn_H_w", "L2_gnn_H_b", "L3_gnn_W", "L3_gnn_b",
            "L3_gnn_w_src", "L3_gnn_w_dst", "L3_gnn_H_w", "L3_gnn_H_b"]


def kernel(**inputs):
    import numpy as np
    import concourse.bacc as bacc
    from concourse import mybir as _mybir
    from concourse.bass_utils import run_bass_kernel_spmd

    arrays = {"x": np.asarray(inputs["x"])}
    adj = np.asarray(inputs["adj"])
    arrays["adj"] = adj
    arrays["adjT"] = adj.transpose(0, 2, 1)
    for name in _WEIGHTS:
        w = np.asarray(inputs[name])
        if name.endswith("gnn_W"):
            w = w.transpose(1, 0, 2).reshape(w.shape[1], -1)
        elif name.endswith("H_w"):
            w = w.T
        elif name.endswith(("w_src", "w_dst")):
            w = w.reshape(-1, 128).T
            name = name.replace("w_", "w")
        elif name.endswith(("bq", "bk")):
            w = w.reshape(-1, 128).T
        arrays[name] = w
    heads, e, chunks = 12, 32, 3
    p = np.arange(128)
    arrays["c_ident"] = np.eye(128, dtype=np.float32)
    arrays["c_head_of"] = np.stack([((k * 128 + p)[:, None] // e == np.arange(heads)[None]) for k in range(chunks)],
                                   axis=1).astype(np.float32)
    arrays["c_part_of"] = (p[:64, None] % 32 == np.arange(heads)[None]).astype(np.float32)
    arrays["c_row_pq"] = np.array([[0, 1, 1, 0], [1, -1, 1, 0], [0, 1, 0, 1], [1, -1, 0, 1]], np.float32)

    nc = bacc.Bacc("TRN2", target_bir_lowering=False, num_devices=1)
    args, ins = {}, {}
    for name, v in arrays.items():
        v = np.ascontiguousarray(v)
        ins[f"in_{name}"] = v
        args[name] = nc.dram_tensor(f"in_{name}", v.shape, _mybir.dt.from_np(v.dtype), kind="ExternalInput").ap()
    out = nc.dram_tensor("out_x", arrays["x"].shape, _mybir.dt.float32, kind="ExternalOutput").ap()
    residual_graph_layers(nc, args, out)
    r = run_bass_kernel_spmd(nc, [ins], core_ids=[0])
    return r.results[0]["out_x"]
```
